# Optimizing a Trainium2 kernel written in Bass

```python
import numpy as np
import jax
import jax.numpy as jnp

def _softmax(x, axis=-1):
    return jax.nn.softmax(x, axis=axis)

def _gelu(x):
    return jax.nn.gelu(x, approximate=True)

def _silu(x):
    return jax.nn.silu(x)

def _sigmoid(x):
    return jax.nn.sigmoid(x)

def _layernorm(x, axis=-1, eps=1e-05):
    m = jnp.mean(x, axis=axis, keepdims=True)
    v = jnp.var(x, axis=axis, keepdims=True)
    return (x - m) / jnp.sqrt(v + eps)

def _scatter_add(tgt, idx, src, axis=0):
    return tgt.at[idx].add(src)

def _segment_sum(src, seg, n):
    return jax.ops.segment_sum(src, seg, n)
kernel_name = 'mk_seq_postln_d1_jaxref_r8_2efe65'

def setup_inputs(seed: int=0):
    np.random.seed(seed)
    _w = jnp.asarray

    def _L0_attn_setup():
        import jax, jax.numpy as jnp
        import numpy as np
        H = 64
        HK = 8
        HD = 64
        DM = 128
        WINDOW = 128
        key = jax.random.key(seed)
        ks = jax.random.split(key, 9)
        B, S = (2, 128)
        s = 0.02
        return {'x': jax.random.normal(ks[0], (B, S, DM), jnp.float32), 'Wq': jax.random.normal(ks[1], (H * HD, DM), jnp.float32) * s, 'bq': jax.random.normal(ks[2], (H * HD,), jnp.float32) * s, 'Wk': jax.random.normal(ks[3], (HK * HD, DM), jnp.float32) * s, 'bk': jax.random.normal(ks[4], (HK * HD,), jnp.float32) * s, 'Wv': jax.random.normal(ks[5], (HK * HD, DM), jnp.float32) * s, 'bv': jax.random.normal(ks[6], (HK * HD,), jnp.float32) * s, 'Wo': jax.random.normal(ks[7], (DM, H * HD), jnp.float32) * s, 'bo': jax.random.normal(ks[8], (DM,), jnp.float32) * s, 'sinks': jnp.ones((H,), jnp.float32)}
    _L0_attn_in = _L0_attn_setup()

    def _L0_ffn_setup():
        import jax, jax.numpy as jnp
        import numpy as np
        DIM = 128
        DEPTH = 6
        HEADS = 16
        DIM_HEAD = 64
        WINDOW = 32
        INNER = HEADS * DIM_HEAD
        DIM_INNER = int(DIM * 4 * 2 / 3)
        QK_SCALE = 8.0

        def shift_tokens(t):
            a, s = jnp.split(t, 2, -1)
            s = jnp.pad(s, ((0, 0), (1, 0), (0, 0)))[:, :-1]
            return jnp.concatenate([a, s], -1)

        def l2norm(t):
            return t / jnp.maximum(jnp.linalg.norm(t, axis=-1, keepdims=True), 1e-12)

        def rotate_half(x):
            x1, x2 = jnp.split(x, 2, -1)
            return jnp.concatenate([-x2, x1], -1)

        def rotary_tables(n):
            half = jnp.arange(0, DIM_HEAD, 2, dtype=jnp.float32)
            inv_freq = 1.0 / 10000.0 ** (half / DIM_HEAD)
            t = jnp.arange(n, dtype=jnp.float32)
            freqs = t[:, None] * inv_freq[None, :]
            freqs = jnp.concatenate([freqs, freqs], -1)
            base_scale = (half + 0.4 * DIM_HEAD) / (1.4 * DIM_HEAD)
            power = (t - n // 2) / (WINDOW // 2)
            scale = base_scale[None, :] ** power[:, None]
            scale = jnp.concatenate([scale, scale], -1)
            return (freqs, scale)

        def local_attention(q, k, v):
            b, h, n, d = q.shape
            w = WINDOW
            nw = n // w
            bq = q.reshape(b, h, nw, w, d)
            bk = k.reshape(b, h, nw, w, d)
            bv = v.reshape(b, h, nw, w, d)

            def look(t):
                p = jnp.pad(t, ((0, 0), (0, 0), (1, 0), (0, 0), (0, 0)))
                return jnp.concatenate([p[:, :, :nw], p[:, :, 1:]], axis=3)
            bk2, bv2 = (look(bk), look(bv))
            seq = jnp.arange(n).reshape(nw, w)
            seq_p = jnp.pad(seq, ((1, 0), (0, 0)), constant_values=-1)
            jt = jnp.concatenate([seq_p[:nw], seq_p[1:]], axis=1)
            it = seq[:, :, None]
            jb = jt[:, None, :]
            mask = (it < jb) | (it > jb + w) | (jb == -1)
            sim = jnp.einsum('bhwie,bhwje->bhwij', bq, bk2) * QK_SCALE
            sim = jnp.where(mask, -jnp.finfo(sim.dtype).max, sim)
            attn = jax.nn.softmax(sim, -1)
            out = jnp.einsum('bhwij,bhwje->bhwie', attn, bv2)
            return out.reshape(b, h, n, d)

        def attn_layer(x, Wqkv, qs, ksc, Wo):
            b, n, _ = x.shape
            qkv = x @ Wqkv
            q, k, v = jnp.split(qkv, 3, -1)
            sh = lambda t: t.reshape(b, n, HEADS, DIM_HEAD).transpose(0, 2, 1, 3)
            q, k, v = (sh(q), sh(k), sh(v))
            q = l2norm(q) * qs
            k = l2norm(k) * ksc
            freqs, scale = rotary_tables(n)
            cos, sin = (jnp.cos(freqs), jnp.sin(freqs))
            q = q * cos * scale + rotate_half(q) * sin * scale
            inv = 1.0 / scale
            k = k * cos * inv + rotate_half(k) * sin * inv
            out = local_attention(q, k, v)
            out = out.transpose(0, 2, 1, 3).reshape(b, n, INNER)
            return out @ Wo

        def ffn_layer(x, g, bln, W1, b1, W2, b2):
            mu = x.mean(-1, keepdims=True)
            var = ((x - mu) ** 2).mean(-1, keepdims=True)
            xn = (x - mu) / jnp.sqrt(var + 1e-05) * g + bln
            hg = xn @ W1 + b1
            a, gate = jnp.split(hg, 2, -1)
            return a * jax.nn.gelu(gate, approximate=False) @ W2 + b2
        key = jax.random.key(seed)
        ks = jax.random.split(key, 8)
        B, N = (2, 256)
        init = lambda k, shape: jax.random.normal(k, shape, jnp.float32) * 0.02
        return {'x': jax.random.normal(ks[0], (B, N, DIM), jnp.float32), 'Wqkv': init(ks[1], (DEPTH, DIM, 3 * INNER)), 'q_scale': jnp.ones((DEPTH, DIM_HEAD), jnp.float32), 'k_scale': jnp.ones((DEPTH, DIM_HEAD), jnp.float32), 'Wo': init(ks[2], (DEPTH, INNER, DIM)), 'ln_g': jnp.ones((DEPTH, DIM), jnp.float32), 'ln_b': jnp.zeros((DEPTH, DIM), jnp.float32), 'W1': init(ks[3], (DEPTH, DIM, 2 * DIM_INNER)), 'b1': jnp.zeros((DEPTH, 2 * DIM_INNER), jnp.float32), 'W2': init(ks[4], (DEPTH, DIM_INNER, DIM)), 'b2': jnp.zeros((DEPTH, DIM), jnp.float32)}
    _L0_ffn_in = _L0_ffn_setup()
    _d = {'L0_attn_x': _L0_attn_in['x'], 'L0_attn_Wq': _L0_attn_in['Wq'], 'L0_attn_bq': _L0_attn_in['bq'], 'L0_attn_Wk': _L0_attn_in['Wk'], 'L0_attn_bk': _L0_attn_in['bk'], 'L0_attn_Wv': _L0_attn_in['Wv'], 'L0_attn_bv': _L0_attn_in['bv'], 'L0_attn_Wo': _L0_attn_in['Wo'], 'L0_attn_bo': _L0_attn_in['bo'], 'L0_attn_sinks': _L0_attn_in['sinks'], 'L0_ffn_Wqkv': _L0_ffn_in['Wqkv'], 'L0_ffn_q_scale': _L0_ffn_in['q_scale'], 'L0_ffn_k_scale': _L0_ffn_in['k_scale'], 'L0_ffn_Wo': _L0_ffn_in['Wo'], 'L0_ffn_ln_g': _L0_ffn_in['ln_g'], 'L0_ffn_ln_b': _L0_ffn_in['ln_b'], 'L0_ffn_W1': _L0_ffn_in['W1'], 'L0_ffn_b1': _L0_ffn_in['b1'], 'L0_ffn_W2': _L0_ffn_in['W2'], 'L0_ffn_b2': _L0_ffn_in['b2']}
    _x0 = _d['L0_attn_x']
    _d['L0_attn_x'] = jax.random.normal(jax.random.fold_in(jax.random.key(seed), 1), (8, 256, 128), dtype=_x0.dtype)
    del _x0
    return _d

def reference(L0_attn_x, L0_attn_Wq, L0_attn_bq, L0_attn_Wk, L0_attn_bk, L0_attn_Wv, L0_attn_bv, L0_attn_Wo, L0_attn_bo, L0_attn_sinks, L0_ffn_Wqkv, L0_ffn_q_scale, L0_ffn_k_scale, L0_ffn_Wo, L0_ffn_ln_g, L0_ffn_ln_b, L0_ffn_W1, L0_ffn_b1, L0_ffn_W2, L0_ffn_b2):

    def _L0_attn_ref(x, Wq, bq, Wk, bk, Wv, bv, Wo, bo, sinks):
        import jax, jax.numpy as jnp
        import numpy as np
        H = 64
        HK = 8
        HD = 64
        DM = 128
        WINDOW = 128
        B, S, _ = x.shape
        G = H // HK
        q = (x @ Wq.T + bq).reshape(B, S, H, HD).transpose(0, 2, 1, 3)
        k = (x @ Wk.T + bk).reshape(B, S, HK, HD).transpose(0, 2, 1, 3)
        v = (x @ Wv.T + bv).reshape(B, S, HK, HD).transpose(0, 2, 1, 3)
        k = jnp.repeat(k, G, axis=1)
        v = jnp.repeat(v, G, axis=1)
        scale = 1.0 / np.sqrt(HD).astype(np.float32)
        scores = jnp.einsum('bhqd,bhkd->bhqk', q, k) * scale
        qi = jnp.arange(S)[:, None]
        kj = jnp.arange(S)[None, :]
        allowed = (qi >= kj) & (qi - kj < WINDOW)
        neg = jnp.asarray(-1e+30, scores.dtype)
        scores = jnp.where(allowed[None, None], scores, neg)
        sink = jnp.broadcast_to(sinks[None, :, None, None], (B, H, S, 1))
        logits = jnp.concatenate([scores, sink], axis=-1)
        probs = jax.nn.softmax(logits, axis=-1)[..., :-1]
        o = jnp.einsum('bhqk,bhkd->bhqd', probs, v)
        o = o.transpose(0, 2, 1, 3).reshape(B, S, H * HD)
        return o @ Wo.T + bo

    def _L0_ffn_ref(x, Wqkv, q_scale, k_scale, Wo, ln_g, ln_b, W1, b1, W2, b2):
        import jax, jax.numpy as jnp
        import numpy as np
        DIM = 128
        DEPTH = 6
        HEADS = 16
        DIM_HEAD = 64
        WINDOW = 32
        INNER = HEADS * DIM_HEAD
        DIM_INNER = int(DIM * 4 * 2 / 3)
        QK_SCALE = 8.0

        def shift_tokens(t):
            a, s = jnp.split(t, 2, -1)
            s = jnp.pad(s, ((0, 0), (1, 0), (0, 0)))[:, :-1]
            return jnp.concatenate([a, s], -1)

        def l2norm(t):
            return t / jnp.maximum(jnp.linalg.norm(t, axis=-1, keepdims=True), 1e-12)

        def rotate_half(x):
            x1, x2 = jnp.split(x, 2, -1)
            return jnp.concatenate([-x2, x1], -1)

        def rotary_tables(n):
            half = jnp.arange(0, DIM_HEAD, 2, dtype=jnp.float32)
            inv_freq = 1.0 / 10000.0 ** (half / DIM_HEAD)
            t = jnp.arange(n, dtype=jnp.float32)
            freqs = t[:, None] * inv_freq[None, :]
            freqs = jnp.concatenate([freqs, freqs], -1)
            base_scale = (half + 0.4 * DIM_HEAD) / (1.4 * DIM_HEAD)
            power = (t - n // 2) / (WINDOW // 2)
            scale = base_scale[None, :] ** power[:, None]
            scale = jnp.concatenate([scale, scale], -1)
            return (freqs, scale)

        def local_attention(q, k, v):
            b, h, n, d = q.shape
            w = WINDOW
            nw = n // w
            bq = q.reshape(b, h, nw, w, d)
            bk = k.reshape(b, h, nw, w, d)
            bv = v.reshape(b, h, nw, w, d)

            def look(t):
                p = jnp.pad(t, ((0, 0), (0, 0), (1, 0), (0, 0), (0, 0)))
                return jnp.concatenate([p[:, :, :nw], p[:, :, 1:]], axis=3)
            bk2, bv2 = (look(bk), look(bv))
            seq = jnp.arange(n).reshape(nw, w)
            seq_p = jnp.pad(seq, ((1, 0), (0, 0)), constant_values=-1)
            jt = jnp.concatenate([seq_p[:nw], seq_p[1:]], axis=1)
            it = seq[:, :, None]
            jb = jt[:, None, :]
            mask = (it < jb) | (it > jb + w) | (jb == -1)
            sim = jnp.einsum('bhwie,bhwje->bhwij', bq, bk2) * QK_SCALE
            sim = jnp.where(mask, -jnp.finfo(sim.dtype).max, sim)
            attn = jax.nn.softmax(sim, -1)
            out = jnp.einsum('bhwij,bhwje->bhwie', attn, bv2)
            return out.reshape(b, h, n, d)

        def attn_layer(x, Wqkv, qs, ksc, Wo):
            b, n, _ = x.shape
            qkv = x @ Wqkv
            q, k, v = jnp.split(qkv, 3, -1)
            sh = lambda t: t.reshape(b, n, HEADS, DIM_HEAD).transpose(0, 2, 1, 3)
            q, k, v = (sh(q), sh(k), sh(v))
            q = l2norm(q) * qs
            k = l2norm(k) * ksc
            freqs, scale = rotary_tables(n)
            cos, sin = (jnp.cos(freqs), jnp.sin(freqs))
            q = q * cos * scale + rotate_half(q) * sin * scale
            inv = 1.0 / scale
            k = k * cos * inv + rotate_half(k) * sin * inv
            out = local_attention(q, k, v)
            out = out.transpose(0, 2, 1, 3).reshape(b, n, INNER)
            return out @ Wo

        def ffn_layer(x, g, bln, W1, b1, W2, b2):
            mu = x.mean(-1, keepdims=True)
            var = ((x - mu) ** 2).mean(-1, keepdims=True)
            xn = (x - mu) / jnp.sqrt(var + 1e-05) * g + bln
            hg = xn @ W1 + b1
            a, gate = jnp.split(hg, 2, -1)
            return a * jax.nn.gelu(gate, approximate=False) @ W2 + b2
        for i in range(DEPTH):
            x = attn_layer(shift_tokens(x), Wqkv[i], q_scale[i], k_scale[i], Wo[i]) + x
            x = ffn_layer(shift_tokens(x), ln_g[i], ln_b[i], W1[i], b1[i], W2[i], b2[i]) + x
        return x
    x = L0_attn_x
    x = _layernorm(x + _L0_attn_ref(x, L0_attn_Wq, L0_attn_bq, L0_attn_Wk, L0_attn_bk, L0_attn_Wv, L0_attn_bv, L0_attn_Wo, L0_attn_bo, L0_attn_sinks), axis=-1)
    x = _layernorm(x + _L0_ffn_ref(x, L0_ffn_Wqkv, L0_ffn_q_scale, L0_ffn_k_scale, L0_ffn_Wo, L0_ffn_ln_g, L0_ffn_ln_b, L0_ffn_W1, L0_ffn_b1, L0_ffn_W2, L0_ffn_b2), axis=-1)
    return x

_drawn_inputs = setup_inputs


def setup_inputs(seed=0):
    import zlib

    import numpy as np

    out = dict(_drawn_inputs(seed))
    spreads = {'L0_attn_sinks': (1.0, 0.6),
     'L0_ffn_q_scale': (1.0, 0.6),
     'L0_ffn_k_scale': (1.0, 0.6),
     'L0_ffn_ln_g': (1.0, 0.6),
     'L0_ffn_ln_b': (0.0, 0.8),
     'L0_ffn_b1': (0.0, 0.8),
     'L0_ffn_b2': (0.0, 0.1)}
    factors = {'L0_attn_Wq': 8.0,
     'L0_attn_bq': 8.0,
     'L0_attn_Wk': 8.0,
     'L0_attn_bk': 200.0,
     'L0_attn_bo': 2.688,
     'L0_ffn_W1': 3.674,
     'L0_ffn_W2': 3.607}
    for name, (base, spread) in spreads.items():
        noise = np.random.default_rng([zlib.crc32(name.encode()), seed]).standard_normal(out[name].shape)
        drawn = base * np.exp(spread * noise) if base else spread * noise
        out[name] = jnp.asarray(drawn.astype(out[name].dtype))
    for name, factor in factors.items():
        out[name] = (out[name] * factor).astype(out[name].dtype)
    return out
```

```python
from contextlib import ExitStack

import concourse.bass as bass
from concourse import mybir

F32 = mybir.dt.float32
F32R = mybir.dt.float32r
BF16 = mybir.dt.bfloat16
ACT = mybir.ActivationFunctionType
ALU = mybir.AluOpType
AX = mybir.AxisListType
P = 128


class Signal:

    def __init__(self, sem, per, prime=0):
        self.sem, self.per, self.prime = sem, per, prime

    def after(self, it, n):
        return it * self.per + (self.prime + n)


def block_program(nc, x, wq_t, wkv_t, wo_t_in, cols, rows, Wqkv, qk_scale, Wo2, W1, W2, b2, lcols, rot_cos, rot_sin, out):
    NB, S, DM = x.shape
    TT = S // P
    NT = NB * TT
    HD = 64
    KV = (wkv_t.shape[1]) // (3 * HD)
    GH = wq_t.shape[1] // HD // KV
    GP = GH // 2
    PAIRS = KV * GP
    L, _, QKV = Wqkv.shape
    INNER = QKV // 3
    LH = INNER // HD
    LP = LH // 2
    DI = W2.shape[1]
    FB = [(o, min(P, DI - o)) for o in range(0, DI, P)]
    NF = len(FB)
    FT = 4
    FC = NT // FT
    LOCAL = 32
    NEG = -1e30

    ctx = ExitStack()
    with ctx:
        def sb(name, shape, dt=F32):
            return ctx.enter_context(nc.sbuf_tensor(name, shape, dt))

        def sig(name, per=1, prime=0):
            return Signal(ctx.enter_context(nc.semaphore(name)), per, prime)

        x_cur = sb("x_cur", [P, NT, DM])
        x_mid = sb("x_mid", [P, NT, DM])
        ident = sb("ident", [P, P])
        mask_w = sb("mask_w", [P, 384])
        mask_l = sb("mask_l", [P, 288])
        zero_b = sb("zero_b", [1, 256], BF16)
        neg_half = sb("neg_half", [P, 16])
        UG = 2 * GP * P + 2 * P
        wr_arena = sb("wr_arena", [P, KV * UG], F32R)
        w_grp = wr_arena[:, :].rearrange("p (g n) -> p g n", n=UG)
        w_stage = sb("w_stage", [P, UG], F32R)
        wv_hi = sb("wv_hi", [P, KV * HD], F32R)
        wv_lo = sb("wv_lo", [P, KV * HD], F32R)
        f_arena = sb("f_arena", [P, PAIRS * DM])
        wo_t = f_arena[:, :].rearrange("p (q d) -> p q d", d=DM)
        cols_c = sb("cols_c", [P, PAIRS + KV])
        bq_c, bk_c = cols_c[:, 0:PAIRS], cols_c[:, PAIRS:PAIRS + KV]
        rows_b = sb("rows_b", [P, KV * HD + DM + KV * GH])
        bv_b, bo_b = rows_b[:, 0:KV * HD], rows_b[:, KV * HD:KV * HD + DM]
        sink_b = rows_b[:, KV * HD + DM:KV * HD + DM + KV * GH]
        sink_n = sb("sink_n", [P, KV * GH])
        sink_g = sb("sink_g", [P, GH])
        raw = sb("raw", [P, PAIRS * P])
        x_in = sb("x_in", [P, TT, DM])
        x_bo = sb("x_bo", [P, TT * DM])
        xt_hi = sb("xt_hi", [P, S + 1], F32R)
        xt_lo = sb("xt_lo", [P, S + 1], F32R)
        k_hi = sb("k_hi", [P, S], F32R)
        k_lo = sb("k_lo", [P, S], F32R)
        v_a = sb("v_a", [P, TT, HD])
        q_hi = sb("q_hi", [P, 2, S], F32R)
        q_lo = sb("q_lo", [P, 2, S], F32R)
        s_m = sb("s_m", [P, 2, 384])
        p_e = sb("p_e", [P, 2, 384])
        p_t = sb("p_t", [P, 2, 384])
        row_min = sb("row_min", [P, 2 * LH])
        row_sum = sb("row_sum", [P, 2 * LH])
        row_sink = sb("row_sink", [P, 2 * LH])
        row_esink = sb("row_esink", [P, 2 * LH])
        row_den = sb("row_den", [P, 2 * LH])
        row_inv = sb("row_inv", [P, 2 * LH])
        inv_x = sb("inv_x", [P, 2, 2, HD])
        inv_t = sb("inv_t", [P, 2, S])
        o_t = sb("o_t", [P, 2, S])
        z_b = sb("z_b", [P, TT, DM])
        stats = sb("stats", [P, FT, 6])
        moments = sb("moments", [P, FT, 2])
        var_e = sb("var_e", [P, FT])
        rstd = sb("rstd", [P, FT])
        w_raw = raw
        w_hi = wr_arena[:, 0:QKV]
        w_lo = wr_arena[:, QKV:2 * QKV]
        wo_l = sb("wo_l", [P, LP, DM])
        w1_raw = sb("w1_raw", [P, 2 * DI])
        w1_hi = wr_arena[:, 2 * QKV:2 * QKV + 2 * DI]
        w1_lo = wr_arena[:, 2 * QKV + 2 * DI:2 * QKV + 4 * DI]
        w2_l = sb("w2_l", [P, NF, DM])
        lcols_c = sb("lcols_c", [P, 2 * NF + 2])
        b2_b = sb("b2_b", [P, DM])
        b1_c, lng_c, lnb_c = lcols_c, lcols_c[:, 2 * NF:2 * NF + 1], lcols_c[:, 2 * NF + 1:2 * NF + 2]
        qs_b = sb("qs_b", [P, 2, HD])
        qs_r = sb("qs_r", [P, 2, HD])
        cos_t = sb("cos_t", [P, 2, TT, HD])
        sin_t = sb("sin_t", [P, 2, TT, HD])
        cos_s = sb("cos_s", [P, 2, TT, HD])
        sin_s = sb("sin_s", [P, 2, TT, HD])
        HC = 8
        sq = sb("sq", [P, 2, 512])
        r_a = sb("r_a", [P, 2, 512])
        r_b = sb("r_b", [P, 2, 512])
        r_s = sb("r_s", [P, 2, 512])
        r_n = sb("r_n", [P, 2, 512])
        ssum = sb("ssum", [P, 2, HC])
        sfl = sb("sfl", [P, 2, HC])
        rinv = sb("rinv", [P, 2, HC])
        q_neg = sb("q_neg", [P, TT, LH])
        qt_l = f_arena[:, 0:LP * S].rearrange("p (q s) -> p q s", s=S)
        kt_l = f_arena[:, LP * S:2 * LP * S].rearrange("p (q s) -> p q s", s=S)
        v_l = sb("v_l", [P, TT, INNER])
        f_in = sb("f_in", [P, FT, DM])
        f_sh = sb("f_sh", [P, FT * P])
        f_xn = sb("f_xn", [P, FT, DM])
        f_x = sb("f_x", [P, FT * P])
        fx_hi = sb("fx_hi", [P, FT * P], F32R)
        fx_lo = sb("fx_lo", [P, FT * P], F32R)
        f_gate = sb("f_gate", [P, NF, FT * P])
        f_act = sb("f_act", [P, NF, FT * P])
        f_y = sb("f_y", [P, FT, DM])
        kv_raw = f_gate[:, :, :].rearrange("p j n -> p (j n)")

        bank = [ctx.enter_context(nc.psum_tensor(f"bank{i}", [P, 512], F32)) for i in range(8)]
        B_PROJ, B_S, B_T, B_O, B_Y = [0, 1], [2, 3], [4, 5], 6, 7

        phase_end = sig("phase_end")
        const_ready = sig("const_ready")
        ld_x, ld_w, ld_kv, ld_small, ld_wo = (sig(n) for n in ("ld_x", "ld_w", "ld_kv", "ld_small", "ld_wo"))
        split_hi, split_lo = sig("split_hi"), sig("split_lo")
        staged = sig("staged", 16)
        sink_set = sig("sink_set", 1)
        stage_used = sig("stage_used", 1, 1)
        xin_ready = sig("xin_ready", 2)
        xt_ps, xt_hi_done, xt_lo_done = sig("xt_ps", 1, 1), sig("xt_hi_done", 1), sig("xt_lo_done", 1)
        proj_ready = sig("proj_ready", 6)
        proj_hi = sig("proj_hi", 5)
        proj_done = sig("proj_done", 6, 2)
        y_zero = sig("y_zero", 1)
        y_full = sig("y_full", 1)
        z_done, st_done, mom_done = sig("z_done", 1, 1), sig("st_done", 1), sig("mom_done", 1)
        var_done = sig("var_done", 3)
        ln_done = sig("ln_done", 2)
        cur_done = sig("cur_done", 1)
        out_done = sig("out_done")

        class Att:

            def __init__(self, n, H):
                h = H // 2
                self.H = H
                self.scores = sig(n + "scores", H, 4)
                self.masked = sig(n + "masked", 2 * H)
                self.exped = sig(n + "exped", H, 2)
                self.transposed = sig(n + "transposed", H, 2)
                self.pt_act = sig(n + "pt_act", h, 1)
                self.pt_dve = sig(n + "pt_dve", h, 1)
                self.pv = sig(n + "pv", H, 2)
                self.sink_sub = sig(n + "sink_sub", h)
                self.sink_exp = sig(n + "sink_exp", h)
                self.den = sig(n + "den", h)
                self.inv = sig(n + "inv", h)
                self.inv_x = sig(n + "inv_x", h)
                self.inv_ps = sig(n + "inv_ps", h, 1)
                self.inv_sb = sig(n + "inv_sb", h, 1)
                self.o = sig(n + "o", h, 1)
                self.y = sig(n + "y", h, 2)

        A = Att("w_", GH)
        B = Att("l_", LH)
        lw = sig("lw", 16 * 5)
        lw2 = sig("lw2", 16 * 4)
        lw_hi = sig("lw_hi", 2)
        lw_lo = sig("lw_lo", 2)
        swap = sig("swap", 1)
        tab = sig("tab", 4)
        zeros = sig("zeros", 1)
        lx_in = sig("lx_in", 1)
        lxt_ps = sig("lxt_ps", 2, 1)
        lxt_hi = sig("lxt_hi", 2)
        lxt_lo = sig("lxt_lo", 2)
        lp_ps = sig("lp_ps", 12)
        lp_act = sig("lp_act", 12, 2)
        lp_dve = sig("lp_dve", 8)
        lp_sum = sig("lp_sum", 8, 2)
        lp_max = sig("lp_max", 8)
        lp_rot = sig("lp_rot", 8, 2)
        lp_inv = sig("lp_inv", 8)
        lp_out = sig("lp_out", 8)
        lt_ps = sig("lt_ps", 8, 2)
        lt_act = sig("lt_act", 4, 1)
        lt_dve = sig("lt_dve", 4, 1)
        l_res = sig("l_res", 1, 1)
        f_inr = sig("f_inr", 1)
        f_t1 = sig("f_t1", 1, 1)
        f_s1 = sig("f_s1", 1, 1)
        f_t2 = sig("f_t2", 1, 1)
        f_st, f_mom, f_var = sig("f_st", 1), sig("f_mom", 1), sig("f_var", 3)
        f_xnr = sig("f_xnr", 1, 1)
        f_t3 = sig("f_t3", 1, 1)
        f_aff = sig("f_aff", 1, 1)
        f_hi, f_lo = sig("f_hi", 1), sig("f_lo", 1, 1)
        f_gp, f_ap = sig("f_gp", NF), sig("f_ap", NF, 1)
        f_gl, f_ac = sig("f_gl", NF, 1), sig("f_ac", NF, 3)
        f_yp, f_ys, f_res = sig("f_yp", 1, 1), sig("f_ys", 1, 1), sig("f_res", 1, 1)
        n_z, n_st, n_mom, n_var, n_out = sig("n_z", 1), sig("n_st", 1), sig("n_mom", 1), sig("n_var", 3), sig("n_out", 1, 1)

        block = ctx.enter_context(nc.Block())

        met = {eng: ctx.enter_context(nc.semaphore("met_" + name)) for eng, name in (
            (nc.sync, "sp"), (nc.gpsimd, "pool"), (nc.scalar, "act"), (nc.vector, "dve"), (nc.tensor, "pe"))}

        def settle(eng):
            eng.sem_inc(met[eng], 1)

        def end_phase(eng, k):
            settle(eng)
            eng.drain().then_inc(phase_end.sem, 1)
            eng.wait_ge(phase_end.sem, k * 5)
            settle(eng)

        def chunk_t(c):
            t, j = c // 4, c % 4
            return (qt_l if j < 2 else kt_l)[:, 4 * (j % 2):4 * (j % 2) + 4, t * P:(t + 1) * P]

        def halves(t):
            return t.rearrange("p (h z d) -> p h z d", z=2, d=HD // 2)

        def att_pe(pe, a, it, W, emit_q, scores, tr, pv, emit_y):
            H = a.H
            emit_q(0)
            for i in range(-1, H + 3):
                if i >= 0 and i % 2 == 0 and i // 2 + 1 < H // 2:
                    emit_q(i // 2 + 1)
                if i + 1 < H:
                    h = i + 1
                    if h >= 2:
                        pe.wait_ge(a.masked.sem, a.masked.after(it, 2 * (h - 1)))
                    scores(h).then_inc(a.scores.sem, 1)
                if 0 <= i < H:
                    pe.wait_ge(a.exped.sem, a.exped.after(it, i + 1))
                    free = a.pt_act if i % 2 == 0 else a.pt_dve
                    pe.wait_ge(free.sem, free.after(it, i // 2))
                    tr(i).then_inc(a.transposed.sem, 1)
                if 1 <= i <= H:
                    h = i - 1
                    done = a.pt_act if h % 2 == 0 else a.pt_dve
                    pe.wait_ge(done.sem, done.after(it, h // 2 + 1))
                    if h % 2 == 0:
                        pe.wait_ge(a.o.sem, a.o.after(it, h // 2))
                    pv(h).then_inc(a.pv.sem, 1)
                if i >= 2 and i % 2 == 0 and i <= H:
                    p = i // 2 - 1
                    pe.wait_ge(a.inv_x.sem, a.inv_x.after(it, p + 1))
                    for t in range(TT):
                        last = nc.tensor.transpose(bank[B_O][:, S + t * P:S + (t + 1) * P],
                                                   inv_x[:, t, :, :].rearrange("p e d -> p (e d)"), ident[:, :])
                    last.then_inc(a.inv_ps.sem, 1)
                if i >= 4 and i % 2 == 0 or i == H + 2:
                    p = i // 2 - 2
                    if p < H // 2:
                        emit_y(p)

        def y_pair(pe, a, it, p, wo):
            pe.wait_ge(a.o.sem, a.o.after(it, p + 1))
            for t in range(TT):
                last = nc.tensor.matmul(bank[B_Y][:, t * DM:(t + 1) * DM], o_t[:, p % 2, t * P:(t + 1) * P], wo,
                                        start=False, stop=False, skip_group_check=True)
            last.then_inc(a.y.sem, 1)

        def att_dve(dve, a, it, W0, W, mask, scale, floor, q_lo_of):
            H = a.H
            for i in range(-1, H + 3):
                if i >= 0 and i % 2 == 0 and i // 2 + 1 < H // 2:
                    q_lo_of(i // 2 + 1)
                if i + 1 < H:
                    h = i + 1
                    dve.wait_ge(a.scores.sem, a.scores.after(it, h + 1))
                    dve.wait_ge(a.exped.sem, a.exped.after(it, h - 1))
                    settle(dve)
                    for t, (lo, hi) in enumerate(((0, W0), (W0, W))):
                        nc.vector.tensor_tensor_reduce(
                            out=s_m[:, h % 2, lo:hi], in0=bank[B_S[h % 2]][:, lo:hi], in1=mask[:, lo:hi],
                            scale=scale(t, h), scalar=floor(h), op0=ALU.add, op1=ALU.min,
                            accum_out=row_min[:, 2 * h + t:2 * h + t + 1]).then_inc(a.masked.sem, 1)
                if i >= 2 and i % 2 == 0 and i <= H:
                    h, p = i - 1, i // 2 - 1
                    dve.wait_ge(a.transposed.sem, a.transposed.after(it, h + 1))
                    dve.wait_ge(a.pv.sem, a.pv.after(it, h - 1))
                    nc.vector.tensor_copy(p_t[:, 1, 0:W], bank[B_T[1]][:, 0:W]).then_inc(a.pt_dve.sem, 1)
                    dve.wait_ge(a.den.sem, a.den.after(it, p + 1))
                    nc.vector.reciprocal(row_inv[:, 4 * p:4 * p + 4], row_den[:, 4 * p:4 * p + 4]).then_inc(a.inv.sem, 1)
                if i >= 3 and i % 2 == 1 and i <= H + 1:
                    p = (i - 3) // 2
                    dve.wait_ge(a.inv_sb.sem, a.inv_sb.after(it, p + 1))
                    dve.wait_ge(a.pv.sem, a.pv.after(it, 2 * p + 2))
                    dve.wait_ge(a.y.sem, a.y.after(it, p - 1))
                    nc.vector.tensor_tensor(o_t[:, p % 2, :], bank[B_O][:, 0:S], inv_t[:, p % 2, :],
                                            ALU.mult).then_inc(a.o.sem, 1)

        def att_act(act, a, it, W0, W, q_hi_of, sink):
            H = a.H
            for i in range(0, H + 3):
                if i % 2 == 0 and i // 2 + 1 < H // 2:
                    q_hi_of(i // 2 + 1)
                if i < H:
                    act.wait_ge(a.transposed.sem, a.transposed.after(it, i - 1))
                    for t, (lo, hi) in enumerate(((0, W0), (W0, W))):
                        act.wait_ge(a.masked.sem, a.masked.after(it, 2 * i + t + 1))
                        last = nc.scalar.activation(p_e[:, i % 2, lo:hi], s_m[:, i % 2, lo:hi], ACT.Exp,
                                                    bias=row_min[:, 2 * i + t:2 * i + t + 1], scale=-1.0,
                                                    accum_out=row_sum[:, 2 * i + t:2 * i + t + 1])
                    last.then_inc(a.exped.sem, 1)
                if sink and i % 2 == 1 and i < H:
                    p = i // 2
                    act.wait_ge(a.sink_sub.sem, a.sink_sub.after(it, p + 1))
                    nc.scalar.activation(row_esink[:, 4 * p:4 * p + 4], row_sink[:, 4 * p:4 * p + 4],
                                         ACT.Exp).then_inc(a.sink_exp.sem, 1)
                if i % 2 == 1 and i <= H:
                    h = i - 1
                    act.wait_ge(a.transposed.sem, a.transposed.after(it, h + 1))
                    act.wait_ge(a.pv.sem, a.pv.after(it, h - 1))
                    nc.scalar.activation(p_t[:, 0, 0:W], bank[B_T[0]][:, 0:W], ACT.Copy).then_inc(a.pt_act.sem, 1)
                if i % 2 == 1 and i >= 3:
                    p = (i - 3) // 2
                    act.wait_ge(a.inv_ps.sem, a.inv_ps.after(it, p + 1))
                    act.wait_ge(a.o.sem, a.o.after(it, p - 1) if p >= 1 else a.o.after(it, 0))
                    nc.scalar.activation(inv_t[:, p % 2, :], bank[B_O][:, S:2 * S], ACT.Copy).then_inc(a.inv_sb.sem, 1)

        def att_pool(pool, a, it, sink_of):
            for p in range(a.H // 2):
                c = slice(4 * p, 4 * p + 4)
                if sink_of is not None:
                    pool.wait_ge(a.masked.sem, a.masked.after(it, 4 * p + 4))
                    settle(pool)
                    nc.gpsimd.tensor_tensor(row_sink[:, c].rearrange("p (h t) -> p h t", t=2),
                                            row_min[:, c].rearrange("p (h t) -> p h t", t=2),
                                            sink_of(p), ALU.add).then_inc(a.sink_sub.sem, 1)
                    pool.wait_ge(a.sink_exp.sem, a.sink_exp.after(it, p + 1))
                    pool.wait_ge(a.exped.sem, a.exped.after(it, 2 * p + 2))
                    nc.gpsimd.tensor_tensor(row_den[:, c], row_sum[:, c], row_esink[:, c],
                                            ALU.add).then_inc(a.den.sem, 1)
                else:
                    pool.wait_ge(a.exped.sem, a.exped.after(it, 2 * p + 2))
                    settle(pool)
                    nc.gpsimd.tensor_copy(row_den[:, c], row_sum[:, c]).then_inc(a.den.sem, 1)
                pool.wait_ge(a.inv.sem, a.inv.after(it, p + 1))
                pool.wait_ge(a.inv_ps.sem, a.inv_ps.after(it, p))
                settle(pool)
                nc.gpsimd.tensor_copy(inv_x[:, :, :, :].rearrange("p t e d -> p e t d"),
                                      row_inv[:, c].rearrange("p (e t) -> p e t", t=2).unsqueeze(3)
                                      .broadcast_to([P, 2, 2, HD])).then_inc(a.inv_x.sem, 1)

        @block.sync
        def _(sp):
            sp.dma_start(x_cur[:, :, :], x.rearrange("b (t p) d -> p (b t) d", p=P)).then_inc(ld_x.sem, 16)
            sp.dma_start(raw[:, :], wq_t).then_inc(ld_w.sem, 16)
            sp.dma_start(kv_raw, wkv_t).then_inc(ld_kv.sem, 16)
            for dst, src in [(cols_c[:, :], cols), (rows_b[:, :], rows.partition_broadcast(P)),
                             (cos_t[:, :, :, :], rot_cos.rearrange("k (t p) d -> p k t d", p=P)),
                             (sin_t[:, :, :, :], rot_sin.rearrange("k (t p) d -> p k t d", p=P))]:
                sp.dma_start(dst, src).then_inc(ld_small.sem, 16)
            sp.dma_start(wo_t, wo_t_in.rearrange("(q p) n -> p q n", p=P)).then_inc(ld_wo.sem, 16)
            sp.wait_ge(split_lo.sem, KV + 2)
            with sp.Fori(0, NB) as b:
                with sp.Fori(0, KV) as g:
                    it = b * KV + g
                    sp.wait_ge(stage_used.sem, stage_used.after(it, 0))
                    sp.dma_start(w_stage[:, :].bitcast(F32),
                                 w_grp[:, bass.ds(g, 1), :].rearrange("p g n -> p (g n)").bitcast(F32)).then_inc(staged.sem, 16)
            end_phase(sp, 1)
            with sp.Fori(0, L) as l:
                sp.dma_start(w_raw[:, 0:QKV], Wqkv[bass.ds(l, 1)].rearrange("l p n -> p (l n)")).then_inc(lw.sem, 16)
                sp.dma_start(wo_l[:, :, :], Wo2[bass.ds(l, 1)].rearrange("l (q p) n -> p (l q) n", p=P)).then_inc(lw.sem, 16)
                sp.dma_start(w1_raw[:, :], W1[bass.ds(l, 1)].rearrange("l p n -> p (l n)")).then_inc(lw.sem, 16)
                sp.dma_start(qs_b[:, :, :].rearrange("p k d -> p (k d)"),
                             qk_scale[bass.ds(l, 1)].rearrange("l n -> (l n)").partition_broadcast(P)).then_inc(lw.sem, 16)
                sp.dma_start(b2_b[:, :], b2[bass.ds(l, 1)].rearrange("l n -> (l n)").partition_broadcast(P)).then_inc(lw.sem, 16)
                for j, (o, n) in enumerate(FB):
                    sp.dma_start(w2_l[0:n, j, :], W2[bass.ds(l, 1), o:o + n, :].rearrange("l p n -> p (l n)")).then_inc(lw2.sem, 16)
                sp.dma_start(lcols_c[:, :], lcols[bass.ds(l, 1)].rearrange("l p n -> p (l n)")).then_inc(lw2.sem, 16)
                end_phase(sp, l * 2 + 2)
                end_phase(sp, l * 2 + 3)
            o_v = out.rearrange("b (t p) d -> p (b t) d", p=P)
            with sp.Fori(0, NB) as b:
                sp.wait_ge(n_out.sem, n_out.after(b, 1))
                sp.dma_start(o_v[:, bass.ds(b * TT, TT), :], x_cur[:, bass.ds(b * TT, TT), :]).then_inc(out_done.sem, 16)
            sp.wait_ge(out_done.sem, 16 * NB)

        N_SMALL = 16 * 4

        def pool_rstd(pool, n, done, it, moments_ready):
            pool.wait_ge(moments_ready.sem, moments_ready.after(it, 1))
            settle(pool)
            nc.gpsimd.tensor_copy(var_e[:, 0:n], moments[:, 0:n, 1]).then_inc(done.sem, 1)
            pool.wait_ge(done.sem, done.after(it, 1))
            settle(pool)
            nc.gpsimd.tensor_scalar(var_e[:, 0:n], var_e[:, 0:n], 1e-5, 1.0, ALU.add, ALU.mult).then_inc(done.sem, 1)
            pool.wait_ge(done.sem, done.after(it, 2))
            nc.gpsimd.tensor_tensor(rstd[:, 0:n], var_e[:, 0:n], neg_half[:, 0:n], ALU.pow).then_inc(done.sem, 1)

        @block.gpsimd
        def _(pool):
            nc.gpsimd.memset(ident[:, :], 0.0).then_inc(const_ready.sem, 1)
            nc.gpsimd.memset(mask_w[:, :], 0.0).then_inc(const_ready.sem, 1)
            nc.gpsimd.memset(mask_l[:, :], 0.0).then_inc(const_ready.sem, 1)
            nc.gpsimd.memset(zero_b[:, :], 0.0).then_inc(const_ready.sem, 1)
            nc.gpsimd.memset(neg_half[:, :], -0.5).then_inc(const_ready.sem, 1)
            pool.sem_inc(lp_rot.sem, 2)
            pool.sem_inc(f_lo.sem, 1)
            pool.sem_inc(f_res.sem, 1)
            pool.wait_ge(const_ready.sem, 5)
            nc.gpsimd.affine_select(out=ident[:, :], in_=ident[:, :], compare_op=ALU.not_equal, fill=1.0, base=0,
                                    pattern=[[-1, P]], channel_multiplier=1).then_inc(const_ready.sem, 1)
            nc.gpsimd.affine_select(out=mask_w[:, 0:P], in_=mask_w[:, 0:P], compare_op=ALU.is_ge, fill=NEG, base=0,
                                    pattern=[[-1, P]], channel_multiplier=1).then_inc(const_ready.sem, 1)
            nc.gpsimd.affine_select(out=mask_w[:, P:384], in_=mask_w[:, P:384], compare_op=ALU.is_gt, fill=NEG, base=0,
                                    pattern=[[1, S]], channel_multiplier=-1).then_inc(const_ready.sem, 1)
            nc.gpsimd.affine_select(out=mask_l[:, 0:P], in_=mask_l[:, 0:P], compare_op=ALU.is_ge, fill=NEG, base=0,
                                    pattern=[[-1, P]], channel_multiplier=1).then_inc(const_ready.sem, 1)
            nc.gpsimd.affine_select(out=mask_l[:, P:288], in_=mask_l[:, P:288], compare_op=ALU.is_ge, fill=NEG, base=0,
                                    pattern=[[1, 160]], channel_multiplier=-1).then_inc(const_ready.sem, 1)
            pool.wait_ge(const_ready.sem, 10)
            nc.gpsimd.affine_select(out=mask_w[:, P:384], in_=mask_w[:, P:384], compare_op=ALU.is_ge, fill=NEG, base=P,
                                    pattern=[[-1, S]], channel_multiplier=1).then_inc(const_ready.sem, 1)
            nc.gpsimd.affine_select(out=mask_l[:, 0:P], in_=mask_l[:, 0:P], compare_op=ALU.is_ge, fill=NEG, base=LOCAL,
                                    pattern=[[1, P]], channel_multiplier=-1).then_inc(const_ready.sem, 1)
            nc.gpsimd.affine_select(out=mask_l[:, P:288], in_=mask_l[:, P:288], compare_op=ALU.is_ge, fill=NEG, base=LOCAL,
                                    pattern=[[-1, 160]], channel_multiplier=1).then_inc(const_ready.sem, 1)
            pool.wait_ge(ld_small.sem, N_SMALL)
            nc.gpsimd.tensor_scalar(sink_n[:, :], sink_b[:, :], -1.0, 0.0, ALU.mult, ALU.add).then_inc(const_ready.sem, 1)
            pool.wait_ge(ld_x.sem, 16)
            with pool.Fori(0, NB) as b:
                pool.wait_ge(xt_ps.sem, xt_ps.after(b, 0))
                settle(pool)
                xb = x_cur[:, bass.ds(b * TT, TT), :]
                nc.gpsimd.tensor_copy(x_in[:, :, :], xb).then_inc(xin_ready.sem, 1)
                nc.gpsimd.tensor_tensor(x_bo[:, :].rearrange("p (t d) -> p t d", d=DM), xb,
                                        bo_b[:, :].unsqueeze(1).broadcast_to([P, TT, DM]), ALU.add).then_inc(xin_ready.sem, 1)
                with pool.Fori(0, KV) as g:
                    it = b * KV + g
                    att_pool(pool, A, it, lambda p: sink_b[:, bass.ds(g * GH + 2 * p, 2)].unsqueeze(2).broadcast_to([P, 2, 2]))
                pool_rstd(pool, TT, var_done, b, mom_done)
            end_phase(pool, 1)
            with pool.Fori(0, L) as l:
                pool.wait_ge(lw.sem, lw.after(l, 80))
                settle(pool)
                for z in range(2):
                    last = nc.gpsimd.tensor_copy(qs_r[:, :, z * 32:z * 32 + 32], qs_b[:, :, 32 - z * 32:64 - z * 32])
                last.then_inc(swap.sem, 1)
                pool.wait_ge(swap.sem, swap.after(l, 1))
                for k in range(2):
                    nc.gpsimd.tensor_tensor(cos_s[:, k], cos_t[:, k], qs_b[:, k, :].unsqueeze(1).broadcast_to([P, TT, HD]),
                                            ALU.mult).then_inc(tab.sem, 1)
                    nc.gpsimd.tensor_tensor(sin_s[:, k], sin_t[:, k], qs_r[:, k, :].unsqueeze(1).broadcast_to([P, TT, HD]),
                                            ALU.mult).then_inc(tab.sem, 1)
                pool.wait_ge(lw_hi.sem, lw_hi.after(l, 1))
                nc.gpsimd.tensor_tensor(w_lo, w_raw[:, 0:QKV], w_hi.bitcast(F32), ALU.subtract).then_inc(lw_lo.sem, 1)
                pool.wait_ge(lw_hi.sem, lw_hi.after(l, 2))
                nc.gpsimd.tensor_tensor(w1_lo, w1_raw[:, :], w1_hi.bitcast(F32), ALU.subtract).then_inc(lw_lo.sem, 1)
                with pool.Fori(0, NB) as b:
                    it = l * NB + b
                    pool.wait_ge(lxt_ps.sem, lxt_ps.after(it, 0))
                    settle(pool)
                    nc.gpsimd.tensor_copy(x_in[:, :, :], x_cur[:, bass.ds(b * TT, TT), :]).then_inc(lx_in.sem, 1)
                    for c in range(TT * 4):
                        t, kind, buf = c // 4, (c % 4) // 2, c % 2
                        pool.wait_ge(lp_sum.sem, lp_sum.after(it, c + 1))
                        pool.wait_ge(lt_ps.sem, lt_ps.after(it, c - 1))
                        settle(pool)
                        nc.gpsimd.tensor_scalar(sfl[:, buf, :], ssum[:, buf, :], 1e-24, 1.0, ALU.max,
                                                ALU.mult).then_inc(lp_max.sem, 1)
                        nc.gpsimd.tensor_tensor(r_s[:, buf, :], r_a[:, buf, :], r_b[:, buf, :], ALU.add).then_inc(lp_rot.sem, 1)
                        pool.wait_ge(lp_max.sem, lp_max.after(it, c + 1))
                        nc.gpsimd.tensor_tensor(rinv[:, buf, :], sfl[:, buf, :], neg_half[:, 0:HC], ALU.pow).then_inc(lp_inv.sem, 1)
                        pool.wait_ge(lp_inv.sem, lp_inv.after(it, c + 1))
                        settle(pool)
                        if kind == 0:
                            nc.gpsimd.tensor_scalar(q_neg[:, t, (c % 2) * HC:(c % 2 + 1) * HC], rinv[:, buf, :], -8.0, 0.0,
                                                    ALU.mult, ALU.add).then_inc(lp_out.sem, 1)
                        else:
                            pool.wait_ge(lp_rot.sem, lp_rot.after(it, c + 1))
                            nc.gpsimd.tensor_tensor(r_n[:, buf, :].rearrange("p (h d) -> p h d", d=HD),
                                                    r_s[:, buf, :].rearrange("p (h d) -> p h d", d=HD),
                                                    rinv[:, buf, :].unsqueeze(2).broadcast_to([P, HC, HD]),
                                                    ALU.mult).then_inc(lp_out.sem, 1)
                    att_pool(pool, B, it, None)
                end_phase(pool, l * 2 + 2)
                with pool.Fori(0, FC) as c:
                    it = l * FC + c
                    pool.wait_ge(f_t1.sem, f_t1.after(it, 0))
                    settle(pool)
                    nc.gpsimd.tensor_copy(f_in[:, :, :], x_cur[:, bass.ds(c * FT, FT), :]).then_inc(f_inr.sem, 1)
                    pool_rstd(pool, FT, f_var, it, f_mom)
                    pool.wait_ge(f_hi.sem, f_hi.after(it, 1))
                    pool.wait_ge(f_ap.sem, f_ap.after(it, 0))
                    nc.gpsimd.tensor_tensor(fx_lo[:, :], f_x[:, :], fx_hi[:, :].bitcast(F32), ALU.subtract).then_inc(f_lo.sem, 1)
                    pool.wait_ge(f_ys.sem, f_ys.after(it, 1))
                    settle(pool)
                    nc.gpsimd.tensor_tensor(x_cur[:, bass.ds(c * FT, FT), :], f_y[:, :, :],
                                            b2_b[:, :].unsqueeze(1).broadcast_to([P, FT, DM]), ALU.add).then_inc(f_res.sem, 1)
                end_phase(pool, l * 2 + 3)
            with pool.Fori(0, NB) as b:
                pool_rstd(pool, TT, n_var, b, n_mom)

        @block.scalar
        def _(act):
            act.sem_inc(A.exped.sem, 2)
            act.sem_inc(A.pt_act.sem, 1)
            act.sem_inc(A.inv_sb.sem, 1)
            act.sem_inc(B.exped.sem, 2)
            act.sem_inc(B.pt_act.sem, 1)
            act.sem_inc(B.inv_sb.sem, 1)
            act.sem_inc(lt_act.sem, 1)
            act.sem_inc(lp_act.sem, 2)
            act.sem_inc(f_s1.sem, 1)
            act.sem_inc(f_aff.sem, 1)
            act.sem_inc(f_gl.sem, 1)
            K0, KW = 2 * GP * P, KV * P
            act.wait_ge(ld_w.sem, 16)
            for n in range(KV):
                nc.scalar.activation(w_grp[:, n, 0:GP * P], raw[:, n * GP * P:(n + 1) * GP * P], ACT.Copy).then_inc(split_hi.sem, 1)
            act.wait_ge(ld_kv.sem, 16)
            nc.scalar.activation(w_grp[:, :, K0:K0 + P], kv_raw[:, 0:KW].rearrange("p (g n) -> p g n", n=P),
                                 ACT.Copy).then_inc(split_hi.sem, 1)
            nc.scalar.activation(wv_hi[:, :], kv_raw[:, KW:], ACT.Copy).then_inc(split_hi.sem, 1)
            act.wait_ge(ld_small.sem, N_SMALL)
            with act.Fori(0, NB) as b:
                act.wait_ge(xt_ps.sem, xt_ps.after(b, 1))
                nc.scalar.activation(xt_hi[:, 0:S], bank[0][:, 0:S], ACT.Copy).then_inc(xt_hi_done.sem, 1)
                with act.Fori(0, KV) as g:
                    it = b * KV + g

                    def q_hi_of(p):
                        act.wait_ge(proj_ready.sem, proj_ready.after(it, 3 + p))
                        act.wait_ge(A.scores.sem, A.scores.after(it, 2 * p - 2))
                        nc.scalar.activation(q_hi[:, p % 2, :], bank[p % 2][:, 0:S], ACT.Identity,
                                             bias=bq_c[:, bass.ds(g * GP + p, 1)]).then_inc(proj_hi.sem, 1)

                    act.wait_ge(proj_ready.sem, proj_ready.after(it, 1))
                    act.wait_ge(A.scores.sem, A.scores.after(it, 0))
                    nc.scalar.activation(k_hi[:, :], bank[0][:, 0:S], ACT.Identity,
                                         bias=bk_c[:, bass.ds(g, 1)]).then_inc(proj_hi.sem, 1)
                    q_hi_of(0)
                    att_act(act, A, it, P, 384, q_hi_of, True)
                act.wait_ge(ln_done.sem, ln_done.after(b, 2))
                nc.scalar.activation(x_cur[:, bass.ds(b * TT, TT), :], x_mid[:, bass.ds(b * TT, TT), :],
                                     ACT.Copy).then_inc(cur_done.sem, 1)
            end_phase(act, 1)
            with act.Fori(0, L) as l:
                act.wait_ge(lw.sem, lw.after(l, 80))
                nc.scalar.activation(w_hi, w_raw[:, 0:QKV], ACT.Copy).then_inc(lw_hi.sem, 1)
                nc.scalar.activation(w1_hi, w1_raw[:, :], ACT.Copy).then_inc(lw_hi.sem, 1)
                with act.Fori(0, NB) as b:
                    it = l * NB + b
                    for t in range(TT):
                        act.wait_ge(lxt_ps.sem, lxt_ps.after(it, t + 1))
                        nc.scalar.activation(xt_hi[0:HD, t * P:(t + 1) * P], bank[2 + t][0:HD, 0:P], ACT.Copy)
                        nc.scalar.activation(xt_hi[HD:P, t * P + 1:(t + 1) * P + 1], bank[2 + t][HD:P, 0:P],
                                             ACT.Copy).then_inc(lxt_hi.sem, 1)
                    for n in range(12):
                        t, j = n // 6, n % 6
                        act.wait_ge(lp_ps.sem, lp_ps.after(it, n + 1))
                        if j < 4:
                            c = 4 * t + j
                            act.wait_ge(lp_sum.sem, lp_sum.after(it, c - 1))
                            nc.scalar.activation(sq[:, c % 2, :], bank[n % 2][:, :], ACT.Square).then_inc(lp_act.sem, 1)
                        else:
                            act.wait_ge(B.pv.sem, B.pv.after(it, 0))
                            nc.scalar.activation(v_l[:, t, (j - 4) * 512:(j - 3) * 512], bank[n % 2][:, :],
                                                 ACT.Copy).then_inc(lp_act.sem, 1)
                        if j in (2, 4):
                            c = 4 * t + j - 2
                            act.wait_ge(lt_ps.sem, lt_ps.after(it, c + 1))
                            act.wait_ge(B.scores.sem, B.scores.after(it, 0))
                            nc.scalar.activation(chunk_t(c), bank[B_T[0]][:, :].rearrange("p (q c) -> p q c", c=P),
                                                 ACT.Copy).then_inc(lt_act.sem, 1)
                    att_act(act, B, it, P, 288, lambda p: None, False)
                end_phase(act, l * 2 + 2)
                act.wait_ge(lw2.sem, lw2.after(l, 16 * 4))
                settle(act)
                with act.Fori(0, FC) as c:
                    it = l * FC + c
                    act.wait_ge(f_t1.sem, f_t1.after(it, 1))
                    act.wait_ge(f_t2.sem, f_t2.after(it, 0))
                    nc.scalar.activation(f_sh[0:HD, :], bank[0][0:HD, :], ACT.Copy)
                    nc.scalar.activation(f_sh[HD:P, :].rearrange("p (h s) -> p h s", s=S)[:, :, 1:S],
                                         bank[0][HD:P, :].rearrange("p (h s) -> p h s", s=S)[:, :, 0:S - 1],
                                         ACT.Copy).then_inc(f_s1.sem, 1)
                    act.wait_ge(f_t3.sem, f_t3.after(it, 1))
                    act.wait_ge(f_lo.sem, f_lo.after(it, 0))
                    act.wait_ge(f_ap.sem, f_ap.after(it, 0))
                    nc.scalar.activation(f_x[:, :], bank[2][:, :], ACT.Identity, bias=lnb_c[:, 0:1],
                                         scale=lng_c[:, 0:1]).then_inc(f_aff.sem, 1)
                    act.wait_ge(f_aff.sem, f_aff.after(it, 1))
                    nc.scalar.activation(fx_hi[:, :], f_x[:, :], ACT.Copy).then_inc(f_hi.sem, 1)
                    for j, (o, n) in enumerate(FB):
                        act.wait_ge(f_gp.sem, f_gp.after(it, j + 1))
                        act.wait_ge(f_ac.sem, f_ac.after(it, j - 2))
                        nc.scalar.activation(f_gate[0:n, j, :], bank[3 + j % 2][0:n, :], ACT.Gelu,
                                             bias=b1_c[0:n, 2 * j + 1:2 * j + 2]).then_inc(f_gl.sem, 1)
                end_phase(act, l * 2 + 3)

        def dve_stats(dve, n, src, st, mom, it):
            for t in range(n):
                last = nc.vector.bn_stats(stats[:, t, :], src(t))
            last.then_inc(st.sem, 1)
            dve.wait_ge(st.sem, st.after(it, 1))
            settle(dve)
            for t in range(n):
                last = nc.vector.bn_aggr(moments[:, t, :], stats[:, t, :])
            last.then_inc(mom.sem, 1)

        @block.vector
        def _(dve):
            dve.sem_inc(proj_done.sem, 2)
            dve.sem_inc(A.pt_dve.sem, 1)
            dve.sem_inc(A.o.sem, 1)
            dve.sem_inc(B.pt_dve.sem, 1)
            dve.sem_inc(B.o.sem, 1)
            dve.sem_inc(z_done.sem, 1)
            dve.sem_inc(lp_sum.sem, 2)
            dve.sem_inc(lt_dve.sem, 1)
            dve.sem_inc(l_res.sem, 1)
            dve.sem_inc(f_xnr.sem, 1)
            dve.sem_inc(f_ac.sem, 3)
            dve.sem_inc(f_ys.sem, 1)
            dve.sem_inc(n_out.sem, 1)
            K0, KW = 2 * GP * P, KV * P
            for n in range(KV):
                dve.wait_ge(split_hi.sem, n + 1)
                nc.vector.tensor_tensor(w_grp[:, n, GP * P:2 * GP * P], raw[:, n * GP * P:(n + 1) * GP * P],
                                        w_grp[:, n, 0:GP * P].bitcast(F32), ALU.subtract).then_inc(split_lo.sem, 1)
            dve.wait_ge(split_hi.sem, KV + 1)
            nc.vector.tensor_tensor(w_grp[:, :, K0 + P:K0 + 2 * P], kv_raw[:, 0:KW].rearrange("p (g n) -> p g n", n=P),
                                    w_grp[:, :, K0:K0 + P].bitcast(F32), ALU.subtract).then_inc(split_lo.sem, 1)
            dve.wait_ge(split_hi.sem, KV + 2)
            nc.vector.tensor_tensor(wv_lo[:, :], kv_raw[:, KW:], wv_hi[:, :].bitcast(F32), ALU.subtract).then_inc(split_lo.sem, 1)
            dve.wait_ge(ld_small.sem, N_SMALL)
            dve.wait_ge(const_ready.sem, 14)
            with dve.Fori(0, NB) as b:
                dve.wait_ge(xt_hi_done.sem, xt_hi_done.after(b, 1))
                nc.vector.tensor_tensor(xt_lo[:, 0:S], bank[0][:, 0:S], xt_hi[:, 0:S].bitcast(F32),
                                        ALU.subtract).then_inc(xt_lo_done.sem, 1)
                with dve.Fori(0, KV) as g:
                    it = b * KV + g

                    def q_lo_of(p):
                        dve.wait_ge(proj_hi.sem, proj_hi.after(it, 2 + p))
                        nc.vector.scalar_tensor_tensor(q_lo[:, p % 2, :], bank[p % 2][:, 0:S],
                                                       bq_c[:, bass.ds(g * GP + p, 1)],
                                                       q_hi[:, p % 2, :].bitcast(F32), ALU.add,
                                                       ALU.subtract).then_inc(proj_done.sem, 1)

                    nc.vector.tensor_copy(sink_g[:, :], sink_n[:, bass.ds(g * GH, GH)]).then_inc(sink_set.sem, 1)
                    dve.wait_ge(sink_set.sem, sink_set.after(it, 1))
                    dve.wait_ge(proj_hi.sem, proj_hi.after(it, 1))
                    nc.vector.scalar_tensor_tensor(k_lo[:, :], bank[0][:, 0:S], bk_c[:, bass.ds(g, 1)],
                                                   k_hi[:, :].bitcast(F32), ALU.add, ALU.subtract).then_inc(proj_done.sem, 1)
                    dve.wait_ge(proj_ready.sem, proj_ready.after(it, 2))
                    dve.wait_ge(A.pv.sem, A.pv.after(it, 0))
                    nc.vector.tensor_tensor(v_a[:, :, :], bank[1][:, 0:TT * HD].rearrange("p (t d) -> p t d", d=HD),
                                            bv_b[:, bass.ds(g * HD, HD)].unsqueeze(1).broadcast_to([P, TT, HD]),
                                            ALU.add).then_inc(proj_done.sem, 1)
                    q_lo_of(0)
                    att_dve(dve, A, it, P, 384, mask_w, lambda t, h: -0.125,
                            lambda h: sink_g[:, h:h + 1], q_lo_of)
                dve.wait_ge(y_full.sem, y_full.after(b, 1))
                dve.wait_ge(xin_ready.sem, xin_ready.after(b, 2))
                nc.vector.tensor_tensor(z_b[:, :, :].rearrange("p t d -> p (t d)"), bank[B_Y][:, 0:S], x_bo[:, :],
                                        ALU.add).then_inc(z_done.sem, 1)
                dve.wait_ge(z_done.sem, z_done.after(b, 1))
                dve_stats(dve, TT, lambda t: z_b[:, t, :], st_done, mom_done, b)
                dve.wait_ge(var_done.sem, var_done.after(b, 3))
                for t in range(TT):
                    nc.vector.tensor_scalar(x_mid[:, bass.ds(b * TT + t, 1), :].rearrange("p t d -> p (t d)"), z_b[:, t, :],
                                            moments[:, t, 0:1], rstd[:, t:t + 1], ALU.subtract,
                                            ALU.mult).then_inc(ln_done.sem, 1)
            end_phase(dve, 1)
            with dve.Fori(0, L) as l:
                nc.vector.memset(xt_hi[HD:P, 0:1].bitcast(F32), 0.0)
                nc.vector.memset(xt_lo[HD:P, 0:1].bitcast(F32), 0.0)
                nc.vector.memset(f_sh[HD:P, :].rearrange("p (h s) -> p h s", s=S)[:, :, 0:1], 0.0).then_inc(zeros.sem, 1)
                dve.wait_ge(tab.sem, tab.after(l, 4))
                settle(dve)
                with dve.Fori(0, NB) as b:
                    it = l * NB + b
                    for t in range(TT):
                        dve.wait_ge(lxt_hi.sem, lxt_hi.after(it, t + 1))
                        nc.vector.tensor_tensor(xt_lo[0:HD, t * P:(t + 1) * P], bank[2 + t][0:HD, 0:P],
                                                xt_hi[0:HD, t * P:(t + 1) * P].bitcast(F32), ALU.subtract)
                        nc.vector.tensor_tensor(xt_lo[HD:P, t * P + 1:(t + 1) * P + 1], bank[2 + t][HD:P, 0:P],
                                                xt_hi[HD:P, t * P + 1:(t + 1) * P + 1].bitcast(F32),
                                                ALU.subtract).then_inc(lxt_lo.sem, 1)
                    for n in range(12):
                        t, j = n // 6, n % 6
                        if j < 4:
                            c = 4 * t + j
                            kind, buf, ps = j // 2, c % 2, bank[n % 2][:, :]
                            dve.wait_ge(lp_act.sem, lp_act.after(it, n + 1))
                            dve.wait_ge(lp_rot.sem, lp_rot.after(it, c - 1))
                            nc.vector.tensor_tensor(
                                r_a[:, buf, :].rearrange("p (h d) -> p h d", d=HD), ps.rearrange("p (h d) -> p h d", d=HD),
                                cos_s[:, kind, t, :].unsqueeze(1).broadcast_to([P, HC, HD]), ALU.mult)
                            for z in range(2):
                                last = nc.vector.tensor_tensor(
                                    halves(r_b[:, buf, :])[:, :, z, :], halves(ps)[:, :, 1 - z, :],
                                    sin_s[:, kind, t, z * 32:z * 32 + 32].unsqueeze(1).broadcast_to([P, HC, 32]), ALU.mult)
                            last.then_inc(lp_dve.sem, 1)
                            nc.vector.tensor_reduce(ssum[:, buf, :], sq[:, buf, :].rearrange("p (h d) -> p h d", d=HD),
                                                    AX.X, ALU.add).then_inc(lp_sum.sem, 1)
                        if j in (3, 5):
                            c = 4 * t + j - 2
                            dve.wait_ge(lt_ps.sem, lt_ps.after(it, c + 1))
                            dve.wait_ge(B.scores.sem, B.scores.after(it, 0))
                            nc.vector.tensor_copy(chunk_t(c), bank[B_T[1]][:, :].rearrange("p (q c) -> p q c", c=P))\
                                .then_inc(lt_dve.sem, 1)
                    att_dve(dve, B, it, P, 288, mask_l, lambda t, h: q_neg[:, t, h:h + 1], lambda h: 3.0e38, lambda p: None)
                    dve.wait_ge(B.y.sem, B.y.after(it, LP))
                    xb = x_cur[:, bass.ds(b * TT, TT), :].rearrange("p t d -> p (t d)")
                    nc.vector.tensor_tensor(xb, bank[B_Y][:, 0:S], xb, ALU.add).then_inc(l_res.sem, 1)
                end_phase(dve, l * 2 + 2)
                with dve.Fori(0, FC) as c:
                    it = l * FC + c
                    dve.wait_ge(f_t2.sem, f_t2.after(it, 1))
                    dve_stats(dve, FT, lambda t: bank[1][:, t * P:(t + 1) * P], f_st, f_mom, it)
                    dve.wait_ge(f_var.sem, f_var.after(it, 3))
                    dve.wait_ge(f_t3.sem, f_t3.after(it, 0))
                    for t in range(FT):
                        last = nc.vector.tensor_scalar(f_xn[:, t, :], bank[1][:, t * P:(t + 1) * P], moments[:, t, 0:1],
                                                       rstd[:, t:t + 1], ALU.subtract, ALU.mult)
                    last.then_inc(f_xnr.sem, 1)
                    dve.wait_ge(f_yp.sem, f_yp.after(it, 0))
                    for j, (o, n) in enumerate(FB):
                        dve.wait_ge(f_ap.sem, f_ap.after(it, j + 1))
                        dve.wait_ge(f_gl.sem, f_gl.after(it, j + 1))
                        nc.vector.scalar_tensor_tensor(f_act[0:n, j, :], bank[5 + j % 2][0:n, :], b1_c[0:n, 2 * j:2 * j + 1],
                                                       f_gate[0:n, j, :], ALU.add, ALU.mult).then_inc(f_ac.sem, 1)
                    dve.wait_ge(f_yp.sem, f_yp.after(it, 1))
                    dve.wait_ge(f_res.sem, f_res.after(it, 0))
                    nc.vector.tensor_tensor(f_y[:, :, :].rearrange("p t d -> p (t d)"), bank[B_Y][:, :],
                                            x_cur[:, bass.ds(c * FT, FT), :].rearrange("p t d -> p (t d)"),
                                            ALU.add).then_inc(f_ys.sem, 1)
                end_phase(dve, l * 2 + 3)
            with dve.Fori(0, NB) as b:
                dve.wait_ge(n_out.sem, n_out.after(b, 0))
                xb = x_cur[:, bass.ds(b * TT, TT), :]
                nc.vector.tensor_tensor(z_b[:, :, :], xb, x_mid[:, bass.ds(b * TT, TT), :], ALU.add).then_inc(n_z.sem, 1)
                dve.wait_ge(n_z.sem, n_z.after(b, 1))
                dve_stats(dve, TT, lambda t: z_b[:, t, :], n_st, n_mom, b)
                dve.wait_ge(n_var.sem, n_var.after(b, 3))
                for t in range(TT):
                    last = nc.vector.tensor_scalar(x_cur[:, bass.ds(b * TT + t, 1), :].rearrange("p t d -> p (t d)"),
                                                   z_b[:, t, :], moments[:, t, 0:1], rstd[:, t:t + 1], ALU.subtract, ALU.mult)
                last.then_inc(n_out.sem, 1)

        def split_mm(dst, lhs, rhs, start=True):
            nc.tensor.matmul(dst, lhs[0], rhs[0], start=True, stop=False)
            nc.tensor.matmul(dst, lhs[1], rhs[0], start=False, stop=False)
            return nc.tensor.matmul(dst, lhs[0], rhs[1], start=False, stop=True)

        @block.tensor
        def _(pe):
            for a in (A, B):
                pe.sem_inc(a.scores.sem, 4)
                pe.sem_inc(a.transposed.sem, 2)
                pe.sem_inc(a.pv.sem, 2)
                pe.sem_inc(a.inv_ps.sem, 1)
                pe.sem_inc(a.y.sem, 2)
            pe.sem_inc(stage_used.sem, 1)
            pe.sem_inc(xt_ps.sem, 1)
            pe.sem_inc(lxt_ps.sem, 1)
            pe.sem_inc(lt_ps.sem, 2)
            for g in (f_t1, f_t2, f_t3, f_ap, f_yp):
                pe.sem_inc(g.sem, 1)
            pe.wait_ge(const_ready.sem, 14)
            pe.wait_ge(split_lo.sem, KV + 2)
            pe.wait_ge(ld_wo.sem, 16)
            K0 = 2 * GP * P
            xt = (xt_hi[:, 0:S], xt_lo[:, 0:S])
            with pe.Fori(0, NB) as b:
                pe.wait_ge(z_done.sem, z_done.after(b, 0))
                nc.tensor.matmul(bank[B_Y][:, 0:S], zero_b[0:1, 0:P], zero_b[0:1, 0:S], start=True, stop=True)
                pe.wait_ge(xin_ready.sem, xin_ready.after(b, 1))
                pe.wait_ge(proj_done.sem, b * (KV * 6) + 2)
                for t in range(TT):
                    last = nc.tensor.transpose(bank[0][:, t * P:(t + 1) * P], x_in[:, t, :], ident[:, :])
                last.then_inc(xt_ps.sem, 1)
                pe.wait_ge(xt_lo_done.sem, xt_lo_done.after(b, 1))
                settle(pe)
                with pe.Fori(0, KV) as g:
                    it = b * KV + g
                    pe.wait_ge(staged.sem, staged.after(it, 16))
                    pe.wait_ge(proj_done.sem, proj_done.after(it, -1))
                    split_mm(bank[0][:, 0:S], (w_stage[:, K0:K0 + P], w_stage[:, K0 + P:K0 + 2 * P]), xt).then_inc(proj_ready.sem, 1)
                    pe.wait_ge(proj_done.sem, proj_done.after(it, 0))
                    for t in range(TT):
                        ts = slice(t * P, (t + 1) * P)
                        last = split_mm(bank[1][:, t * HD:(t + 1) * HD], (xt_hi[:, ts], xt_lo[:, ts]),
                                        (wv_hi[:, bass.ds(g * HD, HD)], wv_lo[:, bass.ds(g * HD, HD)]))
                    last.then_inc(proj_ready.sem, 1)

                    def emit_q(p):
                        pe.wait_ge(proj_done.sem, proj_done.after(it, 1 + p))
                        last = split_mm(bank[p % 2][:, 0:S], (w_stage[:, p * P:(p + 1) * P],
                                                              w_stage[:, (GP + p) * P:(GP + p + 1) * P]), xt)
                        last.then_inc(proj_ready.sem, 1)

                    def scores(h):
                        p, r = h // 2, slice(HD * (h % 2), HD * (h % 2) + HD)
                        pe.wait_ge(proj_done.sem, proj_done.after(it, 3 + p))
                        ps = bank[B_S[h % 2]]
                        split_mm(ps[:, 0:P], (q_hi[r, p % 2, 0:P], q_lo[r, p % 2, 0:P]), (k_hi[r, 0:P], k_lo[r, 0:P]))
                        return split_mm(ps[:, P:384], (q_hi[r, p % 2, P:S], q_lo[r, p % 2, P:S]), (k_hi[r, :], k_lo[r, :]))

                    def tr(h):
                        for k in range(3):
                            last = nc.tensor.transpose(bank[B_T[h % 2]][:, k * P:(k + 1) * P],
                                                       p_e[:, h % 2, k * P:(k + 1) * P], ident[:, :])
                        return last

                    def pv(h):
                        o, pt = bank[B_O][HD * (h % 2):HD * (h % 2) + HD, 0:S], p_t[:, h % 2, :]
                        nc.tensor.matmul(o[:, 0:P], v_a[:, 0, :], pt[:, 0:P], start=True, stop=True)
                        nc.tensor.matmul(o[:, P:S], v_a[:, 0, :], pt[:, P:2 * P], start=True, stop=False)
                        return nc.tensor.matmul(o[:, P:S], v_a[:, 1, :], pt[:, 2 * P:3 * P], start=False, stop=True)

                    att_pe(pe, A, it, 384, emit_q, scores, tr, pv,
                           lambda p: y_pair(pe, A, it, p, wo_t[:, bass.ds(g * GP + p, 1), :].rearrange("p q d -> p (q d)")))
                    pe.drain().then_inc(stage_used.sem, 1)
                pe.drain().then_inc(y_full.sem, 1)
            end_phase(pe, 1)
            with pe.Fori(0, L) as l:
                pe.wait_ge(lw_lo.sem, lw_lo.after(l, 2))
                pe.wait_ge(zeros.sem, zeros.after(l, 1))
                settle(pe)
                with pe.Fori(0, NB) as b:
                    it = l * NB + b
                    pe.wait_ge(l_res.sem, l_res.after(it, 0))
                    nc.tensor.matmul(bank[B_Y][:, 0:S], zero_b[0:1, 0:P], zero_b[0:1, 0:S], start=True, stop=True)
                    pe.wait_ge(lx_in.sem, lx_in.after(it, 1))
                    for t in range(TT):
                        nc.tensor.transpose(bank[2 + t][:, 0:P], x_in[:, t, :], ident[:, :]).then_inc(lxt_ps.sem, 1)
                    for n in range(12):
                        t, j = n // 6, n % 6
                        if j == 0:
                            pe.wait_ge(lxt_lo.sem, lxt_lo.after(it, t + 1))
                        if n < 2:
                            pe.wait_ge(lp_act.sem, lp_act.after(it, n - 1))
                        elif (n - 2) % 6 < 4:
                            pe.wait_ge(lp_dve.sem, lp_dve.after(it, 4 * ((n - 2) // 6) + (n - 2) % 6 + 1))
                        else:
                            pe.wait_ge(lp_act.sem, lp_act.after(it, n - 1))
                        ts, ws = slice(t * P, (t + 1) * P), slice(j * 512, (j + 1) * 512)
                        split_mm(bank[n % 2][:, :], (xt_hi[:, ts], xt_lo[:, ts]), (w_hi[:, ws], w_lo[:, ws])).then_inc(lp_ps.sem, 1)
                        if j >= 2:
                            c = 4 * t + j - 2
                            pe.wait_ge(lp_out.sem, lp_out.after(it, c + 1))
                            free = lt_act if c % 2 == 0 else lt_dve
                            pe.wait_ge(free.sem, free.after(it, c // 2))
                            src = r_s if (c % 4) < 2 else r_n
                            for k in range(4):
                                last = nc.tensor.transpose(bank[B_T[c % 2]][:, k * P:(k + 1) * P],
                                                           src[:, c % 2, k * P:(k + 1) * P], ident[:, :])
                            last.then_inc(lt_ps.sem, 1)
                    pe.wait_ge(lt_act.sem, lt_act.after(it, 4))
                    pe.wait_ge(lt_dve.sem, lt_dve.after(it, 4))
                    pe.wait_ge(lp_act.sem, lp_act.after(it, 12))

                    def scores(h):
                        p, r = h // 2, slice(HD * (h % 2), HD * (h % 2) + HD)
                        ps = bank[B_S[h % 2]]
                        nc.tensor.matmul(ps[:, 0:P], qt_l[r, p, 0:P], kt_l[r, p, 0:P], start=True, stop=True)
                        return nc.tensor.matmul(ps[:, P:288], qt_l[r, p, P:S], kt_l[r, p, P - LOCAL:S], start=True, stop=True)

                    def tr(h):
                        ps, pr = bank[B_T[h % 2]], p_e[:, h % 2, :]
                        nc.tensor.transpose(ps[:, 0:P], pr[:, 0:P], ident[:, :])
                        nc.tensor.transpose(ps[:, P:2 * P], pr[:, P + LOCAL:2 * P + LOCAL], ident[:, :])
                        return nc.tensor.transpose(ps[:, 2 * P:2 * P + LOCAL], pr[0:LOCAL, LOCAL:P + LOCAL], ident[0:LOCAL, 0:LOCAL])

                    def pv(h):
                        o, pt = bank[B_O][HD * (h % 2):HD * (h % 2) + HD, 0:S], p_t[:, h % 2, :]
                        vh = slice(h * HD, (h + 1) * HD)
                        nc.tensor.matmul(o[:, 0:P], v_l[:, 0, vh], pt[:, 0:P], start=True, stop=True)
                        nc.tensor.matmul(o[:, P:S], v_l[:, 1, vh], pt[:, P:2 * P], start=True, stop=True)
                        return nc.tensor.matmul(o[:, P:P + LOCAL], v_l[P - LOCAL:P, 0, vh], pt[P - LOCAL:P, 2 * P:2 * P + LOCAL],
                                                start=False, stop=True, skip_group_check=True)

                    att_pe(pe, B, it, 288, lambda p: None, scores, tr, pv,
                           lambda p: y_pair(pe, B, it, p, wo_l[:, p, :]))
                end_phase(pe, l * 2 + 2)
                pe.wait_ge(lw2.sem, lw2.after(l, 16 * 4))
                settle(pe)
                with pe.Fori(0, FC) as c:
                    it = l * FC + c
                    pe.wait_ge(f_inr.sem, f_inr.after(it, 1))
                    pe.wait_ge(f_s1.sem, f_s1.after(it, 0))
                    for t in range(FT):
                        last = nc.tensor.transpose(bank[0][:, t * P:(t + 1) * P], f_in[:, t, :], ident[:, :])
                    last.then_inc(f_t1.sem, 1)
                    pe.wait_ge(f_s1.sem, f_s1.after(it, 1))
                    pe.wait_ge(f_xnr.sem, f_xnr.after(it, 0))
                    for t in range(FT):
                        last = nc.tensor.transpose(bank[1][:, t * P:(t + 1) * P], f_sh[:, t * P:(t + 1) * P], ident[:, :])
                    last.then_inc(f_t2.sem, 1)
                    pe.wait_ge(f_xnr.sem, f_xnr.after(it, 1))
                    pe.wait_ge(f_aff.sem, f_aff.after(it, 0))
                    for t in range(FT):
                        last = nc.tensor.transpose(bank[2][:, t * P:(t + 1) * P], f_xn[:, t, :], ident[:, :])
                    last.then_inc(f_t3.sem, 1)
                    pe.wait_ge(f_lo.sem, f_lo.after(it, 1))
                    fx = (fx_hi[:, :], fx_lo[:, :])
                    for j, (o, n) in enumerate(FB):
                        for first, base, free, done in ((DI, 3, f_gl, f_gp), (0, 5, f_ac, f_ap)):
                            pe.wait_ge(free.sem, free.after(it, max(0, j - 1)))
                            cs = slice(first + o, first + o + n)
                            split_mm(bank[base + j % 2][0:n, :], (w1_hi[:, cs], w1_lo[:, cs]), fx).then_inc(done.sem, 1)
                    pe.wait_ge(f_ys.sem, f_ys.after(it, 0))
                    pe.wait_ge(f_ac.sem, f_ac.after(it, NF))
                    for t in range(FT):
                        for j, (o, n) in enumerate(FB):
                            last = nc.tensor.matmul(bank[B_Y][:, t * P:(t + 1) * P], f_act[0:n, j, t * P:(t + 1) * P],
                                                    w2_l[0:n, j, :], start=(j == 0), stop=(j == NF - 1))
                    last.then_inc(f_yp.sem, 1)
                end_phase(pe, l * 2 + 3)


def rotary_tables(n, hd, window):
    import numpy as np
    half = np.arange(0, hd, 2, dtype=np.float32)
    inv_freq = (np.float32(1.0) / np.float32(10000.0) ** (half / np.float32(hd))).astype(np.float32)
    t = np.arange(n, dtype=np.float32)
    freqs = (t[:, None] * inv_freq[None, :]).astype(np.float32)
    freqs = np.concatenate([freqs, freqs], -1)
    base = ((half + np.float32(0.4 * hd)) / np.float32(1.4 * hd)).astype(np.float32)
    power = ((t - n // 2) / np.float32(window // 2)).astype(np.float32)
    scale = (base[None, :] ** power[:, None]).astype(np.float32)
    scale = np.concatenate([scale, scale], -1)
    cos, sin = np.cos(freqs), np.sin(freqs)
    sin = np.concatenate([-sin[:, :hd // 2], sin[:, hd // 2:]], -1)
    inv = np.float32(1.0) / scale
    return (np.stack([cos * scale, cos * inv]).astype(np.float32),
            np.stack([sin * scale, sin * inv]).astype(np.float32))


def kernel(**inputs):
    import numpy as np
    import concourse.bacc as bacc
    from concourse.bass_utils import run_bass_kernel_spmd

    a = {n.replace("L0_", ""): np.asarray(v) for n, v in inputs.items()}
    hd, kv = 64, a["attn_Wk"].shape[0] // 64
    depth, di = a["ffn_W2"].shape[:2]
    k2 = np.repeat(a["attn_Wk"].reshape(kv, 1, hd, -1), 2, axis=1).reshape(2 * kv * hd, -1)
    bk2 = np.repeat(a["attn_bk"].reshape(kv, 1, hd), 2, axis=1).reshape(kv, 2 * hd)
    blocks = [(o, min(128, di - o)) for o in range(0, di, 128)]
    lcols = np.zeros((depth, 128, 2 * len(blocks) + 2), a["ffn_b1"].dtype)
    for j, (o, n) in enumerate(blocks):
        lcols[:, :n, 2 * j] = a["ffn_b1"][:, o:o + n]
        lcols[:, :n, 2 * j + 1] = a["ffn_b1"][:, di + o:di + o + n]
    lcols[:, :, -2], lcols[:, :, -1] = a["ffn_ln_g"], a["ffn_ln_b"]
    cos, sin = rotary_tables(a["attn_x"].shape[1], hd, 32)
    laid = {
        "x": a["attn_x"],
        "wq_t": a["attn_Wq"].T,
        "wkv_t": np.concatenate([k2, a["attn_Wv"]], 0).T,
        "wo_t": a["attn_Wo"].T,
        "cols": np.concatenate([a["attn_bq"].reshape(-1, 128), bk2], 0).T,
        "rows": np.concatenate([a["attn_bv"], a["attn_bo"], a["attn_sinks"]]),
        "wqkv": a["ffn_Wqkv"],
        "qk_scale": np.concatenate([a["ffn_q_scale"], a["ffn_k_scale"]], 1),
        "wo_l": a["ffn_Wo"],
        "w1": a["ffn_W1"],
        "w2": a["ffn_W2"],
        "b2": a["ffn_b2"],
        "lcols": lcols,
        "rot_cos": cos,
        "rot_sin": sin,
    }
    nc = bacc.Bacc("TRN2", target_bir_lowering=False, num_devices=1)
    arrays, args = {}, []
    for name, v in laid.items():
        v = np.ascontiguousarray(v)
        arrays[f"in_{name}"] = v
        args.append(nc.dram_tensor(f"in_{name}", v.shape, mybir.dt.from_np(v.dtype), kind="ExternalInput").ap())
    args.append(nc.dram_tensor("out_0", a["attn_x"].shape, mybir.dt.float32, kind="ExternalOutput").ap())
    block_program(nc, *args)
    r = run_bass_kernel_spmd(nc, [arrays], core_ids=[0])
    return r.results[0]["out_0"]
```

```python
from contextlib import ExitStack

import concourse.bass as bass
from concourse import mybir

F32 = mybir.dt.float32
F32R = mybir.dt.float32r
BF16 = mybir.dt.bfloat16
ACT = mybir.ActivationFunctionType
ALU = mybir.AluOpType
AX = mybir.AxisListType
P = 128


class Signal:

    def __init__(self, sem, per, prime=0):
        self.sem, self.per, self.prime = sem, per, prime

    def after(self, it, n):
        return it * self.per + (self.prime + n)


def block_program(nc, x, wq_t, wkv_t, wo_t_in, cols, rows, Wqkv, qk_scale, Wo2, W1, W2, b2, lcols, rot_cos, rot_sin, out):
    NB, S, DM = x.shape
    TT = S // P
    NT = NB * TT
    HD = 64
    VW = HD + 1
    KV = (wkv_t.shape[1]) // (3 * HD)
    GH = wq_t.shape[1] // HD // KV
    GP = GH // 2
    PAIRS = KV * GP
    L, _, QKV = Wqkv.shape
    INNER = QKV // 3
    LH = INNER // HD
    LP = LH // 2
    DI = W2.shape[1]
    FB = [(o, min(P, DI - o)) for o in range(0, DI, P)]
    NF = len(FB)
    FT = 4
    FC = NT // FT
    LOCAL = 32
    NEG = -1e30

    ctx = ExitStack()
    with ctx:
        def sb(name, shape, dt=F32):
            return ctx.enter_context(nc.sbuf_tensor(name, shape, dt))

        def sig(name, per=1, prime=0):
            return Signal(ctx.enter_context(nc.semaphore(name)), per, prime)

        x_cur = sb("x_cur", [P, NT, DM])
        x_mid = sb("x_mid", [P, NT, DM])
        ident = sb("ident", [P, P])
        mask_w = sb("mask_w", [P, 384])
        mask_l = sb("mask_l", [P, 288])
        zero_b = sb("zero_b", [1, 256], BF16)
        neg_half = sb("neg_half", [P, 16])
        UG = 2 * GP * P + 2 * P
        wr_arena = sb("wr_arena", [P, KV * UG], F32R)
        w_grp = wr_arena[:, :].rearrange("p (g n) -> p g n", n=UG)
        w_stage = sb("w_stage", [P, UG], F32R)
        wv_hi = sb("wv_hi", [P, KV * HD], F32R)
        wv_lo = sb("wv_lo", [P, KV * HD], F32R)
        f_arena = sb("f_arena", [P, PAIRS * DM])
        wo_t = f_arena[:, :].rearrange("p (q d) -> p q d", d=DM)
        cols_c = sb("cols_c", [P, PAIRS + KV])
        bq_c, bk_c = cols_c[:, 0:PAIRS], cols_c[:, PAIRS:PAIRS + KV]
        rows_b = sb("rows_b", [P, KV * HD + DM + KV * GH])
        bv_b, bo_b = rows_b[:, 0:KV * HD], rows_b[:, KV * HD:KV * HD + DM]
        sink_b = rows_b[:, KV * HD + DM:KV * HD + DM + KV * GH]
        sink_n = sb("sink_n", [P, KV * GH])
        sink_g = sb("sink_g", [P, GH])
        raw = sb("raw", [P, PAIRS * P])
        x_in = sb("x_in", [P, TT, DM])
        x_bo = sb("x_bo", [P, TT * DM])
        xt_hi = sb("xt_hi", [P, S + 1], F32R)
        xt_lo = sb("xt_lo", [P, S + 1], F32R)
        k_hi = sb("k_hi", [P, S], F32R)
        k_lo = sb("k_lo", [P, S], F32R)
        v_a = sb("v_a", [P, TT, VW])
        q_hi = sb("q_hi", [P, 2, S], F32R)
        q_lo = sb("q_lo", [P, 2, S], F32R)
        s_m = sb("s_m", [P, 2, 384])
        p_e = sb("p_e", [P, 2, 384])
        p_t = sb("p_t", [P, 2, 384])
        row_min = sb("row_min", [P, 2 * LH])
        row_sink = sb("row_sink", [P, 2 * LH])
        row_esink = sb("row_esink", [P, 2 * LH])
        row_den = sb("row_den", [P, 2 * LH])
        row_inv = sb("row_inv", [P, 2 * LH])
        o_n = sb("o_n", [P, 2, S])
        o_t = sb("o_t", [P, 2, S])
        z_b = sb("z_b", [P, TT, DM])
        stats = sb("stats", [P, FT, 6])
        moments = sb("moments", [P, FT, 2])
        var_e = sb("var_e", [P, FT])
        rstd = sb("rstd", [P, FT])
        w_raw = raw
        w_hi = wr_arena[:, 0:QKV]
        w_lo = wr_arena[:, QKV:2 * QKV]
        wo_l = sb("wo_l", [P, LP, DM])
        w1_raw = sb("w1_raw", [P, 2 * DI])
        w1_hi = wr_arena[:, 2 * QKV:2 * QKV + 2 * DI]
        w1_lo = wr_arena[:, 2 * QKV + 2 * DI:2 * QKV + 4 * DI]
        w2_l = sb("w2_l", [P, NF, DM])
        lcols_c = sb("lcols_c", [P, 2 * NF + 2])
        b2_b = sb("b2_b", [P, DM])
        b1_c, lng_c, lnb_c = lcols_c, lcols_c[:, 2 * NF:2 * NF + 1], lcols_c[:, 2 * NF + 1:2 * NF + 2]
        qs_b = sb("qs_b", [P, 2, HD])
        qs_r = sb("qs_r", [P, 2, HD])
        cos_t = sb("cos_t", [P, 2, TT, HD])
        sin_t = sb("sin_t", [P, 2, TT, HD])
        cos_s = sb("cos_s", [P, 2, TT, HD])
        sin_s = sb("sin_s", [P, 2, TT, HD])
        HC = 8
        sq = sb("sq", [P, 2, 512])
        r_a = sb("r_a", [P, 2, 512])
        r_b = sb("r_b", [P, 2, 512])
        r_s = sb("r_s", [P, 2, 512])
        r_n = sb("r_n", [P, 2, 512])
        ssum = sb("ssum", [P, 2, HC])
        sfl = sb("sfl", [P, 2, HC])
        rinv = sb("rinv", [P, 2, HC])
        q_neg = sb("q_neg", [P, TT, LH])
        qt_l = f_arena[:, 0:LP * S].rearrange("p (q s) -> p q s", s=S)
        kt_l = f_arena[:, LP * S:2 * LP * S].rearrange("p (q s) -> p q s", s=S)
        v_l = sb("v_l", [P, TT, LH, VW])
        f_in = sb("f_in", [P, FT, DM])
        f_sh = sb("f_sh", [P, FT * P])
        f_xn = sb("f_xn", [P, FT, DM])
        f_x = sb("f_x", [P, FT * P])
        fx_hi = sb("fx_hi", [P, FT * P], F32R)
        fx_lo = sb("fx_lo", [P, FT * P], F32R)
        f_gate = sb("f_gate", [P, NF, FT * P])
        f_act = sb("f_act", [P, NF, FT * P])
        f_y = sb("f_y", [P, FT, DM])
        kv_raw = f_gate[:, :, :].rearrange("p j n -> p (j n)")

        bank = [ctx.enter_context(nc.psum_tensor(f"bank{i}", [P, 512], F32)) for i in range(8)]
        B_P, B_OT, B_S, B_T, B_O, B_Y = 0, 1, [2, 3], [4, 5], 6, 7

        phase_end = sig("phase_end")
        const_ready = sig("const_ready")
        ld_x, ld_w, ld_kv, ld_small, ld_wo = (sig(n) for n in ("ld_x", "ld_w", "ld_kv", "ld_small", "ld_wo"))
        split_hi, split_lo = sig("split_hi"), sig("split_lo")
        staged = sig("staged", 16)
        sink_set = sig("sink_set", 1)
        xin_ready = sig("xin_ready", 2)
        xt_ps, xt_hi_done, xt_lo_done = sig("xt_ps", 1, 1), sig("xt_hi_done", 1), sig("xt_lo_done", 1)
        proj_ready = sig("proj_ready", 6, 1)
        proj_hi = sig("proj_hi", 5)
        proj_done = sig("proj_done", 6, 2)
        y_zero = sig("y_zero", 1)
        y_full = sig("y_full", 1)
        z_done, st_done, mom_done = sig("z_done", 1, 1), sig("st_done", 1), sig("mom_done", 1)
        var_done = sig("var_done", 3)
        ln_done = sig("ln_done", 2)
        cur_done = sig("cur_done", 1)
        out_done = sig("out_done")

        class Att:

            def __init__(self, n, H):
                h = H // 2
                self.H = H
                self.scores = sig(n + "scores", H, h + 1)
                self.masked = sig(n + "masked", 2 * H, H + 1)
                self.exped = sig(n + "exped", H, 2)
                self.transposed = sig(n + "transposed", H, 2)
                self.pt_even = sig(n + "pt_even", h, 1)
                self.pt_odd = sig(n + "pt_odd", h, 1)
                self.pv = sig(n + "pv", H, h + 1)
                self.sink_sub = sig(n + "sink_sub", h)
                self.sink_exp = sig(n + "sink_exp", h)
                self.den = sig(n + "den", h)
                self.inv = sig(n + "inv", h)
                self.o = sig(n + "o", h, 1)
                self.ot = sig(n + "ot", h, 2)
                self.o_sb = sig(n + "o_sb", h, 1)
                self.y = sig(n + "y", h, 2)

        A = Att("w_", GH)
        B = Att("l_", LH)
        lw = sig("lw", 16 * 5)
        lw2 = sig("lw2", 16 * 4)
        lw_hi = sig("lw_hi", 2)
        lw_lo = sig("lw_lo", 2)
        swap = sig("swap", 1)
        tab = sig("tab", 4)
        zeros = sig("zeros", 1)
        lx_in = sig("lx_in", 1)
        lxt_ps = sig("lxt_ps", 1, 1)
        lxt_hi = sig("lxt_hi", 1)
        lxt_lo = sig("lxt_lo", 1)
        lp_ps = sig("lp_ps", 6, 1)
        lp_act = sig("lp_act", 6, 2)
        lp_dve = sig("lp_dve", 4, 1)
        lp_sum = sig("lp_sum", 4, 2)
        lp_max = sig("lp_max", 4)
        lp_rot = sig("lp_rot", 4, 2)
        lp_inv = sig("lp_inv", 4)
        lp_out = sig("lp_out", 4)
        lt_ps = sig("lt_ps", 4, 2)
        lt_act = sig("lt_act", 4, 1)
        l_res = sig("l_res", 1, 1)
        f_inr = sig("f_inr", 1)
        f_t1 = sig("f_t1", 1, 1)
        f_s1 = sig("f_s1", 1, 1)
        f_t2 = sig("f_t2", 1, 1)
        f_st, f_mom, f_var = sig("f_st", 1), sig("f_mom", 1), sig("f_var", 3)
        f_xnr = sig("f_xnr", 1, 1)
        f_t3 = sig("f_t3", 1, 1)
        f_aff = sig("f_aff", 1, 1)
        f_hi, f_lo = sig("f_hi", 1), sig("f_lo", 1, 1)
        f_gp, f_ap = sig("f_gp", NF), sig("f_ap", NF, 1)
        f_gl, f_ac = sig("f_gl", NF, 1), sig("f_ac", NF, 3)
        f_yp, f_ys, f_res = sig("f_yp", 1, 1), sig("f_ys", 1, 1), sig("f_res", 1, 1)
        n_z, n_st, n_mom, n_var, n_out = sig("n_z", 1), sig("n_st", 1), sig("n_mom", 1), sig("n_var", 3), sig("n_out", 1, 1)

        block = ctx.enter_context(nc.Block())

        met = {eng: ctx.enter_context(nc.semaphore("met_" + name)) for eng, name in (
            (nc.sync, "sp"), (nc.gpsimd, "pool"), (nc.scalar, "act"), (nc.vector, "dve"), (nc.tensor, "pe"))}

        def settle(eng):
            eng.sem_inc(met[eng], 1)

        def end_phase(eng, k):
            settle(eng)
            eng.drain().then_inc(phase_end.sem, 1)
            eng.wait_ge(phase_end.sem, k * 5)
            settle(eng)

        ORDER = {0: 2, 1: 3, 2: 5, 3: 6}
        assert GP == len(ORDER)

        def chunk_t(z, c):
            t = c % 2
            return (qt_l if c < 2 else kt_l)[:, 4 * z:4 * z + 4, t * P:(t + 1) * P]

        def chunk_columns(z, n):
            kind, t = ((0, 0), (0, 1), (2, 0), (1, 0), (1, 1), (2, 1))[n]
            return slice(kind * INNER + z * 512, kind * INNER + (z + 1) * 512), t

        QK = {0: 0, 1: 1, 3: 2, 4: 3}
        P_AT = {1: (-2, -1, 0, 1, 2, 3), 0: (8, 9, 10, 11, 12, 13)}
        T_AT = {1: (1, 2, 4, 6), 0: (11, 12, 14, 16)}
        X_AT = 7

        def chunk_before(i, nxt):
            z = 0 if nxt and i >= T_AT[0][0] else 1
            return z, sum(1 for j in T_AT[z] if j <= i)

        def half_work(i, nxt):
            for z in (1, 0) if nxt else (1,):
                n = P_AT[z].index(i) if i in P_AT[z] else None
                c = T_AT[z].index(i) if i in T_AT[z] else None
                if n is not None or c is not None:
                    yield z, n, c

        def halves(t):
            return t.rearrange("p (h z d) -> p h z d", z=2, d=HD // 2)

        def stat(h, t):
            return 4 * (h // 2) + 2 * t + h % 2

        def att_pe(pe, a, it, side, scores, tr, pv, wo_of, ot_free=lambda i: None):
            H = a.H
            for i in range(-2, H + 3):
                side(i)
                h = i + 2
                if h < H:
                    if h >= 2:
                        pe.wait_ge(a.masked.sem, a.masked.after(it, 2 * (h - 1)))
                    scores(h).then_inc(a.scores.sem, 1)
                if 0 <= i < H:
                    pe.wait_ge(a.exped.sem, a.exped.after(it, i + 1))
                    free = a.pt_even if i % 2 == 0 else a.pt_odd
                    pe.wait_ge(free.sem, free.after(it, i // 2))
                    tr(i).then_inc(a.transposed.sem, 1)
                h = i - 1
                if 0 <= h < H:
                    done = a.pt_even if h % 2 == 0 else a.pt_odd
                    pe.wait_ge(done.sem, done.after(it, h // 2 + 1))
                    if h % 2 == 0:
                        pe.wait_ge(a.o.sem, a.o.after(it, h // 2))
                    pv(h).then_inc(a.pv.sem, 1)
                if i >= 3 and i % 2 == 1:
                    p = (i - 3) // 2
                    pe.wait_ge(a.o.sem, a.o.after(it, p + 1))
                    pe.wait_ge(a.o_sb.sem, a.o_sb.after(it, p))
                    ot_free(i)
                    for t in range(TT):
                        last = nc.tensor.transpose(bank[B_OT][:, t * P:(t + 1) * P],
                                                   o_n[:, p % 2, t * P:(t + 1) * P], ident[:, :])
                    last.then_inc(a.ot.sem, 1)
                if i >= 4 and i % 2 == 0:
                    p = i // 2 - 2
                    pe.wait_ge(a.o_sb.sem, a.o_sb.after(it, p + 1))
                    for t in range(TT):
                        last = nc.tensor.matmul(bank[B_Y][:, t * DM:(t + 1) * DM], o_t[:, p % 2, t * P:(t + 1) * P], wo_of(p),
                                                start=False, stop=False, skip_group_check=True)
                    last.then_inc(a.y.sem, 1)

        def att_dve(dve, a, it, W0, W, mask, scale, floor, side, sink):
            H = a.H
            for i in range(-2, H + 3):
                side(i)
                h = i + 2
                if h < H:
                    dve.wait_ge(a.scores.sem, a.scores.after(it, h + 1))
                    dve.wait_ge(a.exped.sem, a.exped.after(it, h - 1))
                    settle(dve)
                    for t, (lo, hi) in enumerate(((0, W0), (W0, W))):
                        c = stat(h, t)
                        nc.vector.tensor_tensor_reduce(
                            out=s_m[:, h % 2, lo:hi], in0=bank[B_S[h % 2]][:, lo:hi], in1=mask[:, lo:hi],
                            scale=scale(t, h), scalar=floor(h), op0=ALU.add, op1=ALU.min,
                            accum_out=row_min[:, c:c + 1]).then_inc(a.masked.sem, 1)
                if sink and 0 <= i < H and i % 2 == 1:
                    dve.wait_ge(a.transposed.sem, a.transposed.after(it, i + 1))
                    dve.wait_ge(a.pv.sem, a.pv.after(it, i - 1))
                    nc.vector.tensor_copy(p_t[:, 1, 0:W], bank[B_T[1]][:, 0:W]).then_inc(a.pt_odd.sem, 1)
                if i >= 2 and i % 2 == 0 and i <= H:
                    p = i // 2 - 1
                    o = bank[B_O][:, 0:4 * VW].rearrange("p (c d) -> p c d", d=VW)
                    sums, inv = o[:, :, HD:VW], row_inv[:, 4 * p:4 * p + 4].unsqueeze(2)
                    dve.wait_ge(a.pv.sem, a.pv.after(it, 2 * p + 2))
                    if sink:
                        den = row_den[:, 4 * p:4 * p + 4].unsqueeze(2)
                        dve.wait_ge(a.sink_exp.sem, a.sink_exp.after(it, p + 1))
                        nc.vector.tensor_tensor(den, sums, row_esink[:, 4 * p:4 * p + 4].unsqueeze(2),
                                                ALU.add).then_inc(a.den.sem, 1)
                        dve.wait_ge(a.den.sem, a.den.after(it, p + 1))
                        sums = den
                    nc.vector.reciprocal(inv, sums).then_inc(a.inv.sem, 1)
                    dve.wait_ge(a.inv.sem, a.inv.after(it, p + 1))
                    dve.wait_ge(a.ot.sem, a.ot.after(it, p - 1))
                    nc.vector.tensor_tensor(o_n[:, p % 2, :].rearrange("p (c d) -> p c d", d=HD), o[:, :, 0:HD],
                                            inv.broadcast_to([P, 4, HD]), ALU.mult).then_inc(a.o.sem, 1)

        def att_act(act, a, it, W0, W, side, sink):
            H = a.H
            for i in range(-2, H + 3):
                side(i)
                h = i + 1
                if 0 <= h < H:
                    act.wait_ge(a.transposed.sem, a.transposed.after(it, h - 1))
                    for t, (lo, hi) in enumerate(((0, W0), (W0, W))):
                        act.wait_ge(a.masked.sem, a.masked.after(it, 2 * h + t + 1))
                        c = stat(h, t)
                        last = nc.scalar.activation(p_e[:, h % 2, lo:hi], s_m[:, h % 2, lo:hi], ACT.Exp,
                                                    bias=row_min[:, c:c + 1], scale=-1.0)
                    last.then_inc(a.exped.sem, 1)
                if 0 <= i < H and (i % 2 == 0 or not sink):
                    done = a.pt_even if i % 2 == 0 else a.pt_odd
                    act.wait_ge(a.transposed.sem, a.transposed.after(it, i + 1))
                    act.wait_ge(a.pv.sem, a.pv.after(it, i - 1))
                    nc.scalar.activation(p_t[:, i % 2, 0:W], bank[B_T[i % 2]][:, 0:W], ACT.Copy).then_inc(done.sem, 1)
                    if sink and i % 2 == 0:
                        p = i // 2
                        act.wait_ge(a.sink_sub.sem, a.sink_sub.after(it, p + 1))
                        nc.scalar.activation(row_esink[:, 4 * p:4 * p + 4], row_sink[:, 4 * p:4 * p + 4],
                                             ACT.Exp).then_inc(a.sink_exp.sem, 1)
                if i >= 3 and i % 2 == 1 and i <= H + 1:
                    p = (i - 3) // 2
                    act.wait_ge(a.ot.sem, a.ot.after(it, p + 1))
                    act.wait_ge(a.y.sem, a.y.after(it, p - 1))
                    nc.scalar.activation(o_t[:, p % 2, :], bank[B_OT][:, 0:S], ACT.Copy).then_inc(a.o_sb.sem, 1)

        def sinks_pool(pool, a, it, sink_of):
            for p in range(a.H // 2):
                c = slice(4 * p, 4 * p + 4)
                pool.wait_ge(a.masked.sem, a.masked.after(it, 4 * p + 4))
                settle(pool)
                nc.gpsimd.tensor_tensor(row_sink[:, c].rearrange("p (t e) -> p t e", t=2),
                                        row_min[:, c].rearrange("p (t e) -> p t e", t=2),
                                        sink_of(p), ALU.add).then_inc(a.sink_sub.sem, 1)

        @block.sync
        def _(sp):
            sp.dma_start(x_cur[:, :, :], x.rearrange("b (t p) d -> p (b t) d", p=P)).then_inc(ld_x.sem, 16)
            sp.dma_start(raw[:, :], wq_t).then_inc(ld_w.sem, 16)
            sp.dma_start(kv_raw, wkv_t).then_inc(ld_kv.sem, 16)
            for dst, src in [(cols_c[:, :], cols), (rows_b[:, :], rows.partition_broadcast(P)),
                             (cos_t[:, :, :, :], rot_cos.rearrange("k (t p) d -> p k t d", p=P)),
                             (sin_t[:, :, :, :], rot_sin.rearrange("k (t p) d -> p k t d", p=P))]:
                sp.dma_start(dst, src).then_inc(ld_small.sem, 16)
            sp.dma_start(wo_t, wo_t_in.rearrange("(q p) n -> p q n", p=P)).then_inc(ld_wo.sem, 16)
            sp.wait_ge(split_lo.sem, KV + 2)
            with sp.Fori(0, NB) as b:
                with sp.Fori(0, KV) as g:
                    it = b * KV + g
                    sp.wait_ge(proj_ready.sem, proj_ready.after(it, 0))
                    sp.dma_start(w_stage[:, :].bitcast(F32),
                                 w_grp[:, bass.ds(g, 1), :].rearrange("p g n -> p (g n)").bitcast(F32)).then_inc(staged.sem, 16)
            end_phase(sp, 1)
            with sp.Fori(0, L) as l:
                sp.dma_start(w_raw[:, 0:QKV], Wqkv[bass.ds(l, 1)].rearrange("l p n -> p (l n)")).then_inc(lw.sem, 16)
                sp.dma_start(wo_l[:, :, :], Wo2[bass.ds(l, 1)].rearrange("l (q p) n -> p (l q) n", p=P)).then_inc(lw.sem, 16)
                sp.dma_start(w1_raw[:, :], W1[bass.ds(l, 1)].rearrange("l p n -> p (l n)")).then_inc(lw.sem, 16)
                sp.dma_start(qs_b[:, :, :].rearrange("p k d -> p (k d)"),
                             qk_scale[bass.ds(l, 1)].rearrange("l n -> (l n)").partition_broadcast(P)).then_inc(lw.sem, 16)
                sp.dma_start(b2_b[:, :], b2[bass.ds(l, 1)].rearrange("l n -> (l n)").partition_broadcast(P)).then_inc(lw.sem, 16)
                for j, (o, n) in enumerate(FB):
                    sp.dma_start(w2_l[0:n, j, :], W2[bass.ds(l, 1), o:o + n, :].rearrange("l p n -> p (l n)")).then_inc(lw2.sem, 16)
                sp.dma_start(lcols_c[:, :], lcols[bass.ds(l, 1)].rearrange("l p n -> p (l n)")).then_inc(lw2.sem, 16)
                end_phase(sp, l * 2 + 2)
                end_phase(sp, l * 2 + 3)
            o_v = out.rearrange("b (t p) d -> p (b t) d", p=P)
            with sp.Fori(0, NB) as b:
                sp.wait_ge(n_out.sem, n_out.after(b, 1))
                sp.dma_start(o_v[:, bass.ds(b * TT, TT), :], x_cur[:, bass.ds(b * TT, TT), :]).then_inc(out_done.sem, 16)
            sp.wait_ge(out_done.sem, 16 * NB)

        N_SMALL = 16 * 4

        def pool_rstd(pool, n, done, it, moments_ready):
            pool.wait_ge(moments_ready.sem, moments_ready.after(it, 1))
            settle(pool)
            nc.gpsimd.tensor_copy(var_e[:, 0:n], moments[:, 0:n, 1]).then_inc(done.sem, 1)
            pool.wait_ge(done.sem, done.after(it, 1))
            settle(pool)
            nc.gpsimd.tensor_scalar(var_e[:, 0:n], var_e[:, 0:n], 1e-5, 1.0, ALU.add, ALU.mult).then_inc(done.sem, 1)
            pool.wait_ge(done.sem, done.after(it, 2))
            nc.gpsimd.tensor_tensor(rstd[:, 0:n], var_e[:, 0:n], neg_half[:, 0:n], ALU.pow).then_inc(done.sem, 1)

        @block.gpsimd
        def _(pool):
            nc.gpsimd.memset(ident[:, :], 0.0).then_inc(const_ready.sem, 1)
            nc.gpsimd.memset(mask_w[:, :], 0.0).then_inc(const_ready.sem, 1)
            nc.gpsimd.memset(mask_l[:, :], 0.0).then_inc(const_ready.sem, 1)
            nc.gpsimd.memset(zero_b[:, :], 0.0).then_inc(const_ready.sem, 1)
            nc.gpsimd.memset(neg_half[:, :], -0.5).then_inc(const_ready.sem, 1)
            nc.gpsimd.memset(v_a[:, :, HD:VW], 1.0)
            nc.gpsimd.memset(v_l[:, :, :, HD:VW], 1.0)
            pool.sem_inc(lp_rot.sem, 2)
            pool.sem_inc(f_lo.sem, 1)
            pool.sem_inc(f_res.sem, 1)
            pool.wait_ge(const_ready.sem, 5)
            nc.gpsimd.affine_select(out=ident[:, :], in_=ident[:, :], compare_op=ALU.not_equal, fill=1.0, base=0,
                                    pattern=[[-1, P]], channel_multiplier=1).then_inc(const_ready.sem, 1)
            nc.gpsimd.affine_select(out=mask_w[:, 0:P], in_=mask_w[:, 0:P], compare_op=ALU.is_ge, fill=NEG, base=0,
                                    pattern=[[-1, P]], channel_multiplier=1).then_inc(const_ready.sem, 1)
            nc.gpsimd.affine_select(out=mask_w[:, P:384], in_=mask_w[:, P:384], compare_op=ALU.is_gt, fill=NEG, base=0,
                                    pattern=[[1, S]], channel_multiplier=-1).then_inc(const_ready.sem, 1)
            nc.gpsimd.affine_select(out=mask_l[:, 0:P], in_=mask_l[:, 0:P], compare_op=ALU.is_ge, fill=NEG, base=0,
                                    pattern=[[-1, P]], channel_multiplier=1).then_inc(const_ready.sem, 1)
            nc.gpsimd.affine_select(out=mask_l[:, P:288], in_=mask_l[:, P:288], compare_op=ALU.is_ge, fill=NEG, base=0,
                                    pattern=[[1, 160]], channel_multiplier=-1).then_inc(const_ready.sem, 1)
            pool.wait_ge(const_ready.sem, 10)
            nc.gpsimd.affine_select(out=mask_w[:, P:384], in_=mask_w[:, P:384], compare_op=ALU.is_ge, fill=NEG, base=P,
                                    pattern=[[-1, S]], channel_multiplier=1).then_inc(const_ready.sem, 1)
            nc.gpsimd.affine_select(out=mask_l[:, 0:P], in_=mask_l[:, 0:P], compare_op=ALU.is_ge, fill=NEG, base=LOCAL,
                                    pattern=[[1, P]], channel_multiplier=-1).then_inc(const_ready.sem, 1)
            nc.gpsimd.affine_select(out=mask_l[:, P:288], in_=mask_l[:, P:288], compare_op=ALU.is_ge, fill=NEG, base=LOCAL,
                                    pattern=[[-1, 160]], channel_multiplier=1).then_inc(const_ready.sem, 1)
            pool.wait_ge(ld_small.sem, N_SMALL)
            nc.gpsimd.tensor_scalar(sink_n[:, :], sink_b[:, :], -1.0, 0.0, ALU.mult, ALU.add).then_inc(const_ready.sem, 1)
            pool.wait_ge(ld_x.sem, 16)
            with pool.Fori(0, NB) as b:
                pool.wait_ge(xt_ps.sem, xt_ps.after(b, 0))
                settle(pool)
                xb = x_cur[:, bass.ds(b * TT, TT), :]
                nc.gpsimd.tensor_copy(x_in[:, :, :], xb).then_inc(xin_ready.sem, 1)
                nc.gpsimd.tensor_tensor(x_bo[:, :].rearrange("p (t d) -> p t d", d=DM), xb,
                                        bo_b[:, :].unsqueeze(1).broadcast_to([P, TT, DM]), ALU.add).then_inc(xin_ready.sem, 1)
                with pool.Fori(0, KV) as g:
                    it = b * KV + g
                    sinks_pool(pool, A, it, lambda p: sink_b[:, bass.ds(g * GH + 2 * p, 2)].unsqueeze(1).broadcast_to([P, 2, 2]))
                pool_rstd(pool, TT, var_done, b, mom_done)
            end_phase(pool, 1)
            with pool.Fori(0, L) as l:
                pool.wait_ge(lw.sem, lw.after(l, 80))
                settle(pool)
                for z in range(2):
                    last = nc.gpsimd.tensor_copy(qs_r[:, :, z * 32:z * 32 + 32], qs_b[:, :, 32 - z * 32:64 - z * 32])
                last.then_inc(swap.sem, 1)
                pool.wait_ge(swap.sem, swap.after(l, 1))
                for k in range(2):
                    nc.gpsimd.tensor_tensor(cos_s[:, k], cos_t[:, k], qs_b[:, k, :].unsqueeze(1).broadcast_to([P, TT, HD]),
                                            ALU.mult).then_inc(tab.sem, 1)
                    nc.gpsimd.tensor_tensor(sin_s[:, k], sin_t[:, k], qs_r[:, k, :].unsqueeze(1).broadcast_to([P, TT, HD]),
                                            ALU.mult).then_inc(tab.sem, 1)
                pool.wait_ge(lw_hi.sem, lw_hi.after(l, 1))
                nc.gpsimd.tensor_tensor(w_lo, w_raw[:, 0:QKV], w_hi.bitcast(F32), ALU.subtract).then_inc(lw_lo.sem, 1)
                pool.wait_ge(lw_hi.sem, lw_hi.after(l, 2))
                nc.gpsimd.tensor_tensor(w1_lo, w1_raw[:, :], w1_hi.bitcast(F32), ALU.subtract).then_inc(lw_lo.sem, 1)
                def load_x(b, it):
                    pool.wait_ge(lxt_ps.sem, lxt_ps.after(it, 0))
                    settle(pool)
                    nc.gpsimd.tensor_copy(x_in[:, :, :], x_cur[:, bass.ds(b * TT, TT), :]).then_inc(lx_in.sem, 1)

                def norm_half(z, it):
                    hs = it * 2 + z
                    for c in range(4):
                        t, kind, buf = c % 2, c // 2, c % 2
                        pool.wait_ge(lp_sum.sem, lp_sum.after(hs, c + 1))
                        pool.wait_ge(lt_ps.sem, lt_ps.after(hs, c - 1))
                        settle(pool)
                        nc.gpsimd.tensor_scalar(sfl[:, buf, :], ssum[:, buf, :], 1e-24, 1.0, ALU.max,
                                                ALU.mult).then_inc(lp_max.sem, 1)
                        nc.gpsimd.tensor_tensor(r_s[:, buf, :], r_a[:, buf, :], r_b[:, buf, :], ALU.add).then_inc(lp_rot.sem, 1)
                        pool.wait_ge(lp_max.sem, lp_max.after(hs, c + 1))
                        nc.gpsimd.tensor_tensor(rinv[:, buf, :], sfl[:, buf, :], neg_half[:, 0:HC], ALU.pow).then_inc(lp_inv.sem, 1)
                        pool.wait_ge(lp_inv.sem, lp_inv.after(hs, c + 1))
                        settle(pool)
                        if kind == 0:
                            if c == 0:
                                pool.wait_ge(B.masked.sem, B.masked.after(it, 0 if z else -LH))
                                settle(pool)
                            nc.gpsimd.tensor_scalar(q_neg[:, t, z * HC:(z + 1) * HC], rinv[:, buf, :], -8.0, 0.0,
                                                    ALU.mult, ALU.add).then_inc(lp_out.sem, 1)
                        else:
                            pool.wait_ge(lp_rot.sem, lp_rot.after(hs, c + 1))
                            nc.gpsimd.tensor_tensor(r_n[:, buf, :].rearrange("p (h d) -> p h d", d=HD),
                                                    r_s[:, buf, :].rearrange("p (h d) -> p h d", d=HD),
                                                    rinv[:, buf, :].unsqueeze(2).broadcast_to([P, HC, HD]),
                                                    ALU.mult).then_inc(lp_out.sem, 1)

                load_x(0, l * NB)
                norm_half(0, l * NB)
                with pool.Fori(0, NB - 1) as b:
                    it = l * NB + b
                    norm_half(1, it)
                    load_x(b + 1, it + 1)
                    norm_half(0, it + 1)
                norm_half(1, l * NB + (NB - 1))
                end_phase(pool, l * 2 + 2)
                with pool.Fori(0, FC) as c:
                    it = l * FC + c
                    pool.wait_ge(f_t1.sem, f_t1.after(it, 0))
                    settle(pool)
                    nc.gpsimd.tensor_copy(f_in[:, :, :], x_cur[:, bass.ds(c * FT, FT), :]).then_inc(f_inr.sem, 1)
                    pool_rstd(pool, FT, f_var, it, f_mom)
                    pool.wait_ge(f_hi.sem, f_hi.after(it, 1))
                    pool.wait_ge(f_ap.sem, f_ap.after(it, 0))
                    nc.gpsimd.tensor_tensor(fx_lo[:, :], f_x[:, :], fx_hi[:, :].bitcast(F32), ALU.subtract).then_inc(f_lo.sem, 1)
                    pool.wait_ge(f_ys.sem, f_ys.after(it, 1))
                    settle(pool)
                    nc.gpsimd.tensor_tensor(x_cur[:, bass.ds(c * FT, FT), :], f_y[:, :, :],
                                            b2_b[:, :].unsqueeze(1).broadcast_to([P, FT, DM]), ALU.add).then_inc(f_res.sem, 1)
                end_phase(pool, l * 2 + 3)
            with pool.Fori(0, NB) as b:
                pool_rstd(pool, TT, n_var, b, n_mom)

        @block.scalar
        def _(act):
            act.sem_inc(A.exped.sem, 2)
            act.sem_inc(A.pt_even.sem, 1)
            act.sem_inc(A.o_sb.sem, 1)
            act.sem_inc(B.exped.sem, 2)
            act.sem_inc(B.pt_even.sem, 1)
            act.sem_inc(B.o_sb.sem, 1)
            act.sem_inc(B.pt_odd.sem, 1)
            act.sem_inc(lt_act.sem, 1)
            act.sem_inc(lp_act.sem, 2)
            act.sem_inc(f_s1.sem, 1)
            act.sem_inc(f_aff.sem, 1)
            act.sem_inc(f_gl.sem, 1)
            K0, KW = 2 * GP * P, KV * P
            act.wait_ge(ld_w.sem, 16)
            for n in range(KV):
                nc.scalar.activation(w_grp[:, n, 0:GP * P], raw[:, n * GP * P:(n + 1) * GP * P], ACT.Copy).then_inc(split_hi.sem, 1)
            act.wait_ge(ld_kv.sem, 16)
            nc.scalar.activation(w_grp[:, :, K0:K0 + P], kv_raw[:, 0:KW].rearrange("p (g n) -> p g n", n=P),
                                 ACT.Copy).then_inc(split_hi.sem, 1)
            nc.scalar.activation(wv_hi[:, :], kv_raw[:, KW:], ACT.Copy).then_inc(split_hi.sem, 1)
            act.wait_ge(ld_small.sem, N_SMALL)
            with act.Fori(0, NB) as b:
                act.wait_ge(xt_ps.sem, xt_ps.after(b, 1))
                nc.scalar.activation(xt_hi[:, 0:S], bank[0][:, 0:S], ACT.Copy).then_inc(xt_hi_done.sem, 1)

                def q_hi_of(p, it, g):
                    act.wait_ge(proj_ready.sem, proj_ready.after(it, ORDER[p]))
                    act.wait_ge(A.scores.sem, A.scores.after(it, 2 * p - 2))
                    nc.scalar.activation(q_hi[:, p % 2, :], bank[B_P][:, 0:S], ACT.Identity,
                                         bias=bq_c[:, bass.ds(g * GP + p, 1)]).then_inc(proj_hi.sem, 1)

                def ahead(k, it, g):
                    if k == 0:
                        act.wait_ge(proj_ready.sem, proj_ready.after(it, 1))
                        act.wait_ge(A.scores.sem, A.scores.after(it, 0))
                        nc.scalar.activation(k_hi[:, :], bank[B_P][:, 0:S], ACT.Identity,
                                             bias=bk_c[:, bass.ds(g, 1)]).then_inc(proj_hi.sem, 1)
                    elif k < 3:
                        q_hi_of(k - 1, it, g)

                def body(g, nxt):
                    it = b * KV + g

                    def side(i):
                        if i in (0, 2):
                            q_hi_of(2 + i // 2, it, g)
                        if nxt and 6 <= i < 10:
                            ahead(i - 6, it + 1, g + 1)

                    att_act(act, A, it, P, 384, side, True)

                for k in range(4):
                    ahead(k, b * KV, 0)
                with act.Fori(0, KV - 1) as g:
                    body(g, True)
                body(KV - 1, False)
                act.wait_ge(ln_done.sem, ln_done.after(b, 2))
                nc.scalar.activation(x_cur[:, bass.ds(b * TT, TT), :], x_mid[:, bass.ds(b * TT, TT), :],
                                     ACT.Copy).then_inc(cur_done.sem, 1)
            end_phase(act, 1)
            with act.Fori(0, L) as l:
                act.wait_ge(lw.sem, lw.after(l, 80))
                nc.scalar.activation(w_hi, w_raw[:, 0:QKV], ACT.Copy).then_inc(lw_hi.sem, 1)
                nc.scalar.activation(w1_hi, w1_raw[:, :], ACT.Copy).then_inc(lw_hi.sem, 1)
                def shift_x(it):
                    act.wait_ge(lxt_ps.sem, lxt_ps.after(it, 1))
                    act.wait_ge(lp_ps.sem, lp_ps.after(it * 2, 0))
                    nc.scalar.activation(xt_hi[0:HD, 0:S], bank[B_P][0:HD, 0:S], ACT.Copy)
                    nc.scalar.activation(xt_hi[HD:P, 1:S + 1], bank[B_P][HD:P, 0:S], ACT.Copy).then_inc(lxt_hi.sem, 1)

                def project(z, n, it):
                    hs = it * 2 + z
                    act.wait_ge(lp_ps.sem, lp_ps.after(hs, n + 1))
                    if n in QK:
                        act.wait_ge(lp_sum.sem, lp_sum.after(hs, QK[n] - 1))
                        nc.scalar.activation(sq[:, QK[n] % 2, :], bank[B_P][:, :], ACT.Square).then_inc(lp_act.sem, 1)
                    else:
                        act.wait_ge(B.pv.sem, B.pv.after(it, 0 if z else -HC))
                        nc.scalar.activation(v_l[:, n // 3, z * HC:(z + 1) * HC, 0:HD],
                                             bank[B_P][:, :].rearrange("p (h d) -> p h d", d=HD), ACT.Copy).then_inc(lp_act.sem, 1)

                def keep_chunk(z, c, it):
                    hs = it * 2 + z
                    act.wait_ge(lt_ps.sem, lt_ps.after(hs, c + 1))
                    act.wait_ge(B.scores.sem, B.scores.after(it, 0 if z else -HC))
                    nc.scalar.activation(chunk_t(z, c), bank[B_OT][:, :].rearrange("p (q c) -> p q c", c=P),
                                         ACT.Copy).then_inc(lt_act.sem, 1)

                def batch(it, nxt):
                    def side(i):
                        if nxt and i == X_AT:
                            shift_x(it + 1)
                        for z, n, c in half_work(i, nxt):
                            if n is not None:
                                project(z, n, it + (1 - z))
                            if c is not None:
                                keep_chunk(z, c, it + (1 - z))

                    att_act(act, B, it, P, 288, side, False)

                shift_x(l * NB)
                for n in range(6):
                    project(0, n, l * NB)
                    if n >= 2:
                        keep_chunk(0, n - 2, l * NB)
                with act.Fori(0, NB - 1) as b:
                    batch(l * NB + b, True)
                batch(l * NB + (NB - 1), False)
                end_phase(act, l * 2 + 2)
                act.wait_ge(lw2.sem, lw2.after(l, 16 * 4))
                settle(act)
                with act.Fori(0, FC) as c:
                    it = l * FC + c
                    act.wait_ge(f_t1.sem, f_t1.after(it, 1))
                    act.wait_ge(f_t2.sem, f_t2.after(it, 0))
                    nc.scalar.activation(f_sh[0:HD, :], bank[0][0:HD, :], ACT.Copy)
                    nc.scalar.activation(f_sh[HD:P, :].rearrange("p (h s) -> p h s", s=S)[:, :, 1:S],
                                         bank[0][HD:P, :].rearrange("p (h s) -> p h s", s=S)[:, :, 0:S - 1],
                                         ACT.Copy).then_inc(f_s1.sem, 1)
                    act.wait_ge(f_t3.sem, f_t3.after(it, 1))
                    act.wait_ge(f_lo.sem, f_lo.after(it, 0))
                    act.wait_ge(f_ap.sem, f_ap.after(it, 0))
                    nc.scalar.activation(f_x[:, :], bank[2][:, :], ACT.Identity, bias=lnb_c[:, 0:1],
                                         scale=lng_c[:, 0:1]).then_inc(f_aff.sem, 1)
                    act.wait_ge(f_aff.sem, f_aff.after(it, 1))
                    nc.scalar.activation(fx_hi[:, :], f_x[:, :], ACT.Copy).then_inc(f_hi.sem, 1)
                    for j, (o, n) in enumerate(FB):
                        act.wait_ge(f_gp.sem, f_gp.after(it, j + 1))
                        act.wait_ge(f_ac.sem, f_ac.after(it, j - 2))
                        nc.scalar.activation(f_gate[0:n, j, :], bank[3 + j % 2][0:n, :], ACT.Gelu,
                                             bias=b1_c[0:n, 2 * j + 1:2 * j + 2]).then_inc(f_gl.sem, 1)
                end_phase(act, l * 2 + 3)

        def dve_stats(dve, n, src, st, mom, it):
            for t in range(n):
                last = nc.vector.bn_stats(stats[:, t, :], src(t))
            last.then_inc(st.sem, 1)
            dve.wait_ge(st.sem, st.after(it, 1))
            settle(dve)
            for t in range(n):
                last = nc.vector.bn_aggr(moments[:, t, :], stats[:, t, :])
            last.then_inc(mom.sem, 1)

        @block.vector
        def _(dve):
            dve.sem_inc(proj_done.sem, 2)
            dve.sem_inc(A.masked.sem, A.masked.prime)
            dve.sem_inc(B.masked.sem, B.masked.prime)
            dve.sem_inc(lp_dve.sem, 1)
            dve.sem_inc(A.pt_odd.sem, 1)
            dve.sem_inc(A.o.sem, 1)
            dve.sem_inc(B.o.sem, 1)
            dve.sem_inc(z_done.sem, 1)
            dve.sem_inc(lp_sum.sem, 2)
            dve.sem_inc(l_res.sem, 1)
            dve.sem_inc(f_xnr.sem, 1)
            dve.sem_inc(f_ac.sem, 3)
            dve.sem_inc(f_ys.sem, 1)
            dve.sem_inc(n_out.sem, 1)
            K0, KW = 2 * GP * P, KV * P
            for n in range(KV):
                dve.wait_ge(split_hi.sem, n + 1)
                nc.vector.tensor_tensor(w_grp[:, n, GP * P:2 * GP * P], raw[:, n * GP * P:(n + 1) * GP * P],
                                        w_grp[:, n, 0:GP * P].bitcast(F32), ALU.subtract).then_inc(split_lo.sem, 1)
            dve.wait_ge(split_hi.sem, KV + 1)
            nc.vector.tensor_tensor(w_grp[:, :, K0 + P:K0 + 2 * P], kv_raw[:, 0:KW].rearrange("p (g n) -> p g n", n=P),
                                    w_grp[:, :, K0:K0 + P].bitcast(F32), ALU.subtract).then_inc(split_lo.sem, 1)
            dve.wait_ge(split_hi.sem, KV + 2)
            nc.vector.tensor_tensor(wv_lo[:, :], kv_raw[:, KW:], wv_hi[:, :].bitcast(F32), ALU.subtract).then_inc(split_lo.sem, 1)
            dve.wait_ge(ld_small.sem, N_SMALL)
            dve.wait_ge(const_ready.sem, 14)
            with dve.Fori(0, NB) as b:
                dve.wait_ge(xt_hi_done.sem, xt_hi_done.after(b, 1))
                nc.vector.tensor_tensor(xt_lo[:, 0:S], bank[0][:, 0:S], xt_hi[:, 0:S].bitcast(F32),
                                        ALU.subtract).then_inc(xt_lo_done.sem, 1)

                def q_lo_of(p, it, g):
                    dve.wait_ge(proj_hi.sem, proj_hi.after(it, ORDER[p] - (1 if p > 1 else 0)))
                    nc.vector.scalar_tensor_tensor(q_lo[:, p % 2, :], bank[B_P][:, 0:S], bq_c[:, bass.ds(g * GP + p, 1)],
                                                   q_hi[:, p % 2, :].bitcast(F32), ALU.add,
                                                   ALU.subtract).then_inc(proj_done.sem, 1)

                def ahead(k, it, g):
                    if k == 0:
                        dve.wait_ge(proj_hi.sem, proj_hi.after(it, 1))
                        nc.vector.scalar_tensor_tensor(k_lo[:, :], bank[B_P][:, 0:S], bk_c[:, bass.ds(g, 1)],
                                                       k_hi[:, :].bitcast(F32), ALU.add, ALU.subtract).then_inc(proj_done.sem, 1)
                    elif k < 3:
                        q_lo_of(k - 1, it, g)
                    else:
                        dve.wait_ge(proj_ready.sem, proj_ready.after(it, 4))
                        dve.wait_ge(A.pv.sem, A.pv.after(it, 0))
                        nc.vector.tensor_tensor(v_a[:, :, 0:HD], bank[B_P][:, 0:TT * HD].rearrange("p (t d) -> p t d", d=HD),
                                                bv_b[:, bass.ds(g * HD, HD)].unsqueeze(1).broadcast_to([P, TT, HD]),
                                                ALU.add).then_inc(proj_done.sem, 1)

                def body(g, nxt):
                    it = b * KV + g
                    nc.vector.tensor_copy(sink_g[:, :], sink_n[:, bass.ds(g * GH, GH)]).then_inc(sink_set.sem, 1)
                    dve.wait_ge(sink_set.sem, sink_set.after(it, 1))

                    def side(i):
                        if i in (0, 2):
                            q_lo_of(2 + i // 2, it, g)
                        if nxt and 6 <= i < 10:
                            ahead(i - 6, it + 1, g + 1)

                    att_dve(dve, A, it, P, 384, mask_w, lambda t, h: -0.125, lambda h: sink_g[:, h:h + 1], side, True)

                for k in range(4):
                    ahead(k, b * KV, 0)
                with dve.Fori(0, KV - 1) as g:
                    body(g, True)
                body(KV - 1, False)
                dve.wait_ge(y_full.sem, y_full.after(b, 1))
                dve.wait_ge(xin_ready.sem, xin_ready.after(b, 2))
                nc.vector.tensor_tensor(z_b[:, :, :].rearrange("p t d -> p (t d)"), bank[B_Y][:, 0:S], x_bo[:, :],
                                        ALU.add).then_inc(z_done.sem, 1)
                dve.wait_ge(z_done.sem, z_done.after(b, 1))
                dve_stats(dve, TT, lambda t: z_b[:, t, :], st_done, mom_done, b)
                dve.wait_ge(var_done.sem, var_done.after(b, 3))
                for t in range(TT):
                    nc.vector.tensor_scalar(x_mid[:, bass.ds(b * TT + t, 1), :].rearrange("p t d -> p (t d)"), z_b[:, t, :],
                                            moments[:, t, 0:1], rstd[:, t:t + 1], ALU.subtract,
                                            ALU.mult).then_inc(ln_done.sem, 1)
            end_phase(dve, 1)
            with dve.Fori(0, L) as l:
                nc.vector.memset(xt_hi[HD:P, 0:1].bitcast(F32), 0.0)
                nc.vector.memset(xt_lo[HD:P, 0:1].bitcast(F32), 0.0)
                nc.vector.memset(f_sh[HD:P, :].rearrange("p (h s) -> p h s", s=S)[:, :, 0:1], 0.0).then_inc(zeros.sem, 1)
                dve.wait_ge(tab.sem, tab.after(l, 4))
                settle(dve)
                def shift_x(it):
                    dve.wait_ge(lxt_hi.sem, lxt_hi.after(it, 1))
                    nc.vector.tensor_tensor(xt_lo[0:HD, 0:S], bank[B_P][0:HD, 0:S], xt_hi[0:HD, 0:S].bitcast(F32), ALU.subtract)
                    nc.vector.tensor_tensor(xt_lo[HD:P, 1:S + 1], bank[B_P][HD:P, 0:S], xt_hi[HD:P, 1:S + 1].bitcast(F32),
                                            ALU.subtract).then_inc(lxt_lo.sem, 1)

                def project(z, n, it):
                    if n not in QK:
                        return
                    hs, c, t = it * 2 + z, QK[n], QK[n] % 2
                    kind, ps = c // 2, bank[B_P][:, :]
                    dve.wait_ge(lp_act.sem, lp_act.after(hs, n + 1))
                    dve.wait_ge(lp_rot.sem, lp_rot.after(hs, c - 1))
                    nc.vector.tensor_tensor(
                        r_a[:, t, :].rearrange("p (h d) -> p h d", d=HD), ps.rearrange("p (h d) -> p h d", d=HD),
                        cos_s[:, kind, t, :].unsqueeze(1).broadcast_to([P, HC, HD]), ALU.mult)
                    for y in range(2):
                        last = nc.vector.tensor_tensor(
                            halves(r_b[:, t, :])[:, :, y, :], halves(ps)[:, :, 1 - y, :],
                            sin_s[:, kind, t, y * 32:y * 32 + 32].unsqueeze(1).broadcast_to([P, HC, 32]), ALU.mult)
                    last.then_inc(lp_dve.sem, 1)
                    nc.vector.tensor_reduce(ssum[:, t, :], sq[:, t, :].rearrange("p (h d) -> p h d", d=HD),
                                            AX.X, ALU.add).then_inc(lp_sum.sem, 1)

                def batch(b, it, nxt):
                    def side(i):
                        if nxt and i == X_AT:
                            shift_x(it + 1)
                        for z, n, c in half_work(i, nxt):
                            if n is not None:
                                project(z, n, it + (1 - z))

                    att_dve(dve, B, it, P, 288, mask_l, lambda t, h: q_neg[:, t, h:h + 1], lambda h: 3.0e38, side, False)
                    dve.wait_ge(B.y.sem, B.y.after(it, LP))
                    xb = x_cur[:, bass.ds(b * TT, TT), :].rearrange("p t d -> p (t d)")
                    nc.vector.tensor_tensor(xb, bank[B_Y][:, 0:S], xb, ALU.add).then_inc(l_res.sem, 1)

                shift_x(l * NB)
                for n in range(6):
                    project(0, n, l * NB)
                with dve.Fori(0, NB - 1) as b:
                    batch(b, l * NB + b, True)
                batch(NB - 1, l * NB + (NB - 1), False)
                end_phase(dve, l * 2 + 2)
                with dve.Fori(0, FC) as c:
                    it = l * FC + c
                    dve.wait_ge(f_t2.sem, f_t2.after(it, 1))
                    dve_stats(dve, FT, lambda t: bank[1][:, t * P:(t + 1) * P], f_st, f_mom, it)
                    dve.wait_ge(f_var.sem, f_var.after(it, 3))
                    dve.wait_ge(f_t3.sem, f_t3.after(it, 0))
                    for t in range(FT):
                        last = nc.vector.tensor_scalar(f_xn[:, t, :], bank[1][:, t * P:(t + 1) * P], moments[:, t, 0:1],
                                                       rstd[:, t:t + 1], ALU.subtract, ALU.mult)
                    last.then_inc(f_xnr.sem, 1)
                    dve.wait_ge(f_yp.sem, f_yp.after(it, 0))
                    for j, (o, n) in enumerate(FB):
                        dve.wait_ge(f_ap.sem, f_ap.after(it, j + 1))
                        dve.wait_ge(f_gl.sem, f_gl.after(it, j + 1))
                        nc.vector.scalar_tensor_tensor(f_act[0:n, j, :], bank[5 + j % 2][0:n, :], b1_c[0:n, 2 * j:2 * j + 1],
                                                       f_gate[0:n, j, :], ALU.add, ALU.mult).then_inc(f_ac.sem, 1)
                    dve.wait_ge(f_yp.sem, f_yp.after(it, 1))
                    dve.wait_ge(f_res.sem, f_res.after(it, 0))
                    nc.vector.tensor_tensor(f_y[:, :, :].rearrange("p t d -> p (t d)"), bank[B_Y][:, :],
                                            x_cur[:, bass.ds(c * FT, FT), :].rearrange("p t d -> p (t d)"),
                                            ALU.add).then_inc(f_ys.sem, 1)
                end_phase(dve, l * 2 + 3)
            with dve.Fori(0, NB) as b:
                dve.wait_ge(n_out.sem, n_out.after(b, 0))
                xb = x_cur[:, bass.ds(b * TT, TT), :]
                nc.vector.tensor_tensor(z_b[:, :, :], xb, x_mid[:, bass.ds(b * TT, TT), :], ALU.add).then_inc(n_z.sem, 1)
                dve.wait_ge(n_z.sem, n_z.after(b, 1))
                dve_stats(dve, TT, lambda t: z_b[:, t, :], n_st, n_mom, b)
                dve.wait_ge(n_var.sem, n_var.after(b, 3))
                for t in range(TT):
                    last = nc.vector.tensor_scalar(x_cur[:, bass.ds(b * TT + t, 1), :].rearrange("p t d -> p (t d)"),
                                                   z_b[:, t, :], moments[:, t, 0:1], rstd[:, t:t + 1], ALU.subtract, ALU.mult)
                last.then_inc(n_out.sem, 1)

        def split_mm(dst, lhs, rhs, start=True):
            nc.tensor.matmul(dst, lhs[0], rhs[0], start=True, stop=False)
            nc.tensor.matmul(dst, lhs[1], rhs[0], start=False, stop=False)
            return nc.tensor.matmul(dst, lhs[0], rhs[1], start=False, stop=True)

        def o_ps(h, t):
            return bank[B_O][:, (2 * t + h % 2) * VW:(2 * t + h % 2 + 1) * VW]

        @block.tensor
        def _(pe):
            for a in (A, B):
                for g in (a.scores, a.transposed, a.pv, a.ot, a.y):
                    pe.sem_inc(g.sem, g.prime)
            pe.sem_inc(proj_ready.sem, 1)
            pe.sem_inc(xt_ps.sem, 1)
            pe.sem_inc(lxt_ps.sem, 1)
            pe.sem_inc(lp_ps.sem, 1)
            pe.sem_inc(lt_ps.sem, 2)
            for g in (f_t1, f_t2, f_t3, f_ap, f_yp):
                pe.sem_inc(g.sem, 1)
            pe.wait_ge(const_ready.sem, 14)
            pe.wait_ge(split_lo.sem, KV + 2)
            pe.wait_ge(ld_wo.sem, 16)
            K0 = 2 * GP * P
            xt = (xt_hi[:, 0:S], xt_lo[:, 0:S])
            with pe.Fori(0, NB) as b:
                pe.wait_ge(z_done.sem, z_done.after(b, 0))
                nc.tensor.matmul(bank[B_Y][:, 0:S], zero_b[0:1, 0:P], zero_b[0:1, 0:S], start=True, stop=True)
                pe.wait_ge(xin_ready.sem, xin_ready.after(b, 1))
                pe.wait_ge(proj_done.sem, b * (KV * 6) + 2)
                for t in range(TT):
                    last = nc.tensor.transpose(bank[0][:, t * P:(t + 1) * P], x_in[:, t, :], ident[:, :])
                last.then_inc(xt_ps.sem, 1)
                pe.wait_ge(xt_lo_done.sem, xt_lo_done.after(b, 1))
                settle(pe)

                def q_of(p, it):
                    pe.wait_ge(proj_done.sem, proj_done.after(it, ORDER[p] - 1))
                    split_mm(bank[B_P][:, 0:S], (w_stage[:, p * P:(p + 1) * P],
                                                 w_stage[:, (GP + p) * P:(GP + p + 1) * P]), xt).then_inc(proj_ready.sem, 1)

                def ahead(k, it, g):
                    if k == 0:
                        pe.wait_ge(staged.sem, staged.after(it, 16))
                        pe.wait_ge(proj_done.sem, proj_done.after(it, 0))
                        split_mm(bank[B_P][:, 0:S], (w_stage[:, K0:K0 + P], w_stage[:, K0 + P:K0 + 2 * P]), xt)\
                            .then_inc(proj_ready.sem, 1)
                    elif k < 3:
                        q_of(k - 1, it)
                    else:
                        pe.wait_ge(proj_done.sem, proj_done.after(it, 3))
                        for t in range(TT):
                            ts = slice(t * P, (t + 1) * P)
                            last = split_mm(bank[B_P][:, t * HD:(t + 1) * HD], (xt_hi[:, ts], xt_lo[:, ts]),
                                            (wv_hi[:, bass.ds(g * HD, HD)], wv_lo[:, bass.ds(g * HD, HD)]))
                        last.then_inc(proj_ready.sem, 1)

                def body(g, nxt):
                    it = b * KV + g

                    def side(i):
                        if i in (0, 2):
                            q_of(2 + i // 2, it)
                        if nxt and 6 <= i < 10:
                            ahead(i - 6, it + 1, g + 1)

                    def scores(h):
                        p, r = h // 2, slice(HD * (h % 2), HD * (h % 2) + HD)
                        pe.wait_ge(proj_done.sem, proj_done.after(it, ORDER[p]))
                        ps = bank[B_S[h % 2]]
                        split_mm(ps[:, 0:P], (q_hi[r, p % 2, 0:P], q_lo[r, p % 2, 0:P]), (k_hi[r, 0:P], k_lo[r, 0:P]))
                        return split_mm(ps[:, P:384], (q_hi[r, p % 2, P:S], q_lo[r, p % 2, P:S]), (k_hi[r, :], k_lo[r, :]))

                    def tr(h):
                        for k in range(3):
                            last = nc.tensor.transpose(bank[B_T[h % 2]][:, k * P:(k + 1) * P],
                                                       p_e[:, h % 2, k * P:(k + 1) * P], ident[:, :])
                        return last

                    def pv(h):
                        pt = p_t[:, h % 2, :]
                        pe.wait_ge(proj_done.sem, proj_done.after(it, 4))
                        nc.tensor.matmul(o_ps(h, 0), pt[:, 0:P], v_a[:, 0, :], start=True, stop=True)
                        nc.tensor.matmul(o_ps(h, 1), pt[:, P:2 * P], v_a[:, 0, :], start=True, stop=False)
                        return nc.tensor.matmul(o_ps(h, 1), pt[:, 2 * P:3 * P], v_a[:, 1, :], start=False, stop=True)

                    att_pe(pe, A, it, side, scores, tr, pv,
                           lambda p: wo_t[:, bass.ds(g * GP + p, 1), :].rearrange("p q d -> p (q d)"))

                for k in range(4):
                    ahead(k, b * KV, 0)
                with pe.Fori(0, KV - 1) as g:
                    body(g, True)
                body(KV - 1, False)
                pe.drain().then_inc(y_full.sem, 1)
            end_phase(pe, 1)
            with pe.Fori(0, L) as l:
                pe.wait_ge(lw_lo.sem, lw_lo.after(l, 2))
                pe.wait_ge(zeros.sem, zeros.after(l, 1))
                settle(pe)
                def turn_x(it):
                    pe.wait_ge(lx_in.sem, lx_in.after(it, 1))
                    pe.wait_ge(lp_act.sem, lp_act.after(it * 2, 0))
                    for t in range(TT):
                        last = nc.tensor.transpose(bank[B_P][:, t * P:(t + 1) * P], x_in[:, t, :], ident[:, :])
                    last.then_inc(lxt_ps.sem, 1)

                def project(z, n, it):
                    hs = it * 2 + z
                    if z == 0 and n == 0:
                        pe.wait_ge(lxt_lo.sem, lxt_lo.after(it, 1))
                    if n - 1 in QK:
                        pe.wait_ge(lp_dve.sem, lp_dve.after(hs, QK[n - 1] + 1))
                    else:
                        pe.wait_ge(lp_act.sem, lp_act.after(hs, n))
                    ws, t = chunk_columns(z, n)
                    ts = slice(t * P, (t + 1) * P)
                    split_mm(bank[B_P][:, :], (xt_hi[:, ts], xt_lo[:, ts]), (w_hi[:, ws], w_lo[:, ws])).then_inc(lp_ps.sem, 1)

                def turn_chunk(z, c, it, last_pair):
                    hs = it * 2 + z
                    pe.wait_ge(lp_out.sem, lp_out.after(hs, c + 1))
                    pe.wait_ge(lt_act.sem, lt_act.after(hs, c))
                    pe.wait_ge(B.o_sb.sem, last_pair)
                    src = r_s if c < 2 else r_n
                    for k in range(4):
                        last = nc.tensor.transpose(bank[B_OT][:, k * P:(k + 1) * P],
                                                   src[:, c % 2, k * P:(k + 1) * P], ident[:, :])
                    last.then_inc(lt_ps.sem, 1)

                def scores(h):
                    p, r = h // 2, slice(HD * (h % 2), HD * (h % 2) + HD)
                    ps = bank[B_S[h % 2]]
                    nc.tensor.matmul(ps[:, 0:P], qt_l[r, p, 0:P], kt_l[r, p, 0:P], start=True, stop=True)
                    return nc.tensor.matmul(ps[:, P:288], qt_l[r, p, P:S], kt_l[r, p, P - LOCAL:S], start=True, stop=True)

                def tr(h):
                    ps, pr = bank[B_T[h % 2]], p_e[:, h % 2, :]
                    nc.tensor.transpose(ps[:, 0:P], pr[:, 0:P], ident[:, :])
                    nc.tensor.transpose(ps[:, P:2 * P], pr[:, P + LOCAL:2 * P + LOCAL], ident[:, :])
                    return nc.tensor.transpose(ps[:, 2 * P:2 * P + LOCAL], pr[0:LOCAL, LOCAL:P + LOCAL], ident[0:LOCAL, 0:LOCAL])

                def pv(h):
                    pt = p_t[:, h % 2, :]
                    nc.tensor.matmul(o_ps(h, 0), pt[:, 0:P], v_l[:, 0, h, :], start=True, stop=True)
                    nc.tensor.matmul(o_ps(h, 1), pt[:, P:2 * P], v_l[:, 1, h, :], start=True, stop=True)
                    return nc.tensor.matmul(o_ps(h, 1)[0:LOCAL], pt[P - LOCAL:P, 2 * P:2 * P + LOCAL],
                                            v_l[P - LOCAL:P, 0, h, :], start=False, stop=True, skip_group_check=True)

                def batch(it, nxt):
                    def side(i):
                        if nxt and i == X_AT:
                            turn_x(it + 1)
                        if i == 3:
                            pe.wait_ge(l_res.sem, l_res.after(it, 0))
                            nc.tensor.matmul(bank[B_Y][:, 0:S], zero_b[0:1, 0:P], zero_b[0:1, 0:S], start=True, stop=True)
                        for z, n, c in half_work(i, nxt):
                            if n is not None:
                                project(z, n, it + (1 - z))
                            if c is not None:
                                turn_chunk(z, c, it + (1 - z), B.o_sb.after(it, min(LP, max(0, (i - 2) // 2))))
                        if i in (-2, 6):
                            hs = it * 2 + (1 if i == 6 else 0)
                            pe.wait_ge(lt_act.sem, lt_act.after(hs, 4))
                            pe.wait_ge(lp_act.sem, lp_act.after(hs, 6))

                    def ot_free(i):
                        z, c = chunk_before(i, nxt)
                        if c:
                            pe.wait_ge(lt_act.sem, lt_act.after((it + (1 - z)) * 2 + z, c))

                    att_pe(pe, B, it, side, scores, tr, pv, lambda p: wo_l[:, p, :], ot_free)

                turn_x(l * NB)
                for n in range(6):
                    project(0, n, l * NB)
                    if n >= 2:
                        turn_chunk(0, n - 2, l * NB, B.o_sb.after(l * NB, 0))
                with pe.Fori(0, NB - 1) as b:
                    batch(l * NB + b, True)
                batch(l * NB + (NB - 1), False)
                end_phase(pe, l * 2 + 2)
                pe.wait_ge(lw2.sem, lw2.after(l, 16 * 4))
                settle(pe)
                with pe.Fori(0, FC) as c:
                    it = l * FC + c
                    pe.wait_ge(f_inr.sem, f_inr.after(it, 1))
                    pe.wait_ge(f_s1.sem, f_s1.after(it, 0))
                    for t in range(FT):
                        last = nc.tensor.transpose(bank[0][:, t * P:(t + 1) * P], f_in[:, t, :], ident[:, :])
                    last.then_inc(f_t1.sem, 1)
                    pe.wait_ge(f_s1.sem, f_s1.after(it, 1))
                    pe.wait_ge(f_xnr.sem, f_xnr.after(it, 0))
                    for t in range(FT):
                        last = nc.tensor.transpose(bank[1][:, t * P:(t + 1) * P], f_sh[:, t * P:(t + 1) * P], ident[:, :])
                    last.then_inc(f_t2.sem, 1)
                    pe.wait_ge(f_xnr.sem, f_xnr.after(it, 1))
                    pe.wait_ge(f_aff.sem, f_aff.after(it, 0))
                    for t in range(FT):
                        last = nc.tensor.transpose(bank[2][:, t * P:(t + 1) * P], f_xn[:, t, :], ident[:, :])
                    last.then_inc(f_t3.sem, 1)
                    pe.wait_ge(f_lo.sem, f_lo.after(it, 1))
                    fx = (fx_hi[:, :], fx_lo[:, :])
                    for j, (o, n) in enumerate(FB):
                        for first, base, free, done in ((DI, 3, f_gl, f_gp), (0, 5, f_ac, f_ap)):
                            pe.wait_ge(free.sem, free.after(it, max(0, j - 1)))
                            cs = slice(first + o, first + o + n)
                            split_mm(bank[base + j % 2][0:n, :], (w1_hi[:, cs], w1_lo[:, cs]), fx).then_inc(done.sem, 1)
                    pe.wait_ge(f_ys.sem, f_ys.after(it, 0))
                    pe.wait_ge(f_ac.sem, f_ac.after(it, NF))
                    for t in range(FT):
                        for j, (o, n) in enumerate(FB):
                            last = nc.tensor.matmul(bank[B_Y][:, t * P:(t + 1) * P], f_act[0:n, j, t * P:(t + 1) * P],
                                                    w2_l[0:n, j, :], start=(j == 0), stop=(j == NF - 1))
                    last.then_inc(f_yp.sem, 1)
                end_phase(pe, l * 2 + 3)


def rotary_tables(n, hd, window):
    import numpy as np
    half = np.arange(0, hd, 2, dtype=np.float32)
    inv_freq = (np.float32(1.0) / np.float32(10000.0) ** (half / np.float32(hd))).astype(np.float32)
    t = np.arange(n, dtype=np.float32)
    freqs = (t[:, None] * inv_freq[None, :]).astype(np.float32)
    freqs = np.concatenate([freqs, freqs], -1)
    base = ((half + np.float32(0.4 * hd)) / np.float32(1.4 * hd)).astype(np.float32)
    power = ((t - n // 2) / np.float32(window // 2)).astype(np.float32)
    scale = (base[None, :] ** power[:, None]).astype(np.float32)
    scale = np.concatenate([scale, scale], -1)
    cos, sin = np.cos(freqs), np.sin(freqs)
    sin = np.concatenate([-sin[:, :hd // 2], sin[:, hd // 2:]], -1)
    inv = np.float32(1.0) / scale
    return (np.stack([cos * scale, cos * inv]).astype(np.float32),
            np.stack([sin * scale, sin * inv]).astype(np.float32))


def kernel(**inputs):
    import numpy as np
    import concourse.bacc as bacc
    from concourse.bass_utils import run_bass_kernel_spmd

    a = {n.replace("L0_", ""): np.asarray(v) for n, v in inputs.items()}
    hd, kv = 64, a["attn_Wk"].shape[0] // 64
    depth, di = a["ffn_W2"].shape[:2]
    k2 = np.repeat(a["attn_Wk"].reshape(kv, 1, hd, -1), 2, axis=1).reshape(2 * kv * hd, -1)
    bk2 = np.repeat(a["attn_bk"].reshape(kv, 1, hd), 2, axis=1).reshape(kv, 2 * hd)
    blocks = [(o, min(128, di - o)) for o in range(0, di, 128)]
    lcols = np.zeros((depth, 128, 2 * len(blocks) + 2), a["ffn_b1"].dtype)
    for j, (o, n) in enumerate(blocks):
        lcols[:, :n, 2 * j] = a["ffn_b1"][:, o:o + n]
        lcols[:, :n, 2 * j + 1] = a["ffn_b1"][:, di + o:di + o + n]
    lcols[:, :, -2], lcols[:, :, -1] = a["ffn_ln_g"], a["ffn_ln_b"]
    cos, sin = rotary_tables(a["attn_x"].shape[1], hd, 32)
    laid = {
        "x": a["attn_x"],
        "wq_t": a["attn_Wq"].T,
        "wkv_t": np.concatenate([k2, a["attn_Wv"]], 0).T,
        "wo_t": a["attn_Wo"].T,
        "cols": np.concatenate([a["attn_bq"].reshape(-1, 128), bk2], 0).T,
        "rows": np.concatenate([a["attn_bv"], a["attn_bo"], a["attn_sinks"]]),
        "wqkv": a["ffn_Wqkv"],
        "qk_scale": np.concatenate([a["ffn_q_scale"], a["ffn_k_scale"]], 1),
        "wo_l": a["ffn_Wo"],
        "w1": a["ffn_W1"],
        "w2": a["ffn_W2"],
        "b2": a["ffn_b2"],
        "lcols": lcols,
        "rot_cos": cos,
        "rot_sin": sin,
    }
    nc = bacc.Bacc("TRN2", target_bir_lowering=False, num_devices=1)
    arrays, args = {}, []
    for name, v in laid.items():
        v = np.ascontiguousarray(v)
        arrays[f"in_{name}"] = v
        args.append(nc.dram_tensor(f"in_{name}", v.shape, mybir.dt.from_np(v.dtype), kind="ExternalInput").ap())
    args.append(nc.dram_tensor("out_0", a["attn_x"].shape, mybir.dt.float32, kind="ExternalOutput").ap())
    block_program(nc, *args)
    r = run_bass_kernel_spmd(nc, [arrays], core_ids=[0])
    return r.results[0]["out_0"]
```

```python
from contextlib import ExitStack

import concourse.bass as bass
from concourse import mybir

F32 = mybir.dt.float32
F32R = mybir.dt.float32r
BF16 = mybir.dt.bfloat16
ACT = mybir.ActivationFunctionType
ALU = mybir.AluOpType
AX = mybir.AxisListType
P = 128


class Signal:

    def __init__(self, sem, per, prime=0):
        self.sem, self.per, self.prime = sem, per, prime

    def after(self, it, n):
        return it * self.per + (self.prime + n)


def block_program(nc, x, wq_t, wkv_t, wo_t_in, cols, rows, Wqkv, qk_scale, Wo2, W1, W2, b2, lcols, rot_cos, rot_sin, out):
    NB, S, DM = x.shape
    TT = S // P
    NT = NB * TT
    HD = 64
    VW = HD + 1
    KV = (wkv_t.shape[1]) // (3 * HD)
    GH = wq_t.shape[1] // HD // KV
    GP = GH // 2
    PAIRS = KV * GP
    L, INNER, _ = Wo2.shape
    QKV = Wqkv.shape[2]
    LH = INNER // HD
    LP = LH // 2
    DI = W2.shape[1]
    FB = [(o, min(P, DI - o)) for o in range(0, DI, P)]
    NF = len(FB)
    FT = 4
    FC = NT // FT
    LOCAL = 32
    NEG = -1e30

    ctx = ExitStack()
    with ctx:
        def sb(name, shape, dt=F32):
            return ctx.enter_context(nc.sbuf_tensor(name, shape, dt))

        def sig(name, per=1, prime=0):
            return Signal(ctx.enter_context(nc.semaphore(name)), per, prime)

        x_cur = sb("x_cur", [P, NT, DM])
        x_mid = sb("x_mid", [P, NT, DM])
        ident = sb("ident", [P, P])
        mask_w = sb("mask_w", [P, 384])
        mask_l = sb("mask_l", [P, 288])
        zero_b = sb("zero_b", [1, 256], BF16)
        neg_half = sb("neg_half", [P, 16])
        UG = 2 * (GP + 1) * P
        wr_arena = sb("wr_arena", [P, KV * UG], F32R)
        w_grp = wr_arena[:, :].rearrange("p (g n) -> p g n", n=UG)
        w_stage = sb("w_stage", [P, UG], F32R)
        wv_hi = sb("wv_hi", [P, KV * HD], F32R)
        wv_lo = sb("wv_lo", [P, KV * HD], F32R)
        f_arena = sb("f_arena", [P, PAIRS * DM])
        wo_t = f_arena[:, :].rearrange("p (q d) -> p q d", d=DM)
        cols_c = sb("cols_c", [P, PAIRS + KV])
        bq_c, bk_c = cols_c[:, 0:PAIRS], cols_c[:, PAIRS:PAIRS + KV]
        rows_b = sb("rows_b", [P, KV * HD + DM + KV * GH])
        bv_b, bo_b = rows_b[:, 0:KV * HD], rows_b[:, KV * HD:KV * HD + DM]
        sink_b = rows_b[:, KV * HD + DM:KV * HD + DM + KV * GH]
        sink_n = sb("sink_n", [P, KV * GH])
        sink_g = sb("sink_g", [P, GH])
        raw = sb("raw", [P, PAIRS * P])
        x_in = sb("x_in", [P, TT, DM])
        x_bo = sb("x_bo", [P, TT * DM])
        xt_hi = sb("xt_hi", [P, S + 1], F32R)
        xt_lo = sb("xt_lo", [P, S + 1], F32R)
        k_hi = sb("k_hi", [P, 2, S], F32R)
        k_lo = sb("k_lo", [P, 2, S], F32R)
        v_a = sb("v_a", [P, TT, KV, VW])
        q_hi = sb("q_hi", [P, 2, S], F32R)
        q_lo = sb("q_lo", [P, 2, S], F32R)
        s_m = sb("s_m", [P, 2, 384])
        p_e = sb("p_e", [P, 2, 384])
        p_t = sb("p_t", [P, 2, 384])
        row_min = sb("row_min", [P, 2 * LH])
        row_sink = sb("row_sink", [P, 2 * LH])
        row_esink = sb("row_esink", [P, 2 * LH])
        row_den = sb("row_den", [P, 2 * LH])
        row_inv = sb("row_inv", [P, 2 * LH])
        o_n = sb("o_n", [P, 2, S])
        o_t = sb("o_t", [P, 2, S])
        z_b = sb("z_b", [P, TT, DM])
        stats = sb("stats", [P, FT, 6])
        moments = sb("moments", [P, FT, 2])
        var_e = sb("var_e", [P, FT])
        rstd = sb("rstd", [P, FT])
        w_raw = raw
        w_hi = wr_arena[:, 0:QKV]
        w_lo = wr_arena[:, QKV:2 * QKV]
        wo_l = sb("wo_l", [P, LP, DM])
        w1_raw = sb("w1_raw", [P, 2 * DI])
        w1_hi = wr_arena[:, 2 * QKV:2 * QKV + 2 * DI]
        w1_lo = wr_arena[:, 2 * QKV + 2 * DI:2 * QKV + 4 * DI]
        w2_l = sb("w2_l", [P, NF, DM])
        lcols_c = sb("lcols_c", [P, 2 * NF + 2])
        b2_b = sb("b2_b", [P, DM])
        b1_c, lng_c, lnb_c = lcols_c, lcols_c[:, 2 * NF:2 * NF + 1], lcols_c[:, 2 * NF + 1:2 * NF + 2]
        qs_b = sb("qs_b", [P, 2, HD])
        qs_r = sb("qs_r", [P, 2, HD])
        cos_t = sb("cos_t", [P, 2, TT, HD])
        sin_t = sb("sin_t", [P, 2, TT, HD])
        cos_s = sb("cos_s", [P, 2, TT, HD])
        sin_s = sb("sin_s", [P, 2, TT, HD])
        HC = 8
        qk_raw = sb("qk_raw", [P, 2, 512])
        sq = sb("sq", [P, 2, 512])
        r_a = sb("r_a", [P, 2, 512])
        r_b = sb("r_b", [P, 2, 512])
        r_s = sb("r_s", [P, 2, 512])
        r_n = sb("r_n", [P, 2, 512])
        ssum = sb("ssum", [P, 2, HC])
        sfl = sb("sfl", [P, 2, HC])
        rinv = sb("rinv", [P, 2, HC])
        q_neg = sb("q_neg", [P, TT, LH])
        qt_l = f_arena[:, 0:LP * S].rearrange("p (q s) -> p q s", s=S)
        kt_l = f_arena[:, LP * S:2 * LP * S].rearrange("p (q s) -> p q s", s=S)
        v_l = sb("v_l", [P, TT, LH, VW])
        f_in = sb("f_in", [P, FT, DM])
        f_sh = sb("f_sh", [P, FT * P])
        f_xn = sb("f_xn", [P, FT, DM])
        f_x = sb("f_x", [P, FT * P])
        fx_hi = sb("fx_hi", [P, FT * P], F32R)
        fx_lo = sb("fx_lo", [P, FT * P], F32R)
        f_gate = sb("f_gate", [P, NF, FT * P])
        f_act = sb("f_act", [P, NF, FT * P])
        f_y = sb("f_y", [P, FT, DM])
        kv_raw = f_gate[:, :, :].rearrange("p j n -> p (j n)")

        bank = [ctx.enter_context(nc.psum_tensor(f"bank{i}", [P, 512], F32)) for i in range(8)]
        B_P, B_OT, B_S, B_T, B_O, B_Y = 0, 1, [2, 3], [4, 5], 6, 7

        phase_end = sig("phase_end")
        const_ready = sig("const_ready")
        ld_x, ld_w, ld_kv, ld_small, ld_wo = (sig(n) for n in ("ld_x", "ld_w", "ld_kv", "ld_small", "ld_wo"))
        split_hi, split_lo = sig("split_hi"), sig("split_lo")
        staged_a = sig("staged_a", 16)
        staged_b = sig("staged_b", 16)
        sink_set = sig("sink_set", 2)
        xin_ready = sig("xin_ready", 2)
        xt_ps, xt_hi_done, xt_lo_done = sig("xt_ps", 1, 1), sig("xt_hi_done", 1), sig("xt_lo_done", 1)
        proj_ready = sig("proj_ready", 1 + GP, 4)
        proj_hi = sig("proj_hi", 1 + GP)
        proj_done = sig("proj_done", 1 + GP, 2)
        v_ps, v_done = sig("v_ps", TT), sig("v_done", TT)
        y_zero = sig("y_zero", 1)
        y_full = sig("y_full", 1)
        z_done, st_done, mom_done = sig("z_done", 1, 1), sig("st_done", 1), sig("mom_done", 1)
        var_done = sig("var_done", 3)
        ln_done = sig("ln_done", 2)
        cur_done = sig("cur_done", 1)
        out_done = sig("out_done")

        class Att:

            def __init__(self, n, H):
                h = H // 2
                self.H = H
                self.scores = sig(n + "scores", H, h + 1)
                self.masked = sig(n + "masked", 2 * H, 2 * H)
                self.exped = sig(n + "exped", H, 2)
                self.transposed = sig(n + "transposed", H, 2)
                self.pt_even = sig(n + "pt_even", h, 1)
                self.pt_odd = sig(n + "pt_odd", h, 1)
                self.pv = sig(n + "pv", H, h + 1)
                self.sink_sub = sig(n + "sink_sub", h)
                self.sink_exp = sig(n + "sink_exp", h)
                self.den = sig(n + "den", h)
                self.inv = sig(n + "inv", h)
                self.o = sig(n + "o", h, 1)
                self.ot = sig(n + "ot", h, 2)
                self.o_sb = sig(n + "o_sb", h, 1)
                self.y = sig(n + "y", h, 2)

        A = Att("w_", GH)
        B = Att("l_", LH)
        la = sig("la", 16 * 2)
        lw = sig("lw", 16 * 3)
        lw2 = sig("lw2", 16 * 4)
        lw_hi = sig("lw_hi", 2)
        lw_lo = sig("lw_lo", 2)
        swap = sig("swap", 1)
        tab = sig("tab", 4)
        zeros = sig("zeros", 1)
        lx_in = sig("lx_in", 1)
        lxt_ps = sig("lxt_ps", 1, 1)
        lxt_hi = sig("lxt_hi", 1)
        lxt_lo = sig("lxt_lo", 1)
        lp_ps = sig("lp_ps", 6, 1)
        lp_act = sig("lp_act", 6, 2)
        lp_sq = sig("lp_sq", 4, 2)
        lp_dve = sig("lp_dve", 4, 2)
        lp_sum = sig("lp_sum", 4, 2)
        lp_max = sig("lp_max", 4)
        lp_rot = sig("lp_rot", 4, 2)
        lp_inv = sig("lp_inv", 4)
        lp_out = sig("lp_out", 4)
        lt_ps = sig("lt_ps", 4, 2)
        lt_act = sig("lt_act", 4, 1)
        l_res = sig("l_res", 1, 1)
        f_inr = sig("f_inr", 1)
        f_t1 = sig("f_t1", 1, 1)
        f_s1 = sig("f_s1", 1, 1)
        f_t2 = sig("f_t2", 1, 1)
        f_st, f_mom, f_var = sig("f_st", 1), sig("f_mom", 1), sig("f_var", 3)
        f_xnr = sig("f_xnr", 1, 1)
        f_t3 = sig("f_t3", 1, 1)
        f_aff = sig("f_aff", 1, 1)
        f_hi, f_lo = sig("f_hi", 1), sig("f_lo", 1, 1)
        f_gp, f_ap = sig("f_gp", NF), sig("f_ap", NF, 1)
        f_gl, f_ac = sig("f_gl", NF, 1), sig("f_ac", NF, 3)
        f_yp, f_ys, f_res = sig("f_yp", 1, 1), sig("f_ys", 1, 1), sig("f_res", 1, 1)
        n_z, n_st, n_mom, n_var, n_out = sig("n_z", 1), sig("n_st", 1), sig("n_mom", 1), sig("n_var", 3), sig("n_out", 1, 1)

        block = ctx.enter_context(nc.Block())

        met = {eng: ctx.enter_context(nc.semaphore("met_" + name)) for eng, name in (
            (nc.sync, "sp"), (nc.gpsimd, "pool"), (nc.scalar, "act"), (nc.vector, "dve"), (nc.tensor, "pe"))}

        def settle(eng):
            eng.sem_inc(met[eng], 1)

        def end_phase(eng, k):
            settle(eng)
            eng.drain().then_inc(phase_end.sem, 1)
            eng.wait_ge(phase_end.sem, k * 5)
            settle(eng)

        def chunk_t(z, c):
            t = c % 2
            return (qt_l if c < 2 else kt_l)[:, 4 * z:4 * z + 4, t * P:(t + 1) * P]

        def chunk_columns(z, n):
            kind, t = n // 2, n % 2
            return slice(kind * INNER + z * 512, kind * INNER + (z + 1) * 512), t

        P_AT = {0: (4, 5, 6, 7, 8, 9), 1: (12, 13, 14, 15, 16, 17)}
        T_AT = {0: (7, 9, 11, 13), 1: (15, 17, 19, 21)}
        X_AT = 2

        FIRST = [(0, n, n - 2 if n >= 2 else None) for n in range(6)] + [(1, n, 0 if n == 3 else None) for n in range(4)]
        QK = range(4)

        def events(i, nxt):
            for z in (0, 1):
                for ahead, j in ((1, i), (0, i + LH)):
                    if (nxt if ahead else z == 1 and i >= 0):
                        n = P_AT[z].index(j) if j in P_AT[z] else None
                        c = T_AT[z].index(j) if j in T_AT[z] else None
                        if n is not None or c is not None:
                            yield z, ahead, n, c

        def chunk_before(i, nxt):
            return max((j - (0 if ahead else LH), z, ahead, c + 1) for z in (0, 1) for ahead in ((0, 1) if z else (1,))
                       for c, j in enumerate(T_AT[z]) if j - (0 if ahead else LH) <= i and (nxt or not ahead))[1:]

        def halves(t):
            return t.rearrange("p (h z d) -> p h z d", z=2, d=HD // 2)

        def pair_part(n, part):
            return w_grp[:, n, 2 * P:UG].rearrange("p (q z c) -> p q z c", z=2, c=P)[:, :, part, :]

        def raw_pairs(n):
            return raw[:, n * GP * P:(n + 1) * GP * P].rearrange("p (q c) -> p q c", c=P)

        A_SIDE = ((0, 3, 0), (2, 4, 0), (3, 0, 1), (4, 1, 1), (6, 2, 1))

        def stat(h, t):
            return 4 * (h // 2) + 2 * t + h % 2

        def nothing(i):
            pass

        def span(a, first, last):
            return (range(-2 if first else 0, a.H + 3 if last else a.H),
                    lambda h: (h >= 0 or not first) and (h < a.H or not last))

        def att_pe(pe, a, it, where, before, beside, scores, tr, pv, wo_of, ot_free=lambda i: None):
            steps, there = where
            for i in steps:
                before(i)
                h = i + 2
                if there(h):
                    pe.wait_ge(a.masked.sem, a.masked.after(it, 2 * (h - 1)))
                    scores(h).then_inc(a.scores.sem, 1)
                beside(i)
                if there(i):
                    pe.wait_ge(a.exped.sem, a.exped.after(it, i + 1))
                    free = a.pt_even if i % 2 == 0 else a.pt_odd
                    pe.wait_ge(free.sem, free.after(it, i // 2))
                    tr(i).then_inc(a.transposed.sem, 1)
                h = i - 1
                if there(h):
                    done = a.pt_even if h % 2 == 0 else a.pt_odd
                    pe.wait_ge(done.sem, done.after(it, h // 2 + 1))
                    if h % 2 == 0:
                        pe.wait_ge(a.o.sem, a.o.after(it, h // 2))
                    pv(h).then_inc(a.pv.sem, 1)
                p = (i - 3) // 2
                if i % 2 == 1 and there(2 * p):
                    pe.wait_ge(a.o.sem, a.o.after(it, p + 1))
                    pe.wait_ge(a.o_sb.sem, a.o_sb.after(it, p))
                    ot_free(i)
                    for t in range(TT):
                        last = nc.tensor.transpose(bank[B_OT][:, t * P:(t + 1) * P],
                                                   o_n[:, p % 2, t * P:(t + 1) * P], ident[:, :])
                    last.then_inc(a.ot.sem, 1)
                p = i // 2 - 2
                if i % 2 == 0 and there(2 * p):
                    pe.wait_ge(a.o_sb.sem, a.o_sb.after(it, p + 1))
                    for t in range(TT):
                        last = nc.tensor.matmul(bank[B_Y][:, t * DM:(t + 1) * DM], o_t[:, p % 2, t * P:(t + 1) * P], wo_of(p),
                                                start=False, stop=False, skip_group_check=True)
                    last.then_inc(a.y.sem, 1)

        def att_dve(dve, a, it, where, W0, W, mask, scale, floor, before, beside, sink):
            steps, there = where
            for i in steps:
                before(i)
                h = i + 2
                if there(h):
                    dve.wait_ge(a.scores.sem, a.scores.after(it, h + 1))
                    dve.wait_ge(a.exped.sem, a.exped.after(it, h - 1))
                    settle(dve)
                    for t, (lo, hi) in enumerate(((0, W0), (W0, W))):
                        c = stat(h % a.H, t)
                        nc.vector.tensor_tensor_reduce(
                            out=s_m[:, h % 2, lo:hi], in0=bank[B_S[h % 2]][:, lo:hi], in1=mask[:, lo:hi],
                            scale=scale(t, h), scalar=floor(h), op0=ALU.add, op1=ALU.min,
                            accum_out=row_min[:, c:c + 1]).then_inc(a.masked.sem, 1)
                beside(i)
                if sink and there(i) and i % 2 == 1:
                    dve.wait_ge(a.transposed.sem, a.transposed.after(it, i + 1))
                    dve.wait_ge(a.pv.sem, a.pv.after(it, i - 1))
                    nc.vector.tensor_copy(p_t[:, 1, 0:W], bank[B_T[1]][:, 0:W]).then_inc(a.pt_odd.sem, 1)
                p = i // 2 - 1
                if i % 2 == 0 and there(2 * p):
                    cols = slice(4 * (p % (a.H // 2)), 4 * (p % (a.H // 2)) + 4)
                    o = bank[B_O][:, 0:4 * VW].rearrange("p (c d) -> p c d", d=VW)
                    sums, inv = o[:, :, HD:VW], row_inv[:, cols].unsqueeze(2)
                    dve.wait_ge(a.pv.sem, a.pv.after(it, 2 * p + 2))
                    if sink:
                        den = row_den[:, cols].unsqueeze(2)
                        dve.wait_ge(a.sink_exp.sem, a.sink_exp.after(it, p + 1))
                        nc.vector.tensor_tensor(den, sums, row_esink[:, cols].unsqueeze(2),
                                                ALU.add).then_inc(a.den.sem, 1)
                        dve.wait_ge(a.den.sem, a.den.after(it, p + 1))
                        sums = den
                    nc.vector.reciprocal(inv, sums).then_inc(a.inv.sem, 1)
                    dve.wait_ge(a.inv.sem, a.inv.after(it, p + 1))
                    dve.wait_ge(a.ot.sem, a.ot.after(it, p - 1))
                    nc.vector.tensor_tensor(o_n[:, p % 2, :].rearrange("p (c d) -> p c d", d=HD), o[:, :, 0:HD],
                                            inv.broadcast_to([P, 4, HD]), ALU.mult).then_inc(a.o.sem, 1)

        def att_act(act, a, it, where, W0, W, before, beside, sink):
            steps, there = where
            for i in steps:
                before(i)
                h = i + 1
                if there(h):
                    act.wait_ge(a.transposed.sem, a.transposed.after(it, h - 1))
                    for t, (lo, hi) in enumerate(((0, W0), (W0, W))):
                        act.wait_ge(a.masked.sem, a.masked.after(it, 2 * h + t + 1))
                        c = stat(h % a.H, t)
                        last = nc.scalar.activation(p_e[:, h % 2, lo:hi], s_m[:, h % 2, lo:hi], ACT.Exp,
                                                    bias=row_min[:, c:c + 1], scale=-1.0)
                    last.then_inc(a.exped.sem, 1)
                beside(i)
                if there(i) and (i % 2 == 0 or not sink):
                    done = a.pt_even if i % 2 == 0 else a.pt_odd
                    act.wait_ge(a.transposed.sem, a.transposed.after(it, i + 1))
                    act.wait_ge(a.pv.sem, a.pv.after(it, i - 1))
                    nc.scalar.activation(p_t[:, i % 2, 0:W], bank[B_T[i % 2]][:, 0:W], ACT.Copy).then_inc(done.sem, 1)
                    if sink and i % 2 == 0:
                        p = i // 2
                        act.wait_ge(a.sink_sub.sem, a.sink_sub.after(it, p + 1))
                        nc.scalar.activation(row_esink[:, 4 * p:4 * p + 4], row_sink[:, 4 * p:4 * p + 4],
                                             ACT.Exp).then_inc(a.sink_exp.sem, 1)
                p = (i - 3) // 2
                if i % 2 == 1 and there(2 * p):
                    act.wait_ge(a.ot.sem, a.ot.after(it, p + 1))
                    act.wait_ge(a.y.sem, a.y.after(it, p - 1))
                    nc.scalar.activation(o_t[:, p % 2, :], bank[B_OT][:, 0:S], ACT.Copy).then_inc(a.o_sb.sem, 1)

        def sinks_pool(pool, a, it, sink_of):
            for p in range(a.H // 2):
                c = slice(4 * p, 4 * p + 4)
                pool.wait_ge(a.masked.sem, a.masked.after(it, 4 * p + 4))
                settle(pool)
                nc.gpsimd.tensor_tensor(row_sink[:, c].rearrange("p (t e) -> p t e", t=2),
                                        row_min[:, c].rearrange("p (t e) -> p t e", t=2),
                                        sink_of(p), ALU.add).then_inc(a.sink_sub.sem, 1)

        @block.sync
        def _(sp):
            sp.dma_start(x_cur[:, :, :], x.rearrange("b (t p) d -> p (b t) d", p=P)).then_inc(ld_x.sem, 16)
            sp.dma_start(raw[:, :], wq_t).then_inc(ld_w.sem, 16)
            sp.dma_start(kv_raw, wkv_t).then_inc(ld_kv.sem, 16)
            for dst, src in [(cols_c[:, :], cols), (rows_b[:, :], rows.partition_broadcast(P)),
                             (cos_t[:, :, :, :], rot_cos.rearrange("k (t p) d -> p k t d", p=P)),
                             (sin_t[:, :, :, :], rot_sin.rearrange("k (t p) d -> p k t d", p=P))]:
                sp.dma_start(dst, src).then_inc(ld_small.sem, 16)
            sp.dma_start(wo_t, wo_t_in.rearrange("(q p) n -> p q n", p=P)).then_inc(ld_wo.sem, 16)
            sp.wait_ge(split_lo.sem, KV + 2)
            with sp.Fori(0, NB) as b:
                with sp.Fori(0, KV) as g:
                    it = b * KV + g
                    for part, used, done in ((slice(0, 4 * P), 2, staged_a), (slice(4 * P, UG), 1 + GP, staged_b)):
                        sp.wait_ge(proj_ready.sem, proj_ready.after(it, used - 1 - GP))
                        sp.dma_start(w_stage[:, part].bitcast(F32),
                                     w_grp[:, bass.ds(g, 1), part].rearrange("p g n -> p (g n)").bitcast(F32)).then_inc(done.sem, 16)
            end_phase(sp, 1)
            def load_qkv(l):
                sp.dma_start(w_raw[:, 0:QKV], Wqkv[bass.ds(l, 1)].rearrange("l p n -> p (l n)")).then_inc(la.sem, 16)
                sp.dma_start(qs_b[:, :, :].rearrange("p k d -> p (k d)"),
                             qk_scale[bass.ds(l, 1)].rearrange("l n -> (l n)").partition_broadcast(P)).then_inc(la.sem, 16)

            load_qkv(0)
            with sp.Fori(0, L) as l:
                sp.dma_start(wo_l[:, :, :], Wo2[bass.ds(l, 1)].rearrange("l (q p) n -> p (l q) n", p=P)).then_inc(lw.sem, 16)
                sp.dma_start(w1_raw[:, :], W1[bass.ds(l, 1)].rearrange("l p n -> p (l n)")).then_inc(lw.sem, 16)
                sp.dma_start(b2_b[:, :], b2[bass.ds(l, 1)].rearrange("l n -> (l n)").partition_broadcast(P)).then_inc(lw.sem, 16)
                for j, (o, n) in enumerate(FB):
                    sp.dma_start(w2_l[0:n, j, :], W2[bass.ds(l, 1), o:o + n, :].rearrange("l p n -> p (l n)")).then_inc(lw2.sem, 16)
                sp.dma_start(lcols_c[:, :], lcols[bass.ds(l, 1)].rearrange("l p n -> p (l n)")).then_inc(lw2.sem, 16)
                sp.wait_ge(lw_lo.sem, lw_lo.after(l, 1))
                sp.wait_ge(tab.sem, tab.after(l, 4))
                settle(sp)
                load_qkv(l + 1)
                end_phase(sp, l * 2 + 2)
                end_phase(sp, l * 2 + 3)
            o_v = out.rearrange("b (t p) d -> p (b t) d", p=P)
            with sp.Fori(0, NB) as b:
                sp.wait_ge(n_out.sem, n_out.after(b, 1))
                sp.dma_start(o_v[:, bass.ds(b * TT, TT), :], x_cur[:, bass.ds(b * TT, TT), :]).then_inc(out_done.sem, 16)
            sp.wait_ge(out_done.sem, 16 * NB)

        N_SMALL = 16 * 4

        def pool_rstd(pool, n, done, it, moments_ready):
            pool.wait_ge(moments_ready.sem, moments_ready.after(it, 1))
            settle(pool)
            nc.gpsimd.tensor_copy(var_e[:, 0:n], moments[:, 0:n, 1]).then_inc(done.sem, 1)
            pool.wait_ge(done.sem, done.after(it, 1))
            settle(pool)
            nc.gpsimd.tensor_scalar(var_e[:, 0:n], var_e[:, 0:n], 1e-5, 1.0, ALU.add, ALU.mult).then_inc(done.sem, 1)
            pool.wait_ge(done.sem, done.after(it, 2))
            nc.gpsimd.tensor_tensor(rstd[:, 0:n], var_e[:, 0:n], neg_half[:, 0:n], ALU.pow).then_inc(done.sem, 1)

        @block.gpsimd
        def _(pool):
            nc.gpsimd.memset(ident[:, :], 0.0).then_inc(const_ready.sem, 1)
            nc.gpsimd.memset(mask_w[:, :], 0.0).then_inc(const_ready.sem, 1)
            nc.gpsimd.memset(mask_l[:, :], 0.0).then_inc(const_ready.sem, 1)
            nc.gpsimd.memset(zero_b[:, :], 0.0).then_inc(const_ready.sem, 1)
            nc.gpsimd.memset(neg_half[:, :], -0.5).then_inc(const_ready.sem, 1)
            nc.gpsimd.memset(v_a[:, :, :, HD:VW], 1.0)
            nc.gpsimd.memset(v_l[:, :, :, HD:VW], 1.0)
            pool.sem_inc(lp_rot.sem, 2)
            pool.sem_inc(f_lo.sem, 1)
            pool.sem_inc(f_res.sem, 1)
            pool.wait_ge(const_ready.sem, 5)
            nc.gpsimd.affine_select(out=ident[:, :], in_=ident[:, :], compare_op=ALU.not_equal, fill=1.0, base=0,
                                    pattern=[[-1, P]], channel_multiplier=1).then_inc(const_ready.sem, 1)
            nc.gpsimd.affine_select(out=mask_w[:, 0:P], in_=mask_w[:, 0:P], compare_op=ALU.is_ge, fill=NEG, base=0,
                                    pattern=[[-1, P]], channel_multiplier=1).then_inc(const_ready.sem, 1)
            nc.gpsimd.affine_select(out=mask_w[:, P:384], in_=mask_w[:, P:384], compare_op=ALU.is_gt, fill=NEG, base=0,
                                    pattern=[[1, S]], channel_multiplier=-1).then_inc(const_ready.sem, 1)
            nc.gpsimd.affine_select(out=mask_l[:, 0:P], in_=mask_l[:, 0:P], compare_op=ALU.is_ge, fill=NEG, base=0,
                                    pattern=[[-1, P]], channel_multiplier=1).then_inc(const_ready.sem, 1)
            nc.gpsimd.affine_select(out=mask_l[:, P:288], in_=mask_l[:, P:288], compare_op=ALU.is_ge, fill=NEG, base=0,
                                    pattern=[[1, 160]], channel_multiplier=-1).then_inc(const_ready.sem, 1)
            pool.wait_ge(const_ready.sem, 10)
            nc.gpsimd.affine_select(out=mask_w[:, P:384], in_=mask_w[:, P:384], compare_op=ALU.is_ge, fill=NEG, base=P,
                                    pattern=[[-1, S]], channel_multiplier=1).then_inc(const_ready.sem, 1)
            nc.gpsimd.affine_select(out=mask_l[:, 0:P], in_=mask_l[:, 0:P], compare_op=ALU.is_ge, fill=NEG, base=LOCAL,
                                    pattern=[[1, P]], channel_multiplier=-1).then_inc(const_ready.sem, 1)
            nc.gpsimd.affine_select(out=mask_l[:, P:288], in_=mask_l[:, P:288], compare_op=ALU.is_ge, fill=NEG, base=LOCAL,
                                    pattern=[[-1, 160]], channel_multiplier=1).then_inc(const_ready.sem, 1)
            pool.wait_ge(ld_small.sem, N_SMALL)
            nc.gpsimd.tensor_scalar(sink_n[:, :], sink_b[:, :], -1.0, 0.0, ALU.mult, ALU.add).then_inc(const_ready.sem, 1)
            pool.wait_ge(ld_x.sem, 16)
            with pool.Fori(0, NB) as b:
                pool.wait_ge(xt_ps.sem, xt_ps.after(b, 0))
                settle(pool)
                xb = x_cur[:, bass.ds(b * TT, TT), :]
                nc.gpsimd.tensor_copy(x_in[:, :, :], xb).then_inc(xin_ready.sem, 1)
                nc.gpsimd.tensor_tensor(x_bo[:, :].rearrange("p (t d) -> p t d", d=DM), xb,
                                        bo_b[:, :].unsqueeze(1).broadcast_to([P, TT, DM]), ALU.add).then_inc(xin_ready.sem, 1)
                with pool.Fori(0, KV) as g:
                    it = b * KV + g
                    sinks_pool(pool, A, it, lambda p: sink_b[:, bass.ds(g * GH + 2 * p, 2)].unsqueeze(1).broadcast_to([P, 2, 2]))
                pool_rstd(pool, TT, var_done, b, mom_done)
            end_phase(pool, 1)
            def split_qkv(l):
                pool.wait_ge(la.sem, la.after(l, 32))
                settle(pool)
                for z in range(2):
                    last = nc.gpsimd.tensor_copy(qs_r[:, :, z * 32:z * 32 + 32], qs_b[:, :, 32 - z * 32:64 - z * 32])
                last.then_inc(swap.sem, 1)
                pool.wait_ge(swap.sem, swap.after(l, 1))
                for k in range(2):
                    nc.gpsimd.tensor_tensor(cos_s[:, k], cos_t[:, k], qs_b[:, k, :].unsqueeze(1).broadcast_to([P, TT, HD]),
                                            ALU.mult).then_inc(tab.sem, 1)
                    nc.gpsimd.tensor_tensor(sin_s[:, k], sin_t[:, k], qs_r[:, k, :].unsqueeze(1).broadcast_to([P, TT, HD]),
                                            ALU.mult).then_inc(tab.sem, 1)
                pool.wait_ge(lw_hi.sem, lw_hi.after(l, 1))
                nc.gpsimd.tensor_tensor(w_lo, w_raw[:, 0:QKV], w_hi.bitcast(F32), ALU.subtract).then_inc(lw_lo.sem, 1)

            split_qkv(0)
            with pool.Fori(0, L) as l:
                def load_x(b, it):
                    pool.wait_ge(lxt_ps.sem, lxt_ps.after(it, 0))
                    settle(pool)
                    nc.gpsimd.tensor_copy(x_in[:, :, :], x_cur[:, bass.ds(b * TT, TT), :]).then_inc(lx_in.sem, 1)

                def norm_half(z, it):
                    hs = it * 2 + z
                    for c in range(4):
                        t, kind, buf = c % 2, c // 2, c % 2
                        pool.wait_ge(lp_sum.sem, lp_sum.after(hs, c + 1))
                        pool.wait_ge(lt_ps.sem, lt_ps.after(hs, c - 1))
                        settle(pool)
                        nc.gpsimd.tensor_scalar(sfl[:, buf, :], ssum[:, buf, :], 1e-24, 1.0, ALU.max,
                                                ALU.mult).then_inc(lp_max.sem, 1)
                        nc.gpsimd.tensor_tensor(r_s[:, buf, :], r_a[:, buf, :], r_b[:, buf, :], ALU.add).then_inc(lp_rot.sem, 1)
                        pool.wait_ge(lp_max.sem, lp_max.after(hs, c + 1))
                        nc.gpsimd.tensor_tensor(rinv[:, buf, :], sfl[:, buf, :], neg_half[:, 0:HC], ALU.pow).then_inc(lp_inv.sem, 1)
                        pool.wait_ge(lp_inv.sem, lp_inv.after(hs, c + 1))
                        settle(pool)
                        if kind == 0:
                            if c == 0:
                                pool.wait_ge(B.masked.sem, B.masked.after(it, 0 if z else -LH))
                                settle(pool)
                            nc.gpsimd.tensor_scalar(q_neg[:, t, z * HC:(z + 1) * HC], rinv[:, buf, :], -8.0, 0.0,
                                                    ALU.mult, ALU.add).then_inc(lp_out.sem, 1)
                        else:
                            pool.wait_ge(lp_rot.sem, lp_rot.after(hs, c + 1))
                            nc.gpsimd.tensor_tensor(r_n[:, buf, :].rearrange("p (h d) -> p h d", d=HD),
                                                    r_s[:, buf, :].rearrange("p (h d) -> p h d", d=HD),
                                                    rinv[:, buf, :].unsqueeze(2).broadcast_to([P, HC, HD]),
                                                    ALU.mult).then_inc(lp_out.sem, 1)

                load_x(0, l * NB)
                with pool.Fori(0, NB - 1) as b:
                    it = l * NB + b
                    norm_half(0, it)
                    load_x(b + 1, it + 1)
                    norm_half(1, it)
                pool.wait_ge(lw_hi.sem, lw_hi.after(l, 2))
                nc.gpsimd.tensor_tensor(w1_lo, w1_raw[:, :], w1_hi.bitcast(F32), ALU.subtract).then_inc(lw_lo.sem, 1)
                norm_half(0, l * NB + (NB - 1))
                norm_half(1, l * NB + (NB - 1))
                end_phase(pool, l * 2 + 2)

                def load_tokens(c, it):
                    pool.wait_ge(f_t1.sem, f_t1.after(it, 0))
                    settle(pool)
                    nc.gpsimd.tensor_copy(f_in[:, :, :], x_cur[:, bass.ds(c * FT, FT), :]).then_inc(f_inr.sem, 1)

                def lo_part(it):
                    pool.wait_ge(f_hi.sem, f_hi.after(it, 1))
                    pool.wait_ge(f_ap.sem, f_ap.after(it, 0))
                    nc.gpsimd.tensor_tensor(fx_lo[:, :], f_x[:, :], fx_hi[:, :].bitcast(F32), ALU.subtract).then_inc(f_lo.sem, 1)

                def residual(c, it):
                    pool.wait_ge(f_ys.sem, f_ys.after(it, 1))
                    settle(pool)
                    nc.gpsimd.tensor_tensor(x_cur[:, bass.ds(c * FT, FT), :], f_y[:, :, :],
                                            b2_b[:, :].unsqueeze(1).broadcast_to([P, FT, DM]), ALU.add).then_inc(f_res.sem, 1)

                load_tokens(0, l * FC)
                pool_rstd(pool, FT, f_var, l * FC, f_mom)
                lo_part(l * FC)
                load_tokens(1, l * FC + 1)
                with pool.Fori(0, FC - 2) as c:
                    it = l * FC + c
                    pool_rstd(pool, FT, f_var, it + 1, f_mom)
                    lo_part(it + 1)
                    load_tokens(c + 2, it + 2)
                    residual(c, it)
                pool_rstd(pool, FT, f_var, l * FC + (FC - 1), f_mom)
                lo_part(l * FC + (FC - 1))
                residual(FC - 2, l * FC + (FC - 2))
                split_qkv(l + 1)
                residual(FC - 1, l * FC + (FC - 1))
                end_phase(pool, l * 2 + 3)
            with pool.Fori(0, NB) as b:
                pool_rstd(pool, TT, n_var, b, n_mom)

        @block.scalar
        def _(act):
            act.sem_inc(A.exped.sem, 2)
            act.sem_inc(A.pt_even.sem, 1)
            act.sem_inc(A.o_sb.sem, 1)
            act.sem_inc(B.exped.sem, 2)
            act.sem_inc(B.pt_even.sem, 1)
            act.sem_inc(B.o_sb.sem, 1)
            act.sem_inc(B.pt_odd.sem, 1)
            act.sem_inc(lt_act.sem, 1)
            act.sem_inc(lp_act.sem, 2)
            act.sem_inc(lp_sq.sem, 2)
            act.sem_inc(f_s1.sem, 1)
            act.sem_inc(f_aff.sem, 1)
            act.sem_inc(f_gl.sem, 1)
            KW = KV * P
            act.wait_ge(ld_w.sem, 16)
            for n in range(KV):
                nc.scalar.activation(pair_part(n, 0), raw_pairs(n), ACT.Copy).then_inc(split_hi.sem, 1)
            act.wait_ge(ld_kv.sem, 16)
            nc.scalar.activation(w_grp[:, :, 0:P], kv_raw[:, 0:KW].rearrange("p (g n) -> p g n", n=P),
                                 ACT.Copy).then_inc(split_hi.sem, 1)
            nc.scalar.activation(wv_hi[:, :], kv_raw[:, KW:], ACT.Copy).then_inc(split_hi.sem, 1)
            act.wait_ge(ld_small.sem, N_SMALL)
            with act.Fori(0, NB) as b:
                act.wait_ge(xt_ps.sem, xt_ps.after(b, 1))
                nc.scalar.activation(xt_hi[:, 0:S], bank[0][:, 0:S], ACT.Copy).then_inc(xt_hi_done.sem, 1)

                def project(n, it, g, odd):
                    act.wait_ge(proj_ready.sem, proj_ready.after(it, n + 1))
                    if n == 0:
                        dst, bias = k_hi[:, odd, :], bk_c[:, bass.ds(g, 1)]
                    else:
                        p = n - 1
                        act.wait_ge(A.scores.sem, A.scores.after(it, 2 * p - 2))
                        dst, bias = q_hi[:, p % 2, :], bq_c[:, bass.ds(g * GP + p, 1)]
                    nc.scalar.activation(dst, bank[B_P][:, 0:S], ACT.Identity, bias=bias).then_inc(proj_hi.sem, 1)

                def body(g, odd, first, last):
                    it = b * KV + g

                    def side(i):
                        for step, n, ahead in A_SIDE:
                            if step == i and not (ahead and last):
                                project(n, it + ahead, g + ahead, (odd + ahead) % 2)

                    att_act(act, A, it, span(A, first, last), P, 384, side, nothing, True)

                for n in range(3):
                    project(n, b * KV, 0, 0)
                body(0, 0, True, False)
                with act.Fori(0, KV // 2 - 1) as j:
                    body(2 * j + 1, 1, False, False)
                    body(2 * j + 2, 0, False, False)
                body(KV - 1, 1, False, True)
                act.wait_ge(ln_done.sem, ln_done.after(b, 2))
                nc.scalar.activation(x_cur[:, bass.ds(b * TT, TT), :], x_mid[:, bass.ds(b * TT, TT), :],
                                     ACT.Copy).then_inc(cur_done.sem, 1)
            end_phase(act, 1)
            def split_qkv(l):
                act.wait_ge(la.sem, la.after(l, 32))
                nc.scalar.activation(w_hi, w_raw[:, 0:QKV], ACT.Copy).then_inc(lw_hi.sem, 1)

            split_qkv(0)
            with act.Fori(0, L) as l:
                def shift_x(it):
                    act.wait_ge(lxt_ps.sem, lxt_ps.after(it, 1))
                    act.wait_ge(lp_ps.sem, lp_ps.after(it * 2, 0))
                    nc.scalar.activation(xt_hi[0:HD, 0:S], bank[B_P][0:HD, 0:S], ACT.Copy)
                    nc.scalar.activation(xt_hi[HD:P, 1:S + 1], bank[B_P][HD:P, 0:S], ACT.Copy).then_inc(lxt_hi.sem, 1)

                def project(z, n, it):
                    hs = it * 2 + z
                    act.wait_ge(lp_ps.sem, lp_ps.after(hs, n + 1))
                    if n in QK:
                        act.wait_ge(lp_dve.sem, lp_dve.after(hs, n - 1))
                        act.wait_ge(lp_sq.sem, lp_sq.after(hs, n - 1))
                        nc.scalar.activation(qk_raw[:, n % 2, :], bank[B_P][:, :], ACT.Copy).then_inc(lp_act.sem, 1)
                        act.wait_ge(lp_act.sem, lp_act.after(hs, n + 1))
                        act.wait_ge(lp_sum.sem, lp_sum.after(hs, n - 1))
                        nc.scalar.activation(sq[:, n % 2, :], qk_raw[:, n % 2, :], ACT.Square).then_inc(lp_sq.sem, 1)
                    else:
                        act.wait_ge(B.pv.sem, B.pv.after(it, 0 if z else -HC))
                        nc.scalar.activation(v_l[:, n % 2, z * HC:(z + 1) * HC, 0:HD],
                                             bank[B_P][:, :].rearrange("p (h d) -> p h d", d=HD), ACT.Copy).then_inc(lp_act.sem, 1)

                def keep_chunk(z, c, it):
                    hs = it * 2 + z
                    act.wait_ge(lt_ps.sem, lt_ps.after(hs, c + 1))
                    act.wait_ge(B.scores.sem, B.scores.after(it, 0 if z else -HC))
                    nc.scalar.activation(chunk_t(z, c), bank[B_OT][:, :].rearrange("p (q c) -> p q c", c=P),
                                         ACT.Copy).then_inc(lt_act.sem, 1)

                def batch(it, first, last):
                    def side(i):
                        if not last and i == X_AT:
                            shift_x(it + 1)
                        for z, ahead, n, c in events(i, not last):
                            if n is not None:
                                project(z, n, it + ahead)
                            if c is not None:
                                keep_chunk(z, c, it + ahead)

                    att_act(act, B, it, span(B, first, last), P, 288, nothing, side, False)

                shift_x(l * NB)
                for z, n, c in FIRST:
                    if n is not None:
                        project(z, n, l * NB)
                    if c is not None:
                        keep_chunk(z, c, l * NB)
                act.wait_ge(lw.sem, lw.after(l, 48))
                nc.scalar.activation(w1_hi, w1_raw[:, :], ACT.Copy).then_inc(lw_hi.sem, 1)
                batch(l * NB, True, False)
                with act.Fori(1, NB - 1) as b:
                    batch(l * NB + b, False, False)
                batch(l * NB + (NB - 1), False, True)
                end_phase(act, l * 2 + 2)
                split_qkv(l + 1)
                act.wait_ge(lw2.sem, lw2.after(l, 16 * 4))
                settle(act)

                def shift(it):
                    act.wait_ge(f_t1.sem, f_t1.after(it, 1))
                    act.wait_ge(f_t2.sem, f_t2.after(it, 0))
                    nc.scalar.activation(f_sh[0:HD, :], bank[0][0:HD, :], ACT.Identity)
                    nc.scalar.activation(f_sh[HD:P, :].rearrange("p (h s) -> p h s", s=S)[:, :, 1:S],
                                         bank[0][HD:P, :].rearrange("p (h s) -> p h s", s=S)[:, :, 0:S - 1],
                                         ACT.Identity).then_inc(f_s1.sem, 1)

                def affine(it):
                    act.wait_ge(f_t3.sem, f_t3.after(it, 1))
                    act.wait_ge(f_lo.sem, f_lo.after(it, 0))
                    act.wait_ge(f_ap.sem, f_ap.after(it, 0))
                    nc.scalar.activation(f_x[:, :], bank[2][:, :], ACT.Identity, bias=lnb_c[:, 0:1],
                                         scale=lng_c[:, 0:1]).then_inc(f_aff.sem, 1)
                    act.wait_ge(f_aff.sem, f_aff.after(it, 1))
                    nc.scalar.activation(fx_hi[:, :], f_x[:, :], ACT.Identity).then_inc(f_hi.sem, 1)

                def gelu(j, it):
                    n = FB[j][1]
                    act.wait_ge(f_gp.sem, f_gp.after(it, j + 1))
                    act.wait_ge(f_ac.sem, f_ac.after(it, j - 2))
                    nc.scalar.activation(f_gate[0:n, j, :], bank[3 + j % 2][0:n, :], ACT.Gelu,
                                         bias=b1_c[0:n, 2 * j + 1:2 * j + 2]).then_inc(f_gl.sem, 1)

                shift(l * FC)
                affine(l * FC)
                with act.Fori(0, FC - 1) as c:
                    it = l * FC + c
                    shift(it + 1)
                    for j in range(NF):
                        gelu(j, it)
                    affine(it + 1)
                for j in range(NF):
                    gelu(j, l * FC + (FC - 1))
                end_phase(act, l * 2 + 3)

        def dve_stats(dve, n, src, st, mom, it):
            for t in range(n):
                last = nc.vector.bn_stats(stats[:, t, :], src(t))
            last.then_inc(st.sem, 1)
            dve.wait_ge(st.sem, st.after(it, 1))
            settle(dve)
            for t in range(n):
                last = nc.vector.bn_aggr(moments[:, t, :], stats[:, t, :])
            last.then_inc(mom.sem, 1)

        @block.vector
        def _(dve):
            dve.sem_inc(proj_done.sem, 2)
            dve.sem_inc(A.masked.sem, A.masked.prime)
            dve.sem_inc(B.masked.sem, B.masked.prime)
            dve.sem_inc(lp_dve.sem, 2)
            dve.sem_inc(A.pt_odd.sem, 1)
            dve.sem_inc(A.o.sem, 1)
            dve.sem_inc(B.o.sem, 1)
            dve.sem_inc(z_done.sem, 1)
            dve.sem_inc(lp_sum.sem, 2)
            dve.sem_inc(l_res.sem, 1)
            dve.sem_inc(f_xnr.sem, 1)
            dve.sem_inc(f_ac.sem, 3)
            dve.sem_inc(f_ys.sem, 1)
            dve.sem_inc(n_out.sem, 1)
            KW = KV * P
            for n in range(KV):
                dve.wait_ge(split_hi.sem, n + 1)
                nc.vector.tensor_tensor(pair_part(n, 1), raw_pairs(n), pair_part(n, 0).bitcast(F32),
                                        ALU.subtract).then_inc(split_lo.sem, 1)
            dve.wait_ge(split_hi.sem, KV + 1)
            nc.vector.tensor_tensor(w_grp[:, :, P:2 * P], kv_raw[:, 0:KW].rearrange("p (g n) -> p g n", n=P),
                                    w_grp[:, :, 0:P].bitcast(F32), ALU.subtract).then_inc(split_lo.sem, 1)
            dve.wait_ge(split_hi.sem, KV + 2)
            nc.vector.tensor_tensor(wv_lo[:, :], kv_raw[:, KW:], wv_hi[:, :].bitcast(F32), ALU.subtract).then_inc(split_lo.sem, 1)
            dve.wait_ge(ld_small.sem, N_SMALL)
            dve.wait_ge(const_ready.sem, 14)
            with dve.Fori(0, NB) as b:
                dve.wait_ge(xt_hi_done.sem, xt_hi_done.after(b, 1))
                nc.vector.tensor_tensor(xt_lo[:, 0:S], bank[0][:, 0:S], xt_hi[:, 0:S].bitcast(F32),
                                        ALU.subtract).then_inc(xt_lo_done.sem, 1)
                dve.wait_ge(A.pv.sem, A.pv.after(b * KV, 0))
                for t in range(TT):
                    dve.wait_ge(v_ps.sem, v_ps.after(b, t + 1))
                    nc.vector.tensor_tensor(v_a[:, t, :, 0:HD], bank[t][:, :].rearrange("p (g d) -> p g d", d=HD),
                                            bv_b[:, :].rearrange("p (g d) -> p g d", d=HD), ALU.add).then_inc(v_done.sem, 1)

                def project(n, it, g, odd):
                    dve.wait_ge(proj_hi.sem, proj_hi.after(it, n + 1))
                    if n == 0:
                        hi, lo, bias = k_hi[:, odd, :], k_lo[:, odd, :], bk_c[:, bass.ds(g, 1)]
                    else:
                        hi, lo, bias = q_hi[:, (n - 1) % 2, :], q_lo[:, (n - 1) % 2, :], bq_c[:, bass.ds(g * GP + n - 1, 1)]
                    nc.vector.scalar_tensor_tensor(lo, bank[B_P][:, 0:S], bias, hi.bitcast(F32), ALU.add,
                                                   ALU.subtract).then_inc(proj_done.sem, 1)

                def set_sinks(part, it, g):
                    lo, hi = ((0, 2), (2, GH))[part]
                    dve.wait_ge(A.masked.sem, A.masked.after(it, -2 * GH + 4 if part == 0 else 0))
                    nc.vector.tensor_copy(sink_g[:, lo:hi], sink_n[:, bass.ds(g * GH + lo, hi - lo)]).then_inc(sink_set.sem, 1)
                    dve.wait_ge(sink_set.sem, sink_set.after(it, part + 1))

                def body(g, odd, first, last):
                    it = b * KV + g

                    def side(i):
                        if i == 0:
                            set_sinks(1, it, g)
                        if i == 4 and not last:
                            set_sinks(0, it + 1, g + 1)
                        for step, n, ahead in A_SIDE:
                            if step == i and not (ahead and last):
                                project(n, it + ahead, g + ahead, (odd + ahead) % 2)

                    att_dve(dve, A, it, span(A, first, last), P, 384, mask_w, lambda t, h: -0.125,
                            lambda h: sink_g[:, h % GH:h % GH + 1], side, nothing, True)

                for n in range(3):
                    project(n, b * KV, 0, 0)
                set_sinks(0, b * KV, 0)
                body(0, 0, True, False)
                with dve.Fori(0, KV // 2 - 1) as j:
                    body(2 * j + 1, 1, False, False)
                    body(2 * j + 2, 0, False, False)
                body(KV - 1, 1, False, True)
                dve.wait_ge(y_full.sem, y_full.after(b, 1))
                dve.wait_ge(xin_ready.sem, xin_ready.after(b, 2))
                nc.vector.tensor_tensor(z_b[:, :, :].rearrange("p t d -> p (t d)"), bank[B_Y][:, 0:S], x_bo[:, :],
                                        ALU.add).then_inc(z_done.sem, 1)
                dve.wait_ge(z_done.sem, z_done.after(b, 1))
                dve_stats(dve, TT, lambda t: z_b[:, t, :], st_done, mom_done, b)
                dve.wait_ge(var_done.sem, var_done.after(b, 3))
                for t in range(TT):
                    nc.vector.tensor_scalar(x_mid[:, bass.ds(b * TT + t, 1), :].rearrange("p t d -> p (t d)"), z_b[:, t, :],
                                            moments[:, t, 0:1], rstd[:, t:t + 1], ALU.subtract,
                                            ALU.mult).then_inc(ln_done.sem, 1)
            end_phase(dve, 1)
            nc.vector.memset(xt_hi[HD:P, 0:1].bitcast(F32), 0.0)
            nc.vector.memset(xt_lo[HD:P, 0:1].bitcast(F32), 0.0)
            nc.vector.memset(f_sh[HD:P, :].rearrange("p (h s) -> p h s", s=S)[:, :, 0:1], 0.0).then_inc(zeros.sem, 1)
            with dve.Fori(0, L) as l:
                dve.wait_ge(tab.sem, tab.after(l, 4))
                settle(dve)

                def shift_x(it):
                    dve.wait_ge(lxt_hi.sem, lxt_hi.after(it, 1))
                    nc.vector.tensor_tensor(xt_lo[0:HD, 0:S], bank[B_P][0:HD, 0:S], xt_hi[0:HD, 0:S].bitcast(F32), ALU.subtract)
                    nc.vector.tensor_tensor(xt_lo[HD:P, 1:S + 1], bank[B_P][HD:P, 0:S], xt_hi[HD:P, 1:S + 1].bitcast(F32),
                                            ALU.subtract).then_inc(lxt_lo.sem, 1)

                def project(z, n, it):
                    if n not in QK:
                        return
                    hs, c, t = it * 2 + z, n, n % 2
                    kind, ps = c // 2, qk_raw[:, t, :]
                    dve.wait_ge(lp_act.sem, lp_act.after(hs, n + 1))
                    dve.wait_ge(lp_rot.sem, lp_rot.after(hs, c - 1))
                    nc.vector.tensor_tensor(
                        r_a[:, t, :].rearrange("p (h d) -> p h d", d=HD), ps.rearrange("p (h d) -> p h d", d=HD),
                        cos_s[:, kind, t, :].unsqueeze(1).broadcast_to([P, HC, HD]), ALU.mult)
                    for y in range(2):
                        last = nc.vector.tensor_tensor(
                            halves(r_b[:, t, :])[:, :, y, :], halves(ps)[:, :, 1 - y, :],
                            sin_s[:, kind, t, y * 32:y * 32 + 32].unsqueeze(1).broadcast_to([P, HC, 32]), ALU.mult)
                    last.then_inc(lp_dve.sem, 1)
                    dve.wait_ge(lp_sq.sem, lp_sq.after(hs, n + 1))
                    nc.vector.tensor_reduce(ssum[:, t, :], sq[:, t, :].rearrange("p (h d) -> p h d", d=HD),
                                            AX.X, ALU.add).then_inc(lp_sum.sem, 1)

                def residual(b, it):
                    dve.wait_ge(B.y.sem, B.y.after(it, LP))
                    xb = x_cur[:, bass.ds(b * TT, TT), :].rearrange("p t d -> p (t d)")
                    nc.vector.tensor_tensor(xb, bank[B_Y][:, 0:S], xb, ALU.add).then_inc(l_res.sem, 1)

                def batch(b, it, first, last):
                    def side(i):
                        if not last and i == X_AT:
                            shift_x(it + 1)
                        if not first and i == 3:
                            residual(b - 1, it - 1)
                        for z, ahead, n, c in events(i, not last):
                            if n is not None:
                                project(z, n, it + ahead)

                    att_dve(dve, B, it, span(B, first, last), P, 288, mask_l, lambda t, h: q_neg[:, t, h % LH:h % LH + 1],
                            lambda h: 3.0e38, nothing, side, False)

                shift_x(l * NB)
                for z, n, c in FIRST:
                    project(z, n, l * NB)
                batch(0, l * NB, True, False)
                with dve.Fori(1, NB - 1) as b:
                    batch(b, l * NB + b, False, False)
                batch(NB - 1, l * NB + (NB - 1), False, True)
                residual(NB - 1, l * NB + (NB - 1))
                end_phase(dve, l * 2 + 2)

                def statistics(it):
                    dve.wait_ge(f_t2.sem, f_t2.after(it, 1))
                    dve_stats(dve, FT, lambda t: bank[1][:, t * P:(t + 1) * P], f_st, f_mom, it)

                def normed(it):
                    dve.wait_ge(f_var.sem, f_var.after(it, 3))
                    dve.wait_ge(f_t3.sem, f_t3.after(it, 0))
                    for t in range(FT):
                        last = nc.vector.tensor_scalar(f_xn[:, t, :], bank[1][:, t * P:(t + 1) * P], moments[:, t, 0:1],
                                                       rstd[:, t:t + 1], ALU.subtract, ALU.mult)
                    last.then_inc(f_xnr.sem, 1)

                def gated(j, it):
                    n = FB[j][1]
                    if j == 0:
                        dve.wait_ge(f_yp.sem, f_yp.after(it, 0))
                    dve.wait_ge(f_ap.sem, f_ap.after(it, j + 1))
                    dve.wait_ge(f_gl.sem, f_gl.after(it, j + 1))
                    nc.vector.scalar_tensor_tensor(f_act[0:n, j, :], bank[5 + j % 2][0:n, :], b1_c[0:n, 2 * j:2 * j + 1],
                                                   f_gate[0:n, j, :], ALU.add, ALU.mult).then_inc(f_ac.sem, 1)

                def summed(c, it):
                    dve.wait_ge(f_yp.sem, f_yp.after(it, 1))
                    dve.wait_ge(f_res.sem, f_res.after(it, 0))
                    nc.vector.tensor_tensor(f_y[:, :, :].rearrange("p t d -> p (t d)"), bank[B_Y][:, :],
                                            x_cur[:, bass.ds(c * FT, FT), :].rearrange("p t d -> p (t d)"),
                                            ALU.add).then_inc(f_ys.sem, 1)

                statistics(l * FC)
                normed(l * FC)
                with dve.Fori(0, FC - 1) as c:
                    it = l * FC + c
                    statistics(it + 1)
                    for j in range(NF - 1):
                        gated(j, it)
                    normed(it + 1)
                    gated(NF - 1, it)
                    summed(c, it)
                for j in range(NF):
                    gated(j, l * FC + (FC - 1))
                summed(FC - 1, l * FC + (FC - 1))
                end_phase(dve, l * 2 + 3)
            with dve.Fori(0, NB) as b:
                dve.wait_ge(n_out.sem, n_out.after(b, 0))
                xb = x_cur[:, bass.ds(b * TT, TT), :]
                nc.vector.tensor_tensor(z_b[:, :, :], xb, x_mid[:, bass.ds(b * TT, TT), :], ALU.add).then_inc(n_z.sem, 1)
                dve.wait_ge(n_z.sem, n_z.after(b, 1))
                dve_stats(dve, TT, lambda t: z_b[:, t, :], n_st, n_mom, b)
                dve.wait_ge(n_var.sem, n_var.after(b, 3))
                for t in range(TT):
                    last = nc.vector.tensor_scalar(x_cur[:, bass.ds(b * TT + t, 1), :].rearrange("p t d -> p (t d)"),
                                                   z_b[:, t, :], moments[:, t, 0:1], rstd[:, t:t + 1], ALU.subtract, ALU.mult)
                last.then_inc(n_out.sem, 1)

        def split_mm(dst, lhs, rhs, start=True):
            nc.tensor.matmul(dst, lhs[1], rhs[0], start=True, stop=False)
            nc.tensor.matmul(dst, lhs[0], rhs[0], start=False, stop=False)
            return nc.tensor.matmul(dst, lhs[0], rhs[1], start=False, stop=True)

        def o_ps(h, t):
            return bank[B_O][:, (2 * t + h % 2) * VW:(2 * t + h % 2 + 1) * VW]

        def keep_warm(n):
            for _ in range(n):
                nc.tensor.matmul(bank[B_OT][:, 0:P], ident[:, :], ident[:, :], start=True, stop=True)

        @block.tensor
        def _(pe):
            for a in (A, B):
                for g in (a.scores, a.transposed, a.pv, a.ot, a.y):
                    pe.sem_inc(g.sem, g.prime)
            pe.sem_inc(proj_ready.sem, proj_ready.prime)
            pe.sem_inc(xt_ps.sem, 1)
            pe.sem_inc(lxt_ps.sem, 1)
            pe.sem_inc(lp_ps.sem, 1)
            pe.sem_inc(lt_ps.sem, 2)
            for g in (f_t1, f_t2, f_t3, f_ap, f_yp):
                pe.sem_inc(g.sem, 1)
            pe.wait_ge(const_ready.sem, 14)
            pe.wait_ge(split_lo.sem, KV + 2)
            pe.wait_ge(ld_wo.sem, 16)
            xt = (xt_hi[:, 0:S], xt_lo[:, 0:S])
            with pe.Fori(0, NB) as b:
                pe.wait_ge(A.o_sb.sem, A.o_sb.after(b * KV, 0))
                pe.wait_ge(xin_ready.sem, xin_ready.after(b, 1))
                pe.wait_ge(proj_done.sem, proj_done.after(b * KV, 0))
                for t in range(TT):
                    last = nc.tensor.transpose(bank[0][:, t * P:(t + 1) * P], x_in[:, t, :], ident[:, :])
                last.then_inc(xt_ps.sem, 1)
                keep_warm(4)
                pe.wait_ge(xt_lo_done.sem, xt_lo_done.after(b, 1))
                settle(pe)

                for t in range(TT):
                    ts = slice(t * P, (t + 1) * P)
                    split_mm(bank[t][:, :], (xt_hi[:, ts], xt_lo[:, ts]), (wv_hi[:, :], wv_lo[:, :])).then_inc(v_ps.sem, 1)
                pe.wait_ge(v_done.sem, v_done.after(b, TT))
                keep_warm(1)

                def project(n, it):
                    if n in (0, 2):
                        part = staged_a if n == 0 else staged_b
                        pe.wait_ge(part.sem, part.after(it, 16))
                    pe.wait_ge(proj_done.sem, proj_done.after(it, n))
                    c = 2 * n * P
                    split_mm(bank[B_P][:, 0:S], (w_stage[:, c:c + P], w_stage[:, c + P:c + 2 * P]), xt).then_inc(proj_ready.sem, 1)

                def body(g, odd, first, last):
                    it = b * KV + g

                    def side(i):
                        for step, n, ahead in A_SIDE:
                            if step == i and not (ahead and last):
                                project(n, it + ahead)

                    def scores(h):
                        ahead, h = divmod(h, GH)
                        p, r = h // 2, slice(HD * (h % 2), HD * (h % 2) + HD)
                        pe.wait_ge(proj_done.sem, proj_done.after(it + ahead, p + 2))
                        ps, q = bank[B_S[h % 2]], (q_hi[r, p % 2, :], q_lo[r, p % 2, :])
                        k = [x[r, (odd + ahead) % 2, :] for x in (k_hi, k_lo)]
                        split_mm(ps[:, 0:P], [x[:, 0:P] for x in q], [x[:, 0:P] for x in k])
                        return split_mm(ps[:, P:384], [x[:, P:S] for x in q], k)

                    def tr(h):
                        for k in range(3):
                            last = nc.tensor.transpose(bank[B_T[h % 2]][:, k * P:(k + 1) * P],
                                                       p_e[:, h % 2, k * P:(k + 1) * P], ident[:, :])
                        return last

                    def pv(h):
                        pt = p_t[:, h % 2, :]
                        v = [v_a[:, t, bass.ds(g + h // GH, 1), :].rearrange("p g d -> p (g d)") for t in range(TT)]
                        nc.tensor.matmul(o_ps(h, 0), pt[:, 0:P], v[0], start=True, stop=True)
                        nc.tensor.matmul(o_ps(h, 1), pt[:, P:2 * P], v[0], start=True, stop=False)
                        return nc.tensor.matmul(o_ps(h, 1), pt[:, 2 * P:3 * P], v[1], start=False, stop=True)

                    att_pe(pe, A, it, span(A, first, last), side, nothing, scores, tr, pv,
                           lambda p: wo_t[:, bass.ds(g * GP + p, 1), :].rearrange("p q d -> p (q d)"))

                for n in range(3):
                    project(n, b * KV)
                    keep_warm(4)
                pe.wait_ge(z_done.sem, z_done.after(b, 0))
                nc.tensor.matmul(bank[B_Y][:, 0:S], zero_b[0:1, 0:P], zero_b[0:1, 0:S], start=True, stop=True)
                body(0, 0, True, False)
                with pe.Fori(0, KV // 2 - 1) as j:
                    body(2 * j + 1, 1, False, False)
                    body(2 * j + 2, 0, False, False)
                body(KV - 1, 1, False, True)
                pe.drain().then_inc(y_full.sem, 1)
            end_phase(pe, 1)
            pe.wait_ge(zeros.sem, 1)
            with pe.Fori(0, L) as l:
                pe.wait_ge(lw_lo.sem, lw_lo.after(l, 1))
                settle(pe)
                def turn_x(it):
                    pe.wait_ge(lx_in.sem, lx_in.after(it, 1))
                    pe.wait_ge(lp_act.sem, lp_act.after(it * 2, 0))
                    for t in range(TT):
                        last = nc.tensor.transpose(bank[B_P][:, t * P:(t + 1) * P], x_in[:, t, :], ident[:, :])
                    last.then_inc(lxt_ps.sem, 1)

                def project(z, n, it):
                    hs = it * 2 + z
                    if z == 0 and n == 0:
                        pe.wait_ge(lxt_lo.sem, lxt_lo.after(it, 1))
                    pe.wait_ge(lp_act.sem, lp_act.after(hs, n))
                    ws, t = chunk_columns(z, n)
                    ts = slice(t * P, (t + 1) * P)
                    split_mm(bank[B_P][:, :], (xt_hi[:, ts], xt_lo[:, ts]), (w_hi[:, ws], w_lo[:, ws])).then_inc(lp_ps.sem, 1)

                def turn_chunk(z, c, it, last_pair):
                    hs = it * 2 + z
                    pe.wait_ge(lp_out.sem, lp_out.after(hs, c + 1))
                    pe.wait_ge(lt_act.sem, lt_act.after(hs, c))
                    pe.wait_ge(B.o_sb.sem, last_pair)
                    src = r_s if c < 2 else r_n
                    for k in range(4):
                        last = nc.tensor.transpose(bank[B_OT][:, k * P:(k + 1) * P],
                                                   src[:, c % 2, k * P:(k + 1) * P], ident[:, :])
                    last.then_inc(lt_ps.sem, 1)

                def scores(h):
                    h %= LH
                    p, r = h // 2, slice(HD * (h % 2), HD * (h % 2) + HD)
                    ps = bank[B_S[h % 2]]
                    nc.tensor.matmul(ps[:, 0:P], qt_l[r, p, 0:P], kt_l[r, p, 0:P], start=True, stop=True)
                    return nc.tensor.matmul(ps[:, P:288], qt_l[r, p, P:S], kt_l[r, p, P - LOCAL:S], start=True, stop=True)

                def tr(h):
                    ps, pr = bank[B_T[h % 2]], p_e[:, h % 2, :]
                    nc.tensor.transpose(ps[:, 0:P], pr[:, 0:P], ident[:, :])
                    nc.tensor.transpose(ps[:, P:2 * P], pr[:, P + LOCAL:2 * P + LOCAL], ident[:, :])
                    return nc.tensor.transpose(ps[:, 2 * P:2 * P + LOCAL], pr[0:LOCAL, LOCAL:P + LOCAL], ident[0:LOCAL, 0:LOCAL])

                def pv(h):
                    h %= LH
                    pt = p_t[:, h % 2, :]
                    nc.tensor.matmul(o_ps(h, 0), pt[:, 0:P], v_l[:, 0, h, :], start=True, stop=True)
                    nc.tensor.matmul(o_ps(h, 1), pt[:, P:2 * P], v_l[:, 1, h, :], start=True, stop=True)
                    return nc.tensor.matmul(o_ps(h, 1)[0:LOCAL], pt[P - LOCAL:P, 2 * P:2 * P + LOCAL],
                                            v_l[P - LOCAL:P, 0, h, :], start=False, stop=True, skip_group_check=True)

                def batch(it, first, last):
                    def before(i):
                        if i == 4:
                            pe.wait_ge(l_res.sem, l_res.after(it, 0))
                            nc.tensor.matmul(bank[B_Y][:, 0:S], zero_b[0:1, 0:P], zero_b[0:1, 0:S], start=True, stop=True)
                        if i in (-2, 6) or i == 14 and not last:
                            hs = it * 2 + {-2: 0, 6: 1, 14: 2}[i]
                            pe.wait_ge(lt_act.sem, lt_act.after(hs, 4))
                            pe.wait_ge(lp_act.sem, lp_act.after(hs, 6))

                    def side(i):
                        if not last and i == X_AT:
                            turn_x(it + 1)
                        for z, ahead, n, c in events(i, not last):
                            if n is not None:
                                project(z, n, it + ahead)
                            if c is not None:
                                pairs = (i - 2) // 2
                                turn_chunk(z, c, it + ahead, B.o_sb.after(it, max(0, pairs) if first else pairs))

                    def ot_free(i):
                        z, ahead, c = chunk_before(i, not last)
                        pe.wait_ge(lt_act.sem, lt_act.after((it + ahead) * 2 + z, c))

                    att_pe(pe, B, it, span(B, first, last), before, side, scores, tr, pv, lambda p: wo_l[:, p % LP, :], ot_free)

                turn_x(l * NB)
                for z, n, c in FIRST:
                    project(z, n, l * NB)
                    if c is not None:
                        turn_chunk(z, c, l * NB, B.o_sb.after(l * NB, 0))
                pe.wait_ge(lw.sem, lw.after(l, 48))
                batch(l * NB, True, False)
                with pe.Fori(1, NB - 1) as b:
                    batch(l * NB + b, False, False)
                batch(l * NB + (NB - 1), False, True)
                end_phase(pe, l * 2 + 2)
                pe.wait_ge(lw2.sem, lw2.after(l, 16 * 4))
                settle(pe)
                pe.wait_ge(lw_lo.sem, lw_lo.after(l, 2))

                def turn_tokens(it):
                    pe.wait_ge(f_inr.sem, f_inr.after(it, 1))
                    pe.wait_ge(f_s1.sem, f_s1.after(it, 0))
                    for t in range(FT):
                        last = nc.tensor.transpose(bank[0][:, t * P:(t + 1) * P], f_in[:, t, :], ident[:, :])
                    last.then_inc(f_t1.sem, 1)

                def turn_shifted(it):
                    pe.wait_ge(f_s1.sem, f_s1.after(it, 1))
                    pe.wait_ge(f_xnr.sem, f_xnr.after(it, 0))
                    for t in range(FT):
                        last = nc.tensor.transpose(bank[1][:, t * P:(t + 1) * P], f_sh[:, t * P:(t + 1) * P], ident[:, :])
                    last.then_inc(f_t2.sem, 1)

                def turn_normed(it):
                    pe.wait_ge(f_xnr.sem, f_xnr.after(it, 1))
                    pe.wait_ge(f_aff.sem, f_aff.after(it, 0))
                    for t in range(FT):
                        last = nc.tensor.transpose(bank[2][:, t * P:(t + 1) * P], f_xn[:, t, :], ident[:, :])
                    last.then_inc(f_t3.sem, 1)

                def up(j, it):
                    if j == 0:
                        pe.wait_ge(f_lo.sem, f_lo.after(it, 1))
                    o, n = FB[j]
                    for first, base, free, done in ((DI, 3, f_gl, f_gp), (0, 5, f_ac, f_ap)):
                        pe.wait_ge(free.sem, free.after(it, max(0, j - 1)))
                        cs = slice(first + o, first + o + n)
                        split_mm(bank[base + j % 2][0:n, :], (w1_hi[:, cs], w1_lo[:, cs]),
                                 (fx_hi[:, :], fx_lo[:, :])).then_inc(done.sem, 1)

                def down(it):
                    pe.wait_ge(f_ys.sem, f_ys.after(it, 0))
                    pe.wait_ge(f_ac.sem, f_ac.after(it, NF))
                    for t in range(FT):
                        for j, (o, n) in enumerate(FB):
                            last = nc.tensor.matmul(bank[B_Y][:, t * P:(t + 1) * P], f_act[0:n, j, t * P:(t + 1) * P],
                                                    w2_l[0:n, j, :], start=(j == 0), stop=(j == NF - 1))
                    last.then_inc(f_yp.sem, 1)

                turn_tokens(l * FC)
                turn_shifted(l * FC)
                turn_normed(l * FC)
                with pe.Fori(0, FC - 1) as c:
                    it = l * FC + c
                    turn_tokens(it + 1)
                    up(0, it)
                    turn_shifted(it + 1)
                    for j in range(1, NF):
                        up(j, it)
                    turn_normed(it + 1)
                    down(it)
                for j in range(NF):
                    up(j, l * FC + (FC - 1))
                down(l * FC + (FC - 1))
                end_phase(pe, l * 2 + 3)


def rotary_tables(n, hd, window):
    import numpy as np
    half = np.arange(0, hd, 2, dtype=np.float32)
    inv_freq = (np.float32(1.0) / np.float32(10000.0) ** (half / np.float32(hd))).astype(np.float32)
    t = np.arange(n, dtype=np.float32)
    freqs = (t[:, None] * inv_freq[None, :]).astype(np.float32)
    freqs = np.concatenate([freqs, freqs], -1)
    base = ((half + np.float32(0.4 * hd)) / np.float32(1.4 * hd)).astype(np.float32)
    power = ((t - n // 2) / np.float32(window // 2)).astype(np.float32)
    scale = (base[None, :] ** power[:, None]).astype(np.float32)
    scale = np.concatenate([scale, scale], -1)
    cos, sin = np.cos(freqs), np.sin(freqs)
    sin = np.concatenate([-sin[:, :hd // 2], sin[:, hd // 2:]], -1)
    inv = np.float32(1.0) / scale
    return (np.stack([cos * scale, cos * inv]).astype(np.float32),
            np.stack([sin * scale, sin * inv]).astype(np.float32))


def kernel(**inputs):
    import numpy as np
    import concourse.bacc as bacc
    from concourse.bass_utils import run_bass_kernel_spmd

    a = {n.replace("L0_", ""): np.asarray(v) for n, v in inputs.items()}
    hd, kv = 64, a["attn_Wk"].shape[0] // 64
    depth, di = a["ffn_W2"].shape[:2]
    k2 = np.repeat(a["attn_Wk"].reshape(kv, 1, hd, -1), 2, axis=1).reshape(2 * kv * hd, -1)
    bk2 = np.repeat(a["attn_bk"].reshape(kv, 1, hd), 2, axis=1).reshape(kv, 2 * hd)
    blocks = [(o, min(128, di - o)) for o in range(0, di, 128)]
    lcols = np.zeros((depth, 128, 2 * len(blocks) + 2), a["ffn_b1"].dtype)
    for j, (o, n) in enumerate(blocks):
        lcols[:, :n, 2 * j] = a["ffn_b1"][:, o:o + n]
        lcols[:, :n, 2 * j + 1] = a["ffn_b1"][:, di + o:di + o + n]
    lcols[:, :, -2], lcols[:, :, -1] = a["ffn_ln_g"], a["ffn_ln_b"]
    cos, sin = rotary_tables(a["attn_x"].shape[1], hd, 32)
    laid = {
        "x": a["attn_x"],
        "wq_t": a["attn_Wq"].T,
        "wkv_t": np.concatenate([k2, a["attn_Wv"]], 0).T,
        "wo_t": a["attn_Wo"].T,
        "cols": np.concatenate([a["attn_bq"].reshape(-1, 128), bk2], 0).T,
        "rows": np.concatenate([a["attn_bv"], a["attn_bo"], a["attn_sinks"]]),
        "wqkv": np.concatenate([a["ffn_Wqkv"], a["ffn_Wqkv"][:1]]),
        "qk_scale": np.concatenate([a["ffn_q_scale"], a["ffn_k_scale"]], 1)[list(range(depth)) + [0]],
        "wo_l": a["ffn_Wo"],
        "w1": a["ffn_W1"],
        "w2": a["ffn_W2"],
        "b2": a["ffn_b2"],
        "lcols": lcols,
        "rot_cos": cos,
        "rot_sin": sin,
    }
    nc = bacc.Bacc("TRN2", target_bir_lowering=False, num_devices=1)
    arrays, args = {}, []
    for name, v in laid.items():
        v = np.ascontiguousarray(v)
        arrays[f"in_{name}"] = v
        args.append(nc.dram_tensor(f"in_{name}", v.shape, mybir.dt.from_np(v.dtype), kind="ExternalInput").ap())
    args.append(nc.dram_tensor("out_0", a["attn_x"].shape, mybir.dt.float32, kind="ExternalOutput").ap())
    block_program(nc, *args)
    r = run_bass_kernel_spmd(nc, [arrays], core_ids=[0])
    return r.results[0]["out_0"]
```
